# Optimizing a Trainium2 kernel written in Bass

```python
import numpy as np
import jax
import jax.numpy as jnp

def _softmax(x, axis=-1):
    return jax.nn.softmax(x, axis=axis)

def _gelu(x):
    return jax.nn.gelu(x, approximate=True)

def _silu(x):
    return jax.nn.silu(x)

def _sigmoid(x):
    return jax.nn.sigmoid(x)

def _layernorm(x, axis=-1, eps=1e-05):
    m = jnp.mean(x, axis=axis, keepdims=True)
    v = jnp.var(x, axis=axis, keepdims=True)
    return (x - m) / jnp.sqrt(v + eps)

def _scatter_add(tgt, idx, src, axis=0):
    return tgt.at[idx].add(src)

def _segment_sum(src, seg, n):
    return jax.ops.segment_sum(src, seg, n)
kernel_name = 'mk_flamingo_gated_d1_seqx_r8_866368'

def setup_inputs(seed: int=0):
    np.random.seed(seed)
    _w = jnp.asarray

    def _rec_inputs():
        import jax
        import jax.numpy as jnp
        _rk = jax.random.key(seed)
        x = -0.0002928 + 1 * jax.random.normal(jax.random.fold_in(_rk, 1), (8, 256, 128), jnp.float32)
        _lenS = 256 - jax.random.randint(jax.random.fold_in(_rk, 7), (8,), 0, max(1, 256 // 4) + 1, jnp.int32)
        _lenS2 = 1601 - jax.random.randint(jax.random.fold_in(_rk, 8), (8,), 0, max(1, 1601 // 4) + 1, jnp.int32)
        _ctx_1024P = jax.random.normal(jax.random.fold_in(_rk, 11), (8, 16, 128), jnp.float32)
        _ctx_1024c = jax.random.dirichlet(jax.random.fold_in(_rk, 511), 0.3 * jnp.ones((16,), jnp.float32), (8, 1601))
        _ctx_1024t = jnp.einsum('bsk,bkd->bsd', _ctx_1024c, _ctx_1024P)
        _ctx_1024t = _ctx_1024t * jax.lax.rsqrt(jnp.mean(jnp.square(_ctx_1024t)) + 1e-12) * 0.953939
        ctx_1024 = -1.39393e-06 + 0.999914 * (_ctx_1024t + 0.3 * jax.random.normal(jax.random.fold_in(_rk, 611), (8, 1601, 128), jnp.float32))
        _validS = jnp.arange(256)[None, :] < _lenS[:, None]
        _validS2 = jnp.arange(1601)[None, :] < _lenS2[:, None]
        _causal = jnp.tril(jnp.ones((256, 256), dtype=bool))
        mask_BxS2_bf0 = jnp.logical_not(jnp.ones((8, 1601), dtype=bool))
        _g = jax.random.normal(jax.random.fold_in(_rk, 9001), (2, 1), jnp.float32)
        _g = jnp.sign(_g) * jnp.maximum(jnp.abs(_g), 1.0) + (_g == 0) * 1.0
        g_xattn = _g[0]
        g_ffn = _g[1]
        return (x, ctx_1024, mask_BxS2_bf0, g_xattn, g_ffn)
    x, ctx_1024, mask_BxS2_bf0, g_xattn, g_ffn = _rec_inputs()

    def _L0_xattn_setup():
        import jax, jax.numpy as jnp
        import numpy as np
        B, S, D = (2, 256, 128)
        H, DK, DV = (16, 64, 64)
        NEG_INF = -1e+30
        key = jax.random.key(seed)
        ks = jax.random.split(key, 12)
        s = 0.02
        return {'queries': jax.random.normal(ks[0], (B, S, D), jnp.float32), 'keys': jax.random.normal(ks[1], (B, S, D), jnp.float32), 'values': jax.random.normal(ks[2], (B, S, D), jnp.float32), 'mask': jnp.zeros((B, S), dtype=bool), 'Wq': jax.random.normal(ks[3], (D, H * DK), jnp.float32) * s, 'bq': jnp.zeros((H * DK,), jnp.float32), 'Wk': jax.random.normal(ks[4], (D, H * DK), jnp.float32) * s, 'bk': jnp.zeros((H * DK,), jnp.float32), 'Wv': jax.random.normal(ks[5], (D, H * DV), jnp.float32) * s, 'bv': jnp.zeros((H * DV,), jnp.float32), 'Wo': jax.random.normal(ks[6], (H * DV, D), jnp.float32) * s, 'bo': jnp.zeros((D,), jnp.float32)}
    _L0_xattn_all = _L0_xattn_setup()
    _L0_xattn_in = {k: v for k, v in _L0_xattn_all.items() if k in ('Wq', 'bq', 'Wk', 'bk', 'Wv', 'bv', 'Wo', 'bo')}
    del _L0_xattn_all

    def _L0_ffn_setup():
        import jax, jax.numpy as jnp
        import numpy as np
        E, D, H = (8, 128, 512)
        B, S = (4, 512)
        TEMPERATURE = 1.0
        key = jax.random.key(seed)
        ks = jax.random.split(key, 7)
        sc = 0.02
        return {'x': jax.random.normal(ks[0], (B, S, D), dtype=jnp.float32), 'W1': jax.random.normal(ks[1], (E, D, H), dtype=jnp.float32) * sc, 'b1': jax.random.normal(ks[2], (E, H), dtype=jnp.float32) * sc, 'W2': jax.random.normal(ks[3], (E, H, D), dtype=jnp.float32) * sc, 'b2': jax.random.normal(ks[4], (E, D), dtype=jnp.float32) * sc, 'Wr': jax.random.normal(ks[5], (D, E), dtype=jnp.float32) * sc, 'br': jax.random.normal(ks[6], (E,), dtype=jnp.float32) * sc}
    _L0_ffn_all = _L0_ffn_setup()
    _L0_ffn_in = {k: v for k, v in _L0_ffn_all.items() if k in ('W1', 'b1', 'W2', 'b2', 'Wr', 'br')}
    del _L0_ffn_all
    return {'x': x, 'ctx_1024': ctx_1024, 'mask_BxS2_bf0': mask_BxS2_bf0, 'g_xattn': g_xattn, 'g_ffn': g_ffn, 'L0_xattn_Wq': _L0_xattn_in['Wq'], 'L0_xattn_bq': _L0_xattn_in['bq'], 'L0_xattn_Wk': _L0_xattn_in['Wk'], 'L0_xattn_bk': _L0_xattn_in['bk'], 'L0_xattn_Wv': _L0_xattn_in['Wv'], 'L0_xattn_bv': _L0_xattn_in['bv'], 'L0_xattn_Wo': _L0_xattn_in['Wo'], 'L0_xattn_bo': _L0_xattn_in['bo'], 'L0_ffn_W1': _L0_ffn_in['W1'], 'L0_ffn_b1': _L0_ffn_in['b1'], 'L0_ffn_W2': _L0_ffn_in['W2'], 'L0_ffn_b2': _L0_ffn_in['b2'], 'L0_ffn_Wr': _L0_ffn_in['Wr'], 'L0_ffn_br': _L0_ffn_in['br']}

def reference(x, ctx_1024, mask_BxS2_bf0, g_xattn, g_ffn, L0_xattn_Wq, L0_xattn_bq, L0_xattn_Wk, L0_xattn_bk, L0_xattn_Wv, L0_xattn_bv, L0_xattn_Wo, L0_xattn_bo, L0_ffn_W1, L0_ffn_b1, L0_ffn_W2, L0_ffn_b2, L0_ffn_Wr, L0_ffn_br):
    import jax
    import jax.numpy as jnp

    def _L0_xattn_ref(queries, keys, values, mask, Wq, bq, Wk, bk, Wv, bv, Wo, bo):
        import jax, jax.numpy as jnp
        import numpy as np
        B, S, D = (2, 256, 128)
        H, DK, DV = (16, 64, 64)
        NEG_INF = -1e+30
        b, sq, _ = queries.shape
        sk = keys.shape[1]
        q = (queries @ Wq + bq).reshape(b, sq, H, DK).transpose(0, 2, 1, 3)
        k = (keys @ Wk + bk).reshape(b, sk, H, DK).transpose(0, 2, 1, 3)
        v = (values @ Wv + bv).reshape(b, sk, H, DV).transpose(0, 2, 1, 3)
        scores = jnp.einsum('bhqd,bhkd->bhqk', q, k) / jnp.sqrt(jnp.float32(DK))
        scores = jnp.where(mask[:, None, None, :], NEG_INF, scores)
        causal = jnp.triu(jnp.ones((sq, sk), dtype=bool), k=1)
        scores = jnp.where(causal[None, None], NEG_INF, scores)
        attn = jax.nn.softmax(scores, axis=-1)
        out = jnp.einsum('bhqk,bhkd->bhqd', attn, v)
        out = out.transpose(0, 2, 1, 3).reshape(b, sq, H * DV)
        return out @ Wo + bo

    def _L0_ffn_ref(x, W1, b1, W2, b2, Wr, br):
        import jax, jax.numpy as jnp
        import numpy as np
        E, D, H = (8, 128, 512)
        B, S = (4, 512)
        TEMPERATURE = 1.0
        routing_logits = (x @ Wr + br) / TEMPERATURE
        routing_probs = jax.nn.softmax(routing_logits, axis=-1)
        indices = jnp.argmax(routing_probs, axis=-1)
        out = jnp.zeros_like(x)
        num_experts = W1.shape[0]
        for i in range(num_experts):
            mask = (indices == i).astype(x.dtype)[..., None]
            xi = x * mask
            h = jax.nn.relu(xi @ W1[i] + b1[i])
            out = out + (h @ W2[i] + b2[i])
        return out
    x = x + jnp.tanh(g_xattn[0]) * _L0_xattn_ref(_layernorm(x, axis=-1), ctx_1024, ctx_1024, mask_BxS2_bf0, L0_xattn_Wq, L0_xattn_bq, L0_xattn_Wk, L0_xattn_bk, L0_xattn_Wv, L0_xattn_bv, L0_xattn_Wo, L0_xattn_bo)
    x = x + jnp.tanh(g_ffn[0]) * _L0_ffn_ref(_layernorm(x, axis=-1), L0_ffn_W1, L0_ffn_b1, L0_ffn_W2, L0_ffn_b2, L0_ffn_Wr, L0_ffn_br)
    return x

_drawn_inputs = setup_inputs


def setup_inputs(seed=0):
    import zlib

    import numpy as np

    out = dict(_drawn_inputs(seed))
    spreads = {'L0_xattn_bq': (0.0, 0.8),
     'L0_xattn_bk': (0.0, 0.8),
     'L0_xattn_bv': (0.0, 0.1),
     'L0_xattn_bo': (0.0, 0.1)}
    factors = {'L0_xattn_Wq': 8.0, 'L0_xattn_Wk': 8.0, 'L0_ffn_b1': 3.915, 'L0_ffn_br': 2.689}
    for name, (base, spread) in spreads.items():
        noise = np.random.default_rng([zlib.crc32(name.encode()), seed]).standard_normal(out[name].shape)
        drawn = base * np.exp(spread * noise) if base else spread * noise
        out[name] = jnp.asarray(drawn.astype(out[name].dtype))
    for name, factor in factors.items():
        out[name] = (out[name] * factor).astype(out[name].dtype)
    return out
```

```python
import concourse.bass as bass
from concourse import mybir
from contextlib import ExitStack

fp32 = mybir.dt.float32
bf16 = mybir.dt.bfloat16
i32 = mybir.dt.int32
u32 = mybir.dt.uint32
u8 = mybir.dt.uint8
ALU = mybir.AluOpType
ACT = mybir.ActivationFunctionType
AX = mybir.AxisListType

P = 128
B, S, D = 8, 256, 128
SK = 1601
H, DK = 16, 64
E, F = 8, 512
QT = S // P
NT = B * QT
PAIRS = H // 2
FC = F // P
W3 = 3 * P
SLOTS = 4
SCALE = DK ** -0.5
MASKED = -1e30 / SCALE
FLOOR = 5e29
EPS = 1e-5
RS_MAGIC = float(0x5F3759DF)
TAIL = SK - (SK // P) * P
FULL = SK // P
CAP = B * S + P
PADROW = E * CAP
ROW = 2 * D + 1
MT = (B * S + E * (P - 1)) // P
RING = 4
NTILES = (MT + RING - 1) // RING * RING
NOBODY = 1 << 20


class Count:

    def __init__(self, engine, sem):
        self.engine, self.sem, self.base, self.n = engine, sem, 0, 0

    def up(self, instruction):
        instruction.then_inc(self.sem, 1)
        self.n += 1

    def wait(self):
        self.engine.wait_ge(self.sem, self.base + self.n)

    def enter(self, turn, each):
        self.fixed, self.base, self.n, self.each = self.base + self.n, self.base + self.n + turn * each, 0, each

    def leave(self, turns):
        assert self.n == self.each, (self.n, self.each)
        self.base, self.n = self.fixed + turns * self.each, 0


def settle(engine):
    engine.nop(nofuse=True)


def wait(engine, sem, value):
    if not isinstance(value, int) or value > 0:
        engine.wait_ge(sem, value)


def flamingo_layer(nc, x, ctx_in, mask, g_attn, g_ffn, wq, bq, wk, bk, wv, bv, wo, bo, w1, b1, w2, b2, wr, br, out):
    ctx = ExitStack()
    with ctx:
        def sb(name, shape, dt=fp32):
            return ctx.enter_context(nc.sbuf_tensor(name, shape, dt))

        def pb(name):
            return ctx.enter_context(nc.psum_tensor(name, [P, 512], fp32))

        def sem(name):
            return ctx.enter_context(nc.semaphore(name))

        sorted_rows = nc.dram_tensor("sorted_rows", (PADROW + P, ROW), fp32, kind="Internal").ap()

        x_nat = sb("x_nat", [P, NT, D])
        ctx_nat = sb("ctx_nat", [P, NT, D])
        x_norm = sb("x_norm", [P, QT, D])
        ctx_now = sb("ctx_now", [P, QT, D])
        in_T = sb("in_T", [P, 2 * S])
        xT, cT = in_T[:, 0:S], in_T[:, S:2 * S]
        q_pad = sb("q_pad", [P, H, S])
        k_T = sb("k_T", [P, PAIRS, S])
        v_nat = sb("v_nat", [P, QT, H * DK])
        o_T = sb("o_T", [P, PAIRS, S])
        masked = sb("masked", [P, 2, W3])
        prob = sb("prob", [P, SLOTS, W3])
        prob_T = sb("prob_T", [P, SLOTS, W3])
        neg_max = sb("neg_max", [P, SLOTS, QT])
        row_sum = sb("row_sum", [P, SLOTS, QT])
        row_fix = sb("row_fix", [P, SLOTS, QT])
        row_inv = sb("row_inv", [P, SLOTS, QT])
        causal = sb("causal", [P, W3])
        mask_now = sb("mask_now", [P, W3])
        mask_all = sb("mask_all", [P, B, W3], u8)
        mask_rows = sb("mask_rows", [B, S], u8)
        mask_f = sb("mask_f", [B, S])
        blind = sb("blind", [B, S])
        mean_rows = sb("mean_rows", [B, B, D])
        mean_y = sb("mean_y", [B, D])
        wq_s = sb("wq_s", [P, H * DK])
        wk_s = sb("wk_s", [P, H * DK])
        wv_s = sb("wv_s", [P, H * DK])
        wo_s = sb("wo_s", [P, PAIRS, D])
        w1_s = sb("w1_s", [P, E, F])
        w2_s = sb("w2_s", [P, E, FC, D])
        wr_s = sb("wr_s", [P, E])
        NB = 3 * PAIRS + E * FC
        bias_rows = sb("bias_rows", [NB, P])
        bias_T = sb("bias_T", [P, NB])
        relu_b1 = sb("relu_b1", [P, E * FC])
        br_all = sb("br_all", [P, E])
        bo_all = sb("bo_all", [P, D])
        tg_bo = sb("tg_bo", [P, D])
        gates = sb("gates", [P, 2])
        tg = sb("tg", [P, 2])
        ident = sb("ident", [P, P])
        before = sb("before", [P, P], bf16)
        ones_b = sb("ones_b", [P, P], bf16)
        ones_r = sb("ones_r", [1, P])
        mean_w = sb("mean_w", [P, 1])
        CTXR = 2
        ctx_ring = sb("ctx_ring", [P, CTXR, FULL, D])
        tail_ring = sb("tail_ring", [P, CTXR, D])
        ctx_sum = sb("ctx_sum", [P, B, D])
        ctx_mean = sb("ctx_mean", [P, B])
        u_T = sb("u_T", [P, PAIRS, B])
        stats = sb("stats", [P, NT, 6])
        mv = sb("mv", [P, NT, 2])
        rs_a = sb("rs_a", [P, NT])
        rs_y = sb("rs_y", [P, NT])
        rs_t = sb("rs_t", [P, NT])
        rstd = sb("rstd", [P, NT])
        nmr = sb("nmr", [P, NT])
        stats2 = sb("stats2", [P, QT, 6])
        mv2 = sb("mv2", [P, QT, 2])
        rstd2 = sb("rstd2", [P, QT])
        nmr2 = sb("nmr2", [P, QT])
        residual = sb("residual", [P, QT, D])
        rows = sb("rows", [P, QT, ROW])
        token_ids = sb("token_ids", [P, NT], i32)
        x2_T = sb("x2_T", [P, S])
        logits = sb("logits", [P, QT, E])
        best = sb("best", [P, QT])
        hit = sb("hit", [P, QT, E])
        pick = sb("pick", [P, QT])
        choice = sb("choice", [P, QT, E])
        choice_b = sb("choice_b", [P, QT, E], bf16)
        rank = sb("rank", [P, QT, E])
        slot_f = sb("slot_f", [P, QT])
        slot_i = sb("slot_i", [P, QT], i32)
        iota_i = sb("iota_i", [P, 64], i32)
        e_less = sb("e_less", [P, E])
        next_row = sb("next_row", [P, E])
        region = sb("region", [P, E])
        pad_rows = sb("pad_rows", [P, ROW])
        steps_f = sb("steps_f", [1, FULL + 8])
        tile_f = sb("tile_f", [1, NTILES])
        count_1 = sb("count_1", [1, E])
        full_c = sb("full_c", [1, E, 16])
        tiles_e = sb("tiles_e", [1, E])
        tiles_to = sb("tiles_to", [1, E])
        jump = sb("jump", [1, E])
        passed = sb("passed", [1, NTILES, E])
        jumped = sb("jumped", [1, NTILES, E])
        tab_f = sb("tab_f", [1, 2, NTILES])
        tile_expert = sb("tile_expert", [1, NTILES], i32)
        tile_row = sb("tile_row", [1, NTILES], i32)
        pad_at = sb("pad_at", [1, E], i32)
        b2_row = sb("b2_row", [1, E, D])
        c_row = sb("c_row", [1, E, D])
        c_sum = sb("c_sum", [1, D])
        rest_row = sb("rest_row", [1, E, D])
        tile_in = sb("tile_in", [P, RING, ROW])
        tile_T = sb("tile_T", [P, 2, P])
        w1_now = sb("w1_now", [P, 2, F])
        hidden = sb("hidden", [P, 2, F])
        tile_out = sb("tile_out", [P, RING, D])

        ps_s = [pb("ps_s0"), pb("ps_s1")]
        ps_t = [pb("ps_t0"), pb("ps_t1")]
        ps_o = pb("ps_o")
        ps_qk = pb("ps_qk")
        ps_v = pb("ps_v")
        ps_w = pb("ps_w")
        ps_lg = ps_w[:, 0:QT * E].rearrange("p (t e) -> p t e", e=E)
        ps_rk = ps_w[:, 0:QT * E].rearrange("p (t e) -> p t e", e=E)
        ps_ct = ps_w[:, QT * E:QT * E + E]
        ps_mean = ps_w[:, 0:B]
        ps_u = ps_w[:, 0:PAIRS * B]
        ps_y = ps_w[0:B, S:S + D]
        ps_x = ps_s
        ps_h = [(ps_t[0], ps_qk), (ps_t[1], ps_v)]
        ps_out = [ps_o, ps_w]
        ps_c = [ps_qk, ps_v]

        ld_x = [sem(f"ld_x{b}") for b in range(2)]
        ld_c = [sem(f"ld_c{b}") for b in range(2)]
        ld_wq, ld_wk, ld_wv, ld_wo = sem("ld_wq"), sem("ld_wk"), sem("ld_wv"), sem("ld_wo")
        ld_bias, ld_small, ld_mask, ld_ffn = sem("ld_bias"), sem("ld_small"), sem("ld_mask"), sem("ld_ffn")
        ld_ring = [sem(f"ld_ring{r}") for r in range(CTXR)]
        ring_free = sem("ring_free")
        const_ready = sem("const_ready")
        zero_ready, tails_zero = sem("zero_ready"), sem("tails_zero")
        pool_chain, dve_chain, act_chain = sem("pool_chain"), sem("dve_chain"), sem("act_chain")
        biasT_done, biasT_ready = sem("biasT_done"), sem("biasT_ready")
        tg_ready, tgbo_ready = sem("tg_ready"), sem("tgbo_ready")
        xnorm_ready, ctxnow_ready = sem("xnorm_ready"), sem("ctxnow_ready")
        inT_done, inT_ready = sem("inT_done"), sem("inT_ready")
        qk_done, v_done = sem("qk_done"), sem("v_done")
        qk_kept, qodd_kept, v_kept = sem("qk_kept"), sem("qodd_kept"), sem("v_kept")
        scores_done, max_ready, exp_done = sem("scores_done"), sem("max_ready"), sem("exp_done")
        inv_ready, prob_ready = sem("inv_ready"), sem("prob_ready")
        probT_done, probT_kept = sem("probT_done"), sem("probT_kept")
        pv_done, oT_kept = sem("pv_done"), sem("oT_kept")
        wo_done, x2_ready = sem("wo_done"), sem("x2_ready")
        residual_ready = sem("residual_ready")
        rows_ready, x2T_done, x2T_kept = sem("rows_ready"), sem("x2T_done"), sem("x2T_kept")
        logits_done, choice_ready, rank_done, slots_ready = (sem("logits_done"), sem("choice_ready"),
                                                             sem("rank_done"), sem("slots_ready"))
        scattered = sem("scattered")
        csum_ready, mean_done, mean_kept = sem("csum_ready"), sem("mean_done"), sem("mean_kept")
        u_done, u_kept, y_done, y_kept = sem("u_done"), sem("u_kept"), sem("y_done"), sem("y_kept")
        b1_ready, c_done, rest_ready = sem("b1_ready"), sem("c_done"), sem("rest_ready")
        table_ready, padded = sem("table_ready"), sem("padded")
        tile_loaded = [sem(f"tile_loaded{r}") for r in range(RING)]
        tileT_done, tileT_kept = sem("tileT_done"), sem("tileT_kept")
        w1_ready, h_done, h_act, h_dve = sem("w1_ready"), sem("h_done"), sem("h_act"), sem("h_dve")
        y2_done, out_ready = sem("y2_done"), sem("out_ready")
        out_stored = [sem(f"out_stored{r}") for r in range(RING)]

        block = ctx.enter_context(nc.Block())

        @block.sync
        def _(sp):
            x_v = x.rearrange("b (t p) d -> p b t d", p=P)
            c_v = ctx_in[:, 0:S, :].rearrange("b (t p) d -> p b t d", p=P)
            x_d = x_nat[:, :, :].rearrange("p (b t) d -> p b t d", t=QT)
            c_d = ctx_nat[:, :, :].rearrange("p (b t) d -> p b t d", t=QT)
            sp.dma_start(x_d[:, 0], x_v[:, 0]).then_inc(ld_x[0], 16)
            sp.dma_start(c_d[:, 0], c_v[:, 0]).then_inc(ld_c[0], 16)
            sp.dma_start(wq_s[:, :], wq).then_inc(ld_wq, 16)
            for i, (b_, n) in enumerate(((bq, PAIRS), (bk, PAIRS), (bv, PAIRS))):
                sp.dma_start(bias_rows[i * PAIRS:i * PAIRS + n, :],
                             b_.rearrange("(n p) -> n p", p=P)).then_inc(ld_bias, 16)
            sp.dma_start(bias_rows[3 * PAIRS:NB, :], b1.rearrange("e (c p) -> (e c) p", p=P)).then_inc(ld_bias, 16)
            sp.dma_start(wk_s[:, :], wk).then_inc(ld_wk, 16)
            sp.dma_start(wv_s[:, :], wv).then_inc(ld_wv, 16)
            sp.dma_start(mask_all[:, :, 0:P], mask[:, 0:P].partition_broadcast(P)).then_inc(ld_mask, 16)
            sp.dma_start(mask_all[:, :, P:W3], mask[:, 0:S].partition_broadcast(P)).then_inc(ld_mask, 16)
            sp.dma_start(mask_rows[:, :], mask[:, 0:S]).then_inc(ld_mask, 16)
            sp.dma_start(gates[:, 0:1], g_attn.partition_broadcast(P)).then_inc(ld_small, 16)
            sp.dma_start(gates[:, 1:2], g_ffn.partition_broadcast(P)).then_inc(ld_small, 16)
            sp.dma_start(bo_all[:, :], bo.partition_broadcast(P)).then_inc(ld_small, 16)
            sp.dma_start(br_all[:, :], br.partition_broadcast(P)).then_inc(ld_small, 16)
            sp.dma_start(wr_s[:, :], wr).then_inc(ld_small, 16)
            for b in range(1, B):
                sp.dma_start(x_d[:, b], x_v[:, b]).then_inc(ld_x[1], 16)
                sp.dma_start(c_d[:, b], c_v[:, b]).then_inc(ld_c[1], 16)
            sp.dma_start(wo_s[:, :, :], wo.rearrange("(c p) d -> p c d", p=P)).then_inc(ld_wo, 16)
            sp.wait_ge(tails_zero, 1)
            for b in range(B):
                r = b % CTXR
                wait(sp, ring_free, b - CTXR + 1)
                sp.dma_start(ctx_ring[:, r], ctx_in[b, 0:FULL * P, :].rearrange("(p j) d -> p j d", p=P)
                             ).then_inc(ld_ring[r], 16)
                sp.dma_start(tail_ring[0:TAIL, r], ctx_in[b, FULL * P:SK, :]).then_inc(ld_ring[r], 16)
            sp.dma_start(w1_s[:, :, :], w1.rearrange("e d f -> d e f")).then_inc(ld_ffn, 16)
            for e in range(E):
                sp.dma_start(w2_s[:, e], w2[e].rearrange("(c p) d -> p c d", p=P)).then_inc(ld_ffn, 16)
            sp.dma_start(b2_row[:, :, :], b2.rearrange("(o e) d -> o e d", o=1)).then_inc(ld_ffn, 16)

            sp.wait_ge(table_ready, 1)
            for e in range(E):
                at = sp.value_load(pad_at[0:1, e:e + 1], min_val=0, max_val=PADROW - P)
                sp.dma_start(sorted_rows[bass.ds(at, P), :], pad_rows[:, :]).then_inc(padded, 16)
            sp.dma_start(sorted_rows[PADROW:PADROW + P, :], pad_rows[:, :]).then_inc(padded, 16)
            sp.wait_ge(padded, 16 * (E + 1))
            sp.wait_ge(scattered, 16 * NT)
            for k in range(RING):
                at = sp.value_load(tile_row[0:1, k:k + 1], min_val=0, max_val=PADROW)
                sp.dma_start(tile_in[:, k], sorted_rows[bass.ds(at, P), :]).then_inc(tile_loaded[k], 16)
            with sp.Fori(1, NTILES // RING) as i:
                for r in range(RING):
                    at = sp.value_load(tile_row[0:1, bass.ds(i * RING + r, 1)], min_val=0, max_val=PADROW)
                    sp.wait_ge(out_stored[r], i * 16)
                    sp.dma_start(tile_in[:, r], sorted_rows[bass.ds(at, P), :]).then_inc(tile_loaded[r], 16)

        @block.gpsimd
        def _(pool):
            g = nc.gpsimd
            n = Count(pool, pool_chain)
            n.up(g.memset(ident[:, :], 0.0))
            n.up(g.memset(causal[:, :], 0.0))
            n.up(g.memset(ones_b[:, :], 1.0))
            n.wait()
            g.affine_select(out=ident[:, :], in_=ident[:, :], compare_op=ALU.not_equal, fill=1.0, base=0,
                            pattern=[[-1, P]], channel_multiplier=1).then_inc(const_ready, 1)
            for c0 in (0, 2 * P):
                g.affine_select(out=causal[:, c0:c0 + P], in_=causal[:, c0:c0 + P], compare_op=ALU.is_ge,
                                fill=MASKED, base=0, pattern=[[-1, P]], channel_multiplier=1
                                ).then_inc(const_ready, 1)
            g.affine_select(out=before[:, :], in_=ones_b[:, :], compare_op=ALU.is_gt, fill=0.0, base=0,
                            pattern=[[1, P]], channel_multiplier=-1).then_inc(const_ready, 1)
            g.memset(mean_w[:, :], 1.0 / SK).then_inc(const_ready, 1)
            g.memset(ones_r[:, :], 1.0).then_inc(const_ready, 1)
            n.up(g.iota(iota_i[:, :], pattern=[[1, 64]], base=0, channel_multiplier=0))
            g.iota(token_ids[:, :], pattern=[[P, NT]], base=0, channel_multiplier=1).then_inc(const_ready, 1)
            n.up(g.memset(pad_rows[:, :], 0.0))
            n.wait()
            g.memset(pad_rows[:, 2 * D:ROW].bitcast(i32), NOBODY).then_inc(const_ready, 1)
            g.tensor_scalar(e_less[:, :], iota_i[:, 0:E], -1000.0, None, ALU.add).then_inc(const_ready, 1)
            g.tensor_scalar(region[:, :], iota_i[:, 0:E], float(CAP), None, ALU.mult).then_inc(const_ready, 1)
            g.tensor_scalar(next_row[:, :], iota_i[:, 0:E], float(CAP), None, ALU.mult).then_inc(const_ready, 1)
            g.tensor_scalar(tile_f[:, :], iota_i[0:1, 0:NTILES], 1.0, None, ALU.mult).then_inc(const_ready, 1)
            g.tensor_scalar(steps_f[:, :], iota_i[0:1, 0:FULL + 8], float(P), None, ALU.mult
                            ).then_inc(const_ready, 1)
            q_v = q_pad[:, :, :].rearrange("p (n two) s -> p n two s", two=2)
            pool.wait_ge(const_ready, 13)
            g.memset(q_v[0:DK, :, 1, :], 0.0).then_inc(zero_ready, 1)
            pool.wait_ge(zero_ready, 1)
            g.memset(q_v[DK:P, :, 0, :], 0.0).then_inc(zero_ready, 1)
            pool.wait_ge(zero_ready, 2)
            g.memset(tail_ring[:, :, :], 0.0).then_inc(tails_zero, 1)
            pool.wait_ge(tg_ready, 1)
            pool.wait_ge(tails_zero, 1)
            g.tensor_scalar(tg_bo[:, :], bo_all[:, :], tg[:, 0:1], None, ALU.mult).then_inc(tgbo_ready, 1)

            def normalise(p, h, slot):
                head = 2 * p + h
                pool.wait_ge(inv_ready, head + 1)
                g.tensor_tensor(prob[:, slot, 0:P], prob[:, slot, 0:P],
                                row_inv[:, slot, 0:1].to_broadcast([P, P]), ALU.mult).then_inc(prob_ready, 1)
                g.tensor_tensor(prob[:, slot, P:W3], prob[:, slot, P:W3],
                                row_inv[:, slot, 1:2].to_broadcast([P, S]), ALU.mult).then_inc(prob_ready, 1)

            def residual_of(b):
                wait(pool, x2_ready, 2 * b)
                pool.wait_ge(ld_x[1], 16 * (B - 1))
                g.tensor_tensor(residual[:, :, :], x_nat[:, bass.ds(b * QT, QT), :],
                                tg_bo[:, None, :].to_broadcast([P, QT, D]), ALU.add).then_inc(residual_ready, 1)

            def scatter(b):
                pool.wait_ge(slots_ready, b + 1)
                settle(pool)
                for t in range(QT):
                    g.indirect_dma_start(out=sorted_rows[:, :],
                                         out_offset=bass.IndirectOffsetOnAxis(ap=slot_i[:, t:t + 1], axis=0),
                                         in_=rows[:, t, :], in_offset=None).then_inc(scattered, 16)

            def batch(b, first=False, last=False):
                for j in range(PAIRS):
                    if not (last and j == PAIRS - 1):
                        for h in range(2):
                            normalise(8 * b + j + 1, h, (2 * (j + 1) + h) % SLOTS)
                    if j == 1:
                        if first:
                            pool.wait_ge(tgbo_ready, 1)
                        residual_of(b)
                    if j == 6 and not first:
                        scatter(b - 1)

            for h in range(2):
                normalise(0, h, h)
            batch(0, first=True)
            with pool.Fori(1, B - 1) as b:
                batch(b)
            batch(B - 1, last=True)
            scatter(B - 1)

            def store(i, r):
                pool.wait_ge(out_ready, i * RING + r + 1)
                settle(pool)
                g.indirect_dma_start(
                    out=out_rows, out_offset=bass.IndirectOffsetOnAxis(
                        ap=tile_in[:, r, 2 * D:ROW].bitcast(i32), axis=0),
                    in_=tile_out[:, r, :], in_offset=None, bounds_check=B * S - 1, oob_is_err=False
                ).then_inc(out_stored[r], 16)

            out_rows = out.rearrange("b s d -> (b s) d")
            with pool.Fori(0, NTILES // RING) as i:
                for r in range(RING):
                    store(i, r)
            for r in range(RING):
                pool.wait_ge(out_stored[r], 16 * (NTILES // RING))

        @block.scalar
        def _(act):
            s = nc.scalar
            act.wait_ge(ld_small, 16 * 5)
            s.activation(tg[:, :], gates[:, :], ACT.Tanh).then_inc(tg_ready, 1)

            def context_now(b):
                act.wait_ge(ld_c[0], 16)
                if not isinstance(b, int) or b > 0:
                    act.wait_ge(ld_c[1], 16 * (B - 1))
                wait(act, inT_done, b)
                s.activation(ctx_now[:, :, :], ctx_nat[:, bass.ds(b * QT, QT), :], ACT.Copy
                             ).then_inc(ctxnow_ready, 1)

            def keep_inT(b):
                act.wait_ge(inT_done, b + 1)
                s.activation(in_T[:, :], ps_qk[:, :], ACT.Copy).then_inc(inT_ready, 1)

            def keep_qk(p, j):
                act.wait_ge(qk_done, p + 1)
                s.activation(q_pad[0:DK, 2 * j, :], ps_qk[0:DK, 0:S], ACT.Identity,
                             bias=bias_T[0:DK, j:j + 1]).then_inc(qk_kept, 1)
                act.wait_ge(qodd_kept, p + 1)
                s.activation(k_T[:, j, :], ps_qk[:, S:2 * S], ACT.Identity,
                             bias=bias_T[:, PAIRS + j:PAIRS + j + 1]).then_inc(qk_kept, 1)

            def keep_v(p, j):
                act.wait_ge(v_done, p + 1)
                s.activation(v_nat[:, :, j * P:(j + 1) * P],
                             ps_v[:, 0:S].rearrange("p (t n) -> p t n", t=QT), ACT.Copy).then_inc(v_kept, 1)

            def exponential(p, h, slot):
                head = 2 * p + h
                act.wait_ge(max_ready, 2 * head + 2)
                wait(act, probT_done, head + 1 - SLOTS)
                for t, (lo, hi) in enumerate(((0, P), (P, W3))):
                    s.activation(prob[:, slot, lo:hi], masked[:, slot % 2, lo:hi], ACT.Exp,
                                 bias=neg_max[:, slot, t:t + 1], scale=-1.0,
                                 accum_out=row_sum[:, slot, t:t + 1]).then_inc(exp_done, 1)

            def keep_x2T(b):
                act.wait_ge(x2T_done, b + 1)
                s.activation(x2_T[:, :], ps_w[:, S:2 * S], ACT.Copy).then_inc(x2T_kept, 1)

            def batch(b, first=False, last=False):
                for j in range(PAIRS):
                    if j == 0 and not last:
                        context_now(b + 1)
                    if not (last and j == PAIRS - 1):
                        for h in range(2):
                            exponential(8 * b + j + 1, h, (2 * (j + 1) + h) % SLOTS)
                    if not last:
                        if j == 0:
                            keep_inT(b + 1)
                        else:
                            keep_qk(8 * (b + 1) + j - 1, j - 1)
                            keep_v(8 * (b + 1) + j - 1, j - 1)
                    if first and j == 7:
                        act.wait_ge(mean_done, 1)
                        s.activation(ctx_mean[:, :], ps_mean, ACT.Copy).then_inc(mean_kept, 1)
                        act.wait_ge(u_done, 1)
                        s.activation(u_T[:, :, :], ps_u.rearrange("p (n b) -> p n b", b=B), ACT.Copy
                                     ).then_inc(u_kept, 1)
                    if j == 3 and not first:
                        keep_x2T(b - 1)
                if not last:
                    keep_qk(8 * (b + 1) + 7, 7)
                    keep_v(8 * (b + 1) + 7, 7)

            context_now(0)
            act.wait_ge(biasT_done, 1)
            s.activation(bias_T[:, :], ps_w[:, 0:NB], ACT.Copy).then_inc(biasT_ready, 1)
            keep_inT(0)
            act.wait_ge(biasT_ready, 1)
            act.wait_ge(zero_ready, 2)
            for j in range(PAIRS):
                keep_qk(j, j)
                keep_v(j, j)
            for h in range(2):
                exponential(0, h, h)
            batch(0, first=True)
            with act.Fori(1, B - 1) as b:
                batch(b)
            batch(B - 1, last=True)
            s.activation(relu_b1[:, :], bias_T[:, 3 * PAIRS:NB], ACT.Relu).then_inc(b1_ready, 1)
            keep_x2T(B - 1)

            act.wait_ge(table_ready, 1)
            with act.Fori(0, NTILES // RING) as i:
                for r in range(RING):
                    tile = i * RING + r
                    expert = act.value_load(tile_expert[0:1, bass.ds(tile, 1)], min_val=0, max_val=E - 1)
                    act.wait_ge(tileT_done, tile + 1)
                    s.activation(tile_T[:, r % 2, :], ps_x[r % 2][:, 0:P], ACT.Copy).then_inc(tileT_kept, 1)
                    act.wait_ge(h_done, tile + 1)
                    for c in range(2):
                        s.activation(hidden[:, r % 2, c * P:(c + 1) * P], ps_h[r % 2][0][:, c * P:(c + 1) * P], ACT.Relu,
                                     bias=bias_T[:, bass.ds(expert * FC + 3 * PAIRS + c, 1)]).then_inc(h_act, 1)

        @block.vector
        def _(dve):
            v = nc.vector
            n = Count(dve, dve_chain)

            def inverse_root(a, y, t, final):
                n.wait()
                n.up(v.tensor_scalar(y.bitcast(i32), a.bitcast(i32), -0.5, RS_MAGIC, ALU.mult, ALU.add))
                for step in range(3):
                    n.wait()
                    n.up(v.tensor_tensor(t, y, y, ALU.mult))
                    n.wait()
                    n.up(v.scalar_tensor_tensor(out=t, in0=t, scalar=-0.5, in1=a, op0=ALU.mult, op1=ALU.mult))
                    n.wait()
                    n.up(v.scalar_tensor_tensor(out=final if step == 2 else y, in0=t, scalar=1.5, in1=y,
                                                op0=ALU.add, op1=ALU.mult))
                n.wait()

            def norm_stats(t):
                n.up(v.bn_stats(stats[:, t, :], x_nat[:, t, :]))
                n.wait()
                n.up(v.bn_aggr(mv[:, t, :], stats[:, t, :]))

            def norm_scales(lo, hi):
                n.wait()
                n.up(v.tensor_scalar(rs_a[:, lo:hi], mv[:, lo:hi, 1], EPS, None, ALU.add))
                inverse_root(rs_a[:, lo:hi], rs_y[:, lo:hi], rs_t[:, lo:hi], rstd[:, lo:hi])
                n.up(v.scalar_tensor_tensor(out=nmr[:, lo:hi], in0=mv[:, lo:hi, 0], scalar=-1.0, in1=rstd[:, lo:hi],
                                            op0=ALU.mult, op1=ALU.mult))
                n.wait()

            def normalise_x(b):
                wait(dve, inT_done, b)
                for t in range(QT):
                    i = b * QT + t
                    v.tensor_scalar(x_norm[:, t, :], x_nat[:, bass.ds(i, 1), :], rstd[:, bass.ds(i, 1)],
                                    nmr[:, bass.ds(i, 1)], ALU.mult, ALU.add).then_inc(xnorm_ready, 1)

            def mask_of(b):
                n.up(v.scalar_tensor_tensor(out=mask_now[:, :], in0=mask_all[:, bass.ds(b, 1), :], scalar=MASKED,
                                            in1=causal[:, :], op0=ALU.mult, op1=ALU.add))
                n.wait()

            def maximum(p, h, slot):
                head = 2 * p + h
                dve.wait_ge(scores_done, head + 1)
                wait(dve, exp_done, 2 * (head - 1))
                settle(dve)
                for t, (lo, hi) in enumerate(((0, P), (P, W3))):
                    v.tensor_tensor_reduce(out=masked[:, slot % 2, lo:hi], in0=ps_s[slot % 2][:, lo:hi],
                                           in1=mask_now[:, lo:hi], scale=-SCALE, scalar=FLOOR, op0=ALU.add,
                                           op1=ALU.min, accum_out=neg_max[:, slot, t:t + 1]).then_inc(max_ready, 1)

            def inverse_sum(p, h, slot):
                head = 2 * p + h
                dve.wait_ge(exp_done, 2 * head + 2)
                n.up(v.tensor_scalar(row_fix[:, slot, :], row_sum[:, slot, :], 1e-30, None, ALU.max))
                wait(dve, prob_ready, 2 * (head + 1 - SLOTS))
                n.wait()
                v.reciprocal(row_inv[:, slot, :], row_fix[:, slot, :]).then_inc(inv_ready, 1)

            def keep_probT(p, h, slot):
                head = 2 * p + h
                dve.wait_ge(probT_done, head + 1)
                wait(dve, pv_done, p - 1)
                v.tensor_copy(prob_T[:, slot, :], ps_t[slot % 2][:, 0:W3]).then_inc(probT_kept, 1)

            def keep_qodd(p, j):
                dve.wait_ge(qk_done, p + 1)
                v.tensor_scalar(q_pad[DK:P, 2 * j + 1, :], ps_qk[DK:P, 0:S], bias_T[DK:P, j:j + 1], None, ALU.add
                                ).then_inc(qodd_kept, 1)

            def keep_oT(b, p, j):
                dve.wait_ge(pv_done, p + 1)
                wait(dve, wo_done, b)
                v.tensor_scalar(o_T[:, j, :], ps_o[:, 0:S], bias_T[:, 2 * PAIRS + j:2 * PAIRS + j + 1],
                                None, ALU.add).then_inc(oT_kept, 1)

            def second_norm(b):
                dve.wait_ge(wo_done, b + 1)
                dve.wait_ge(residual_ready, b + 1)
                wait(dve, scattered, 16 * QT * b)
                for t in range(QT):
                    v.scalar_tensor_tensor(out=rows[:, t, 0:D], in0=ps_w[:, t * D:(t + 1) * D], scalar=tg[:, 0:1],
                                           in1=residual[:, t, :], op0=ALU.mult, op1=ALU.add).then_inc(x2_ready, 1)
                n.up(v.tensor_copy(rows[:, :, 2 * D].bitcast(i32), token_ids[:, bass.ds(b * QT, QT)]))
                dve.wait_ge(x2_ready, 2 * (b + 1))
                for t in range(QT):
                    n.up(v.bn_stats(stats2[:, t, :], rows[:, t, 0:D]))
                n.wait()
                settle(dve)
                for t in range(QT):
                    n.up(v.bn_aggr(mv2[:, t, :], stats2[:, t, :]))
                n.wait()

            def second_norm_rows(b):
                n.up(v.tensor_scalar(rs_a[:, 0:QT], mv2[:, :, 1], EPS, None, ALU.add))
                inverse_root(rs_a[:, 0:QT], rs_y[:, 0:QT], rs_t[:, 0:QT], rstd2[:, :])
                n.up(v.scalar_tensor_tensor(out=nmr2[:, :], in0=mv2[:, :, 0], scalar=-1.0, in1=rstd2[:, :],
                                            op0=ALU.mult, op1=ALU.mult))
                n.wait()
                for t in range(QT):
                    v.tensor_scalar(rows[:, t, D:2 * D], rows[:, t, 0:D], rstd2[:, t:t + 1], nmr2[:, t:t + 1],
                                    ALU.mult, ALU.add).then_inc(rows_ready, 1)

            def choose(b):
                dve.wait_ge(logits_done, b + 1)
                n.up(v.tensor_tensor(logits[:, :, :], ps_lg, br_all[:, None, :].to_broadcast([P, QT, E]), ALU.add))
                n.wait()
                n.up(v.reduce_max(best[:, :], logits[:, :, :], AX.X))
                n.wait()
                n.up(v.tensor_tensor(hit[:, :, :], logits[:, :, :], best[:, :, None].to_broadcast([P, QT, E]),
                                     ALU.is_equal))
                n.wait()
                n.up(v.tensor_tensor(hit[:, :, :], hit[:, :, :], e_less[:, None, :].to_broadcast([P, QT, E]),
                                     ALU.mult))
                n.wait()
                n.up(v.tensor_reduce(pick[:, :], hit[:, :, :], AX.X, ALU.min))
                n.wait()
                n.up(v.tensor_tensor(choice[:, :, :], e_less[:, None, :].to_broadcast([P, QT, E]),
                                     pick[:, :, None].to_broadcast([P, QT, E]), ALU.is_equal))
                v.tensor_tensor(choice_b[:, :, :], e_less[:, None, :].to_broadcast([P, QT, E]),
                                pick[:, :, None].to_broadcast([P, QT, E]), ALU.is_equal).then_inc(choice_ready, 1)

            def place(b):
                dve.wait_ge(rank_done, b + 1)
                n.wait()
                n.up(v.tensor_tensor(rank[:, :, :], ps_rk, next_row[:, None, :].to_broadcast([P, QT, E]), ALU.add))
                n.wait()
                n.up(v.tensor_tensor(rank[:, :, :], rank[:, :, :], choice[:, :, :], ALU.mult))
                n.up(v.tensor_tensor(next_row[:, :], next_row[:, :], ps_ct, ALU.add))
                n.wait()
                n.up(v.reduce_sum(slot_f[:, :], rank[:, :, :], AX.X))
                n.wait()
                v.tensor_copy(slot_i[:, :], slot_f[:, :]).then_inc(slots_ready, 1)

            def sum_context(b):
                r = b % CTXR
                dve.wait_ge(ld_ring[r], 32 * (b // CTXR + 1))
                n.up(v.reduce_sum(ctx_sum[:, b, :], ctx_ring[:, r].rearrange("p j d -> p d j"), AX.X))
                n.wait()
                v.tensor_tensor(ctx_sum[:, b, :], ctx_sum[:, b, :], tail_ring[:, r, :], ALU.add
                                ).then_inc(csum_ready, 1)
                dve.wait_ge(csum_ready, b + 1)
                v.engine_nop().then_inc(ring_free, 1)

            def batch(b, first=False, last=False):
                for j in range(PAIRS):
                    p = 8 * b + j
                    if j == 0 and not last:
                        normalise_x(b + 1)
                    for h in range(2):
                        if not (last and j == PAIRS - 1):
                            maximum(p + 1, h, (2 * (j + 1) + h) % SLOTS)
                        keep_probT(p, h, (2 * j + h) % SLOTS)
                    if not (last and j == PAIRS - 1):
                        inverse_sum(p + 1, 0, (2 * (j + 1)) % SLOTS)
                        if not last and j > 0:
                            keep_qodd(8 * (b + 1) + j - 1, j - 1)
                        inverse_sum(p + 1, 1, (2 * (j + 1) + 1) % SLOTS)
                    keep_oT(b, p, j)
                    if j == 6 and not last:
                        dve.wait_ge(max_ready, 2 * 16 * (b + 1))
                        mask_of(b + 1)
                    if first:
                        if j < 7:
                            sum_context(j)
                        else:
                            n.up(v.tensor_copy(mask_f[:, :], mask_rows[:, :]))
                            n.wait()
                            v.tensor_tensor_scan(blind[:, :], mask_f[:, :], mask_f[:, :], 1.0, ALU.min, ALU.min
                                                 ).then_inc(y_kept, 1)
                            dve.wait_ge(y_done, 1)
                            n.up(v.tensor_copy(mean_y[:, :], ps_y))
                            n.wait()
                            v.tensor_tensor(mean_rows[:, :, :], mean_y[:, None, :].to_broadcast([B, B, D]),
                                            ident[0:B, 0:B, None].to_broadcast([B, B, D]), ALU.mult
                                            ).then_inc(y_kept, 1)
                        if j == 6:
                            sum_context(7)
                    else:
                        if j == 0:
                            second_norm(b - 1)
                        if j == 1:
                            second_norm_rows(b - 1)
                        if j == 4:
                            choose(b - 1)
                        if j == 5:
                            place(b - 1)
                if not last:
                    keep_qodd(8 * (b + 1) + 7, 7)

            dve.wait_ge(ld_x[0], 16)
            for t in range(QT):
                norm_stats(t)
            norm_scales(0, QT)
            normalise_x(0)
            dve.wait_ge(ld_mask, 16 * 3)
            dve.wait_ge(const_ready, 13)
            mask_of(0)
            dve.wait_ge(biasT_ready, 1)
            dve.wait_ge(zero_ready, 2)
            dve.wait_ge(ld_x[1], 16 * (B - 1))
            for j in range(PAIRS):
                keep_qodd(j, j)
                if j > 0:
                    for t in range(QT):
                        norm_stats(j * QT + t)
            norm_scales(QT, NT)
            for h in range(2):
                maximum(0, h, h)
                inverse_sum(0, h, h)
            batch(0, first=True)
            dve.wait_ge(ld_small, 16 * 5)
            dve.wait_ge(const_ready, 13)
            with dve.Fori(1, B - 1) as b:
                n.enter(b - 1, PER_BATCH)
                batch(b)
                n.leave(B - 2)
            batch(B - 1, last=True)
            second_norm(B - 1)
            second_norm_rows(B - 1)
            choose(B - 1)
            place(B - 1)

            n.up(v.tensor_tensor(count_1[:, :], next_row[0:1, :], region[0:1, :], ALU.subtract))
            n.up(v.tensor_copy(pad_at[:, :], next_row[0:1, :]))
            n.wait()
            n.up(v.tensor_tensor(full_c[:, :, :], count_1[:, :, None].to_broadcast([1, E, 16]),
                                 steps_f[:, None, 0:16].to_broadcast([1, E, 16]), ALU.is_gt))
            n.wait()
            n.up(v.reduce_sum(tiles_e[:, :], full_c[:, :, :], AX.X))
            n.wait()
            n.up(v.tensor_tensor_scan(tiles_to[:, :], ones_r[0:1, 0:E], tiles_e[:, :], 0.0, ALU.mult, ALU.add))
            n.up(v.tensor_scalar(jump[:, :], tiles_e[:, :], -float(P), float(CAP), ALU.mult, ALU.add))
            n.wait()
            n.up(v.tensor_tensor(passed[:, :, :], tile_f[:, :, None].to_broadcast([1, NTILES, E]),
                                 tiles_to[:, None, :].to_broadcast([1, NTILES, E]), ALU.is_ge))
            n.wait()
            n.up(v.reduce_sum(tab_f[:, 0, :], passed[:, :, :], AX.X))
            n.up(v.tensor_tensor(jumped[:, :, :], passed[:, :, :], jump[:, None, :].to_broadcast([1, NTILES, E]),
                                 ALU.mult))
            n.wait()
            n.up(v.reduce_sum(tab_f[:, 1, :], jumped[:, :, :], AX.X))
            n.up(v.tensor_scalar(tile_expert[:, :], tab_f[:, 0, :], float(E - 1), None, ALU.min))
            n.wait()
            n.up(v.scalar_tensor_tensor(out=tab_f[:, 1, :], in0=tile_f[:, :], scalar=float(P), in1=tab_f[:, 1, :],
                                        op0=ALU.mult, op1=ALU.add))
            n.wait()
            n.up(v.tensor_scalar(tile_row[:, :], tab_f[:, 1, :], float(PADROW), None, ALU.min))
            n.wait()
            v.engine_nop().then_inc(table_ready, 1)

            dve.wait_ge(c_done, 1)
            for half in range(2):
                n.up(v.tensor_copy(c_row[:, half * 4:half * 4 + 4, :],
                                   ps_c[half][0:1, :].rearrange("p (e d) -> p e d", d=D)))
            n.wait()
            n.up(v.tensor_tensor(c_row[:, :, :], c_row[:, :, :], b2_row[:, :, :], ALU.add))
            n.wait()
            n.up(v.reduce_sum(c_sum[:, :], c_row[:, :, :].rearrange("p e d -> p d e"), AX.X))
            n.wait()
            n.up(v.tensor_tensor(c_row[:, :, :], b2_row[:, :, :], c_row[:, :, :], ALU.subtract))
            n.wait()
            v.tensor_tensor(rest_row[:, :, :], c_row[:, :, :], c_sum[:, None, :].to_broadcast([1, E, D]), ALU.add
                            ).then_inc(rest_ready, 1)

            def w1_of(tile, r, free):
                expert = dve.value_load(tile_expert[0:1, bass.ds(tile, 1)], min_val=0, max_val=E - 1)
                wait(dve, h_done, free)
                v.tensor_copy(w1_now[:, r % 2, :], w1_s[:, bass.ds(expert, 1), :]).then_inc(w1_ready, 1)

            def relu_half(tile, r):
                expert = dve.value_load(tile_expert[0:1, bass.ds(tile, 1)], min_val=0, max_val=E - 1)
                dve.wait_ge(h_done, tile + 1)
                for c in range(2, FC):
                    v.tensor_scalar(hidden[:, r % 2, c * P:(c + 1) * P], ps_h[r % 2][1][:, c * P:(c + 1) * P],
                                    bias_T[:, bass.ds(expert * FC + 3 * PAIRS + c, 1)], 0.0, ALU.add, ALU.max
                                    ).then_inc(h_dve, 1)

            def finish(tile, r):
                dve.wait_ge(y2_done, tile + 1)
                v.scalar_tensor_tensor(out=tile_out[:, r, :], in0=ps_out[r % 2][:, 0:D], scalar=tg[:, 1:2],
                                       in1=tile_in[:, r, 0:D], op0=ALU.mult, op1=ALU.add).then_inc(out_ready, 1)

            dve.wait_ge(ld_ffn, 16 * (E + 2))
            w1_of(0, 0, 0)
            w1_of(1, 1, 0)
            relu_half(0, 0)
            for r in range(1, RING):
                w1_of(r + 1, r + 1, r)
                relu_half(r, r)
                finish(r - 1, r - 1)
            with dve.Fori(1, NTILES // RING - 1) as i:
                for r in range(RING):
                    tile = i * RING + r
                    w1_of(tile + 1, r + 1, tile)
                    relu_half(tile, r)
                    finish(tile - 1, (r - 1) % RING)
            last = NTILES // RING - 1
            for r in range(RING):
                tile = last * RING + r
                if r < RING - 1:
                    w1_of(tile + 1, r + 1, tile)
                relu_half(tile, r)
                finish(tile - 1, (r - 1) % RING)
            finish(NTILES - 1, RING - 1)

        @block.tensor
        def _(pe):
            t_ = nc.tensor

            def mm(out_, lhsT, rhs, start=True, stop=True, loose=False):
                return t_.matmul(out_, lhsT, rhs, start=start, stop=stop, skip_group_check=loose)

            def input_transposes(b):
                pe.wait_ge(xnorm_ready, 2 * b + 2)
                pe.wait_ge(ctxnow_ready, b + 1)
                wait(pe, qk_kept, 16 * b)
                wait(pe, qodd_kept, 8 * b)
                for t in range(QT):
                    t_.transpose(ps_qk[:, t * P:(t + 1) * P], x_norm[:, t, :], ident[:, :])
                for t in range(QT):
                    last = t_.transpose(ps_qk[:, S + t * P:S + (t + 1) * P], ctx_now[:, t, :], ident[:, :])
                last.then_inc(inT_done, 1)

            def project_qk(b, j):
                p = 8 * b + j
                if j == 0:
                    pe.wait_ge(inT_ready, b + 1)
                wait(pe, qk_kept, 2 * p)
                wait(pe, qodd_kept, p)
                mm(ps_qk[:, 0:S], wq_s[:, j * P:(j + 1) * P], xT)
                mm(ps_qk[:, S:2 * S], wk_s[:, j * P:(j + 1) * P], cT).then_inc(qk_done, 1)

            def project_v(b, j):
                p = 8 * b + j
                wait(pe, v_kept, p)
                for t in range(QT):
                    last = mm(ps_v[:, t * P:(t + 1) * P], cT[:, t * P:(t + 1) * P], wv_s[:, j * P:(j + 1) * P])
                last.then_inc(v_done, 1)

            def scores(p, j, h):
                head = 2 * p + h
                pe.wait_ge(qk_kept, 2 * p + 2)
                if h == 1:
                    pe.wait_ge(qodd_kept, p + 1)
                wait(pe, max_ready, 2 * (head - 1))
                mm(ps_s[h][:, 0:P], q_pad[:, 2 * j + h, 0:P], k_T[:, j, 0:P])
                mm(ps_s[h][:, P:W3], q_pad[:, 2 * j + h, P:S], k_T[:, j, :]).then_inc(scores_done, 1)

            def transpose_probs(p, h, slot):
                head = 2 * p + h
                pe.wait_ge(prob_ready, 2 * head + 2)
                wait(pe, probT_kept, head - 1)
                for i in range(3):
                    last = t_.transpose(ps_t[slot % 2][:, i * P:(i + 1) * P], prob[:, slot, i * P:(i + 1) * P],
                                        ident[:, :])
                last.then_inc(probT_done, 1)

            def values(p, j):
                pe.wait_ge(probT_kept, 2 * p + 2)
                pe.wait_ge(v_kept, p + 1)
                wait(pe, oT_kept, p)
                for t in range(QT):
                    for h in range(2):
                        slot = (2 * j + h) % SLOTS
                        last = mm(ps_o[h * DK:(h + 1) * DK, t * P:S],
                                  v_nat[:, t, (2 * j + h) * DK:(2 * j + h + 1) * DK],
                                  prob_T[:, slot, t * S:t * S + S - t * P], start=t == 0, stop=t == QT - 1)
                last.then_inc(pv_done, 1)

            def output_projection(b):
                pe.wait_ge(oT_kept, 8 * b + 8)
                wait(pe, slots_ready, b)
                for t in range(QT):
                    for c in range(PAIRS):
                        mm(ps_w[:, t * P:(t + 1) * P], o_T[:, c, t * P:(t + 1) * P], wo_s[:, c, :],
                           start=c == 0, stop=False)
                    last = mm(ps_w[:, t * P:(t + 1) * P], blind[:, t * P:(t + 1) * P],
                              mean_rows[:, bass.ds(b, 1), :], start=False, stop=True)
                last.then_inc(wo_done, 1)

            def norm_transposes(b):
                pe.wait_ge(rows_ready, 2 * b + 2)
                for t in range(QT):
                    last = t_.transpose(ps_w[:, S + t * P:S + (t + 1) * P], rows[:, t, D:2 * D], ident[:, :])
                last.then_inc(x2T_done, 1)

            def router(b):
                pe.wait_ge(x2T_kept, b + 1)
                for t in range(QT):
                    last = mm(ps_lg[:, t, :], x2_T[:, t * P:(t + 1) * P], wr_s[:, :])
                last.then_inc(logits_done, 1)

            def ranks(b):
                pe.wait_ge(choice_ready, b + 1)
                mm(ps_rk[:, 0, :], before[:, :], choice_b[:, 0, :])
                mm(ps_rk[:, 1, :], before[:, :], choice_b[:, 1, :], stop=False)
                mm(ps_rk[:, 1, :], ones_b[:, :], choice_b[:, 0, :], start=False)
                mm(ps_ct, ones_b[:, :], choice_b[:, 0, :], stop=False)
                mm(ps_ct, ones_b[:, :], choice_b[:, 1, :], start=False).then_inc(rank_done, 1)

            def blind_rows():
                pe.wait_ge(csum_ready, B)
                for b in range(B):
                    last = mm(ps_mean[:, b:b + 1], ctx_sum[:, b, :], mean_w[:, :])
                last.then_inc(mean_done, 1)
                pe.wait_ge(mean_kept, 1)
                for c in range(PAIRS):
                    last = mm(ps_u[:, c * B:(c + 1) * B], wv_s[:, c * P:(c + 1) * P], ctx_mean[:, :])
                last.then_inc(u_done, 1)
                pe.wait_ge(u_kept, 1)
                for c in range(PAIRS):
                    last = mm(ps_y, u_T[:, c, :], wo_s[:, c, :], start=c == 0, stop=c == PAIRS - 1)
                last.then_inc(y_done, 1)

            def batch(b, first=False, last=False):
                for j in range(PAIRS):
                    p = 8 * b + j
                    for h in range(2):
                        if not (last and j == PAIRS - 1):
                            scores(p + 1, (j + 1) % PAIRS, h)
                        transpose_probs(p, h, (2 * j + h) % SLOTS)
                    if not last:
                        if j == 0:
                            input_transposes(b + 1)
                        else:
                            project_qk(b + 1, j - 1)
                    if not first:
                        if j == 2:
                            norm_transposes(b - 1)
                        if j == 4:
                            router(b - 1)
                        if j == 5:
                            ranks(b - 1)
                    values(p, j)
                    if not last and j > 0:
                        project_v(b + 1, j - 1)
                if first:
                    pe.wait_ge(ld_wo, 16)
                    blind_rows()
                if not last:
                    project_qk(b + 1, 7)
                    project_v(b + 1, 7)
                if first:
                    pe.wait_ge(y_kept, 2)
                output_projection(b)

            pe.wait_ge(const_ready, 13)
            pe.wait_ge(ld_bias, 16 * 4)
            t_.transpose(ps_w[:, 0:NB], bias_rows[:, :], ident[0:NB, 0:NB]).then_inc(biasT_done, 1)
            input_transposes(0)
            pe.wait_ge(ld_wq, 16)
            pe.wait_ge(ld_wk, 16)
            pe.wait_ge(ld_wv, 16)
            for j in range(PAIRS):
                project_qk(0, j)
                project_v(0, j)
            for h in range(2):
                scores(0, 0, h)
            batch(0, first=True)
            pe.wait_ge(ld_small, 16 * 5)
            with pe.Fori(1, B - 1) as b:
                batch(b)
            batch(B - 1, last=True)

            pe.wait_ge(b1_ready, 1)
            pe.wait_ge(ld_ffn, 16 * (E + 2))
            pe.wait_ge(v_kept, 8 * B)
            def constants(e):
                for c in range(FC):
                    last = mm(ps_c[e // 4][0:1, e % 4 * D:(e % 4 + 1) * D], relu_b1[:, e * FC + c:e * FC + c + 1],
                              w2_s[:, e, c, :], start=c == 0, stop=c == FC - 1)
                return last
            for e in range(4):
                constants(e)
            norm_transposes(B - 1)
            router(B - 1)
            ranks(B - 1)
            for e in range(4, E):
                last = constants(e)
            last.then_inc(c_done, 1)

            def tile_transpose(tile, r, turn):
                pe.wait_ge(tile_loaded[r], 16 * turn + 16)
                wait(pe, tileT_kept, tile - 1)
                t_.transpose(ps_x[r % 2][:, 0:P], tile_in[:, r, D:2 * D], ident[:, :]).then_inc(tileT_done, 1)

            def first_product(tile, r):
                pe.wait_ge(tileT_kept, tile + 1)
                pe.wait_ge(w1_ready, tile + 1)
                wait(pe, h_act, 2 * (tile - 1))
                wait(pe, h_dve, 2 * (tile - 1))
                for c in range(FC):
                    last = mm(ps_h[r % 2][c // 2][:, c * P:(c + 1) * P], w1_now[:, r % 2, c * P:(c + 1) * P],
                              tile_T[:, r % 2, :])
                last.then_inc(h_done, 1)

            def second_product(tile, r):
                expert = pe.value_load(tile_expert[0:1, bass.ds(tile, 1)], min_val=0, max_val=E - 1)
                wait(pe, out_ready, tile - 1)
                pe.wait_ge(h_act, 2 * tile + 2)
                pe.wait_ge(h_dve, 2 * tile + 2)
                mm(ps_out[r % 2][:, 0:D], ones_r[:, :], rest_row[:, bass.ds(expert, 1), :], stop=False)
                for c in range(FC):
                    last = mm(ps_out[r % 2][:, 0:D], hidden[:, r % 2, c * P:(c + 1) * P],
                              w2_s[:, bass.ds(expert, 1), c, :], start=False, stop=c == FC - 1)
                last.then_inc(y2_done, 1)

            pe.wait_ge(table_ready, 1)
            pe.wait_ge(rest_ready, 1)
            tile_transpose(0, 0, 0)
            first_product(0, 0)
            tile_transpose(1, 1, 0)
            for r in range(1, RING):
                first_product(r, r)
                tile_transpose(r + 1, (r + 1) % RING, (r + 1) // RING)
                second_product(r - 1, r - 1)
            with pe.Fori(1, NTILES // RING - 1) as i:
                for r in range(RING):
                    tile = i * RING + r
                    first_product(tile, r)
                    tile_transpose(tile + 1, (r + 1) % RING, i + (r + 1) // RING)
                    second_product(tile - 1, (r - 1) % RING)
            last_turn = NTILES // RING - 1
            for r in range(RING):
                tile = last_turn * RING + r
                first_product(tile, r)
                if r < RING - 1:
                    tile_transpose(tile + 1, r + 1, last_turn)
                second_product(tile - 1, (r - 1) % RING)
            second_product(NTILES - 1, RING - 1)


PER_BATCH = 44

_INS = ['x', 'ctx_1024', 'mask_BxS2_bf0', 'g_xattn', 'g_ffn', 'L0_xattn_Wq', 'L0_xattn_bq', 'L0_xattn_Wk', 'L0_xattn_bk',
        'L0_xattn_Wv', 'L0_xattn_bv', 'L0_xattn_Wo', 'L0_xattn_bo', 'L0_ffn_W1', 'L0_ffn_b1', 'L0_ffn_W2', 'L0_ffn_b2',
        'L0_ffn_Wr', 'L0_ffn_br']


def kernel(**inputs):
    import numpy as np
    import concourse.bacc as bacc
    from concourse.bass_utils import run_bass_kernel_spmd

    nc = bacc.Bacc("TRN2", target_bir_lowering=False, num_devices=1)
    arrays, args = {}, []
    for name in _INS:
        a = np.ascontiguousarray(inputs[name])
        arrays[f"in_{name}"] = a
        args.append(nc.dram_tensor(f"in_{name}", a.shape, mybir.dt.from_np(a.dtype), kind="ExternalInput").ap())
    result = nc.dram_tensor("out_0", (B, S, D), fp32, kind="ExternalOutput").ap()
    flamingo_layer(nc, *args, result)
    r = run_bass_kernel_spmd(nc, [arrays], core_ids=[0])
    return r.results[0]["out_0"]
```

```python
import concourse.bass as bass
from concourse import mybir
from contextlib import ExitStack

fp32 = mybir.dt.float32
bf16 = mybir.dt.bfloat16
i32 = mybir.dt.int32
u32 = mybir.dt.uint32
u8 = mybir.dt.uint8
ALU = mybir.AluOpType
ACT = mybir.ActivationFunctionType
AX = mybir.AxisListType

P = 128
B, S, D = 8, 256, 128
SK = 1601
H, DK = 16, 64
E, F = 8, 512
QT = S // P
NT = B * QT
PAIRS = H // 2
FC = F // P
W3 = 3 * P
AHEAD = 3
SLOTS = 8
TSLOTS = 4
SCALE = DK ** -0.5
MASKED = -1e30 / SCALE
FLOOR = 5e29
EPS = 1e-5
RS_MAGIC = float(0x5F3759DF)
TAIL = SK - (SK // P) * P
FULL = SK // P
CAP = B * S + 3 * P
PADS = QT + 1
PADROW = E * CAP
ROW = 2 * D + 1
MT = (B * S + E * (P - 1)) // P
RING = 8
NTILES = (MT + RING - 1) // RING * RING
TURNS = MT // RING
POOL_SUMS = 6
NOBODY = 1 << 20


class Count:

    def __init__(self, engine, sem):
        self.engine, self.sem, self.base, self.n = engine, sem, 0, 0

    def up(self, instruction):
        instruction.then_inc(self.sem, 1)
        self.n += 1

    def wait(self):
        self.engine.wait_ge(self.sem, self.base + self.n)

    def enter(self, turn, each):
        self.fixed, self.base, self.n, self.each = self.base + self.n, self.base + self.n + turn * each, 0, each

    def leave(self, turns):
        assert self.n == self.each, (self.n, self.each)
        self.base, self.n = self.fixed + turns * self.each, 0


def settle(engine):
    engine.nop(nofuse=True)


def wait(engine, sem, value):
    if not isinstance(value, int) or value > 0:
        engine.wait_ge(sem, value)


def flamingo_layer(nc, x, ctx_in, mask, g_attn, g_ffn, wq, bq, wk, bk, wv, bv, wo, bo, w1, b1, w2, b2, wr, br, out):
    ctx = ExitStack()
    with ctx:
        def sb(name, shape, dt=fp32):
            return ctx.enter_context(nc.sbuf_tensor(name, shape, dt))

        def pb(name):
            return ctx.enter_context(nc.psum_tensor(name, [P, 512], fp32))

        def sem(name):
            return ctx.enter_context(nc.semaphore(name))

        sorted_rows = nc.dram_tensor("sorted_rows", (PADROW + P, ROW), fp32, kind="Internal").ap()

        x_nat = sb("x_nat", [P, NT, D])
        ctx_nat = sb("ctx_nat", [P, NT, D])
        x_norm = sb("x_norm", [P, QT, D])
        ctx_now = sb("ctx_now", [P, QT, D])
        in_T = sb("in_T", [P, 2 * S])
        xT, cT = in_T[:, 0:S], in_T[:, S:2 * S]
        q_pad = sb("q_pad", [P, H, S])
        k_T = sb("k_T", [P, PAIRS, S])
        v_nat = sb("v_nat", [P, QT, H * DK])
        o_T = sb("o_T", [P, PAIRS, S])
        masked = sb("masked", [P, 2, W3])
        prob = sb("prob", [P, SLOTS, W3])
        prob_T = sb("prob_T", [P, TSLOTS, W3])
        neg_max = sb("neg_max", [P, SLOTS, QT])
        row_sum = sb("row_sum", [P, SLOTS, QT])
        row_fix = sb("row_fix", [P, SLOTS, QT])
        row_inv = sb("row_inv", [P, SLOTS, QT])
        causal = sb("causal", [P, W3])
        mask_now = sb("mask_now", [P, W3])
        mask_all = sb("mask_all", [P, B, S], u8)
        mask_rows = sb("mask_rows", [B, S], u8)
        mask_f = sb("mask_f", [B, S])
        blind = sb("blind", [B, S])
        mean_rows = sb("mean_rows", [B, B, D])
        mean_y = sb("mean_y", [B, D])
        wq_s = sb("wq_s", [P, H * DK])
        wk_s = sb("wk_s", [P, H * DK])
        wv_s = sb("wv_s", [P, H * DK])
        wo_s = sb("wo_s", [P, PAIRS, D])
        B1_AT, W2_AT = F, F + FC
        SEL_AT = W2_AT + FC * D
        PACK = SEL_AT + P
        packs = sb("packs", [P, E, PACK])
        w1_s = packs[:, :, 0:F]
        w2_s = packs[:, :, W2_AT:SEL_AT].rearrange("p e (c d) -> p e c d", c=FC)
        wr_s = sb("wr_s", [P, E])
        NB = 3 * PAIRS + E * FC
        bias_rows = sb("bias_rows", [NB, P])
        bias_T = sb("bias_T", [P, NB])
        relu_b1 = sb("relu_b1", [P, E, FC])
        relu_col = sb("relu_col", [P, E, FC, E])
        others_p = sb("others_p", [P, E])
        ones_f = sb("ones_f", [P, E])
        eye = sb("eye", [P, E, E])
        br_all = sb("br_all", [P, E])
        bo_all = sb("bo_all", [P, D])
        tg_bo = sb("tg_bo", [P, D])
        gates = sb("gates", [P, 2])
        tg = sb("tg", [P, 2])
        ident = sb("ident", [P, P])
        before = sb("before", [P, P], bf16)
        ones_b = sb("ones_b", [P, P], bf16)
        ones_r = sb("ones_r", [1, P])
        mean_w = sb("mean_w", [P, 1])
        CTXR = 4
        ctx_ring = sb("ctx_ring", [P, CTXR, FULL, D])
        tail_ring = sb("tail_ring", [P, CTXR, D])
        ctx_mean = sb("ctx_mean", [P, B])
        u_T = sb("u_T", [P, PAIRS, B])
        stats = sb("stats", [P, NT, 6])
        mv = sb("mv", [P, NT, 2])
        rs_a = sb("rs_a", [P, NT])
        rs_y = sb("rs_y", [P, NT])
        rs_t = sb("rs_t", [P, NT])
        rstd = sb("rstd", [P, NT])
        nmr = sb("nmr", [P, NT])
        stats2 = sb("stats2", [P, QT, 6])
        mv2 = sb("mv2", [P, QT, 2])
        rstd2 = sb("rstd2", [P, QT])
        nmr2 = sb("nmr2", [P, QT])
        residual = sb("residual", [P, QT, D])
        rows = sb("rows", [P, QT, ROW])
        token_ids = sb("token_ids", [P, NT], i32)
        x2_T = sb("x2_T", [P, S])
        logits = sb("logits", [P, QT, E])
        best = sb("best", [P, QT])
        hit = sb("hit", [P, QT, E])
        pick = sb("pick", [P, QT])
        choice = sb("choice", [P, QT, E])
        choice_b = sb("choice_b", [P, QT, E], bf16)
        rank = sb("rank", [P, QT, E])
        slot_f = sb("slot_f", [P, QT])
        slot_i = sb("slot_i", [P, QT], i32)
        iota_i = sb("iota_i", [P, 64], i32)
        e_less = sb("e_less", [P, E])
        next_row = sb("next_row", [P, E])
        region = sb("region", [P, E])
        pad_rows = sb("pad_rows", [P, PADS, ROW])
        steps_f = sb("steps_f", [1, B * QT])
        tile_f = sb("tile_f", [1, NTILES])
        count_1 = sb("count_1", [1, E])
        full_c = sb("full_c", [1, E, B * QT])
        tiles_e = sb("tiles_e", [1, E])
        tiles_to = sb("tiles_to", [1, E])
        jump = sb("jump", [1, E])
        passed = sb("passed", [1, NTILES, E])
        jumped = sb("jumped", [1, NTILES, E])
        tab_f = sb("tab_f", [1, 2, NTILES])
        tile_expert = sb("tile_expert", [1, NTILES], i32)
        tile_row = sb("tile_row", [1, NTILES], i32)
        pad_at = sb("pad_at", [1, E], i32)
        b2_s = sb("b2_s", [E, D])
        empty = sb("empty", [E, D])
        rest = sb("rest", [E, D])
        room = ctx_ring[:, :, :, :].rearrange("p r j d -> p (r j d)")
        tile_in = room[:, 0:RING * ROW].rearrange("p (r n) -> p r n", r=RING)
        tile_out = room[:, RING * ROW:RING * (ROW + D)].rearrange("p (r n) -> p r n", r=RING)
        tile_T = sb("tile_T", [P, 2, P])
        w1_now = sb("w1_now", [P, 2, W2_AT])
        W2R = 4
        w2_now = q_pad[:, :, :].rearrange("p h s -> p (h s)")[:, 0:W2R * (PACK - W2_AT)].rearrange(
            "p (r n) -> p r n", r=W2R)
        hidden = sb("hidden", [P, 2, F])

        ps_s = [pb("ps_s0"), pb("ps_s1")]
        ps_t = [pb("ps_t0"), pb("ps_t1")]
        ps_o = pb("ps_o")
        ps_qk = pb("ps_qk")
        ps_v = pb("ps_v")
        ps_w = pb("ps_w")
        ps_lg = ps_w[:, 0:QT * E].rearrange("p (t e) -> p t e", e=E)
        ps_rk = ps_w[:, 0:QT * E].rearrange("p (t e) -> p t e", e=E)
        ps_ct = ps_w[:, QT * E:QT * E + E]
        ps_mean = ps_w[:, 0:B]
        ps_u = ps_w[:, 0:PAIRS * B]
        ps_y = ps_w[0:B, S:S + D]
        qk_banks, v_banks = [ps_t[0], ps_qk], [ps_t[1], ps_v]
        ps_x = ps_s
        ps_h = ps_t
        ps_out = [ps_o, ps_w]
        ps_c = ps_v[0:E, 0:D]
        ps_rest = ps_qk[0:E, 0:D]

        ld_x = [sem(f"ld_x{b}") for b in range(2)]
        ld_c = [sem(f"ld_c{b}") for b in range(2)]
        ld_wq, ld_wk, ld_wv, ld_wo = sem("ld_wq"), sem("ld_wk"), sem("ld_wv"), sem("ld_wo")
        ld_bias, ld_small, ld_mask, ld_ffn = sem("ld_bias"), sem("ld_small"), sem("ld_mask"), sem("ld_ffn")
        packs_zero, sel_ready = sem("packs_zero"), sem("sel_ready")
        ld_ring = [sem(f"ld_ring{r}") for r in range(CTXR)]
        ident_ready, const_ready = sem("ident_ready"), sem("const_ready")
        even_zero, odd_zero, tails_zero = sem("even_zero"), sem("odd_zero"), sem("tails_zero")
        pool_chain, dve_chain = sem("pool_chain"), sem("dve_chain")
        biasT_done, biasT_ready = sem("biasT_done"), sem("biasT_ready")
        tg_ready, tgbo_ready = sem("tg_ready"), sem("tgbo_ready")
        xnorm_ready, ctxnow_ready = sem("xnorm_ready"), sem("ctxnow_ready")
        inT_done, inT_ready = sem("inT_done"), sem("inT_ready")
        qk_done, v_done = sem("qk_done"), sem("v_done")
        qk_kept, qodd_kept, v_kept = sem("qk_kept"), sem("qodd_kept"), sem("v_kept")
        scores_done, max_ready, exp_done = sem("scores_done"), sem("max_ready"), sem("exp_done")
        inv_ready, prob_ready = sem("inv_ready"), sem("prob_ready")
        probT_done, probT_kept = sem("probT_done"), sem("probT_kept")
        pv_done, oT_kept = sem("pv_done"), sem("oT_kept")
        wo_done, x2_ready = sem("wo_done"), sem("x2_ready")
        residual_ready = sem("residual_ready")
        rows_ready, x2T_done, x2T_kept = sem("rows_ready"), sem("x2T_done"), sem("x2T_kept")
        logits_done, choice_ready, rank_done, slots_ready = (sem("logits_done"), sem("choice_ready"),
                                                             sem("rank_done"), sem("slots_ready"))
        scattered = sem("scattered")
        csum_ready, late_csum_ready, mean_done, mean_kept = (sem("csum_ready"), sem("late_csum_ready"), sem("mean_done"),
                                                               sem("mean_kept"))
        u_done, u_kept, y_done, y_kept = sem("u_done"), sem("u_kept"), sem("y_done"), sem("y_kept")
        b1_ready, col_ready = sem("b1_ready"), sem("col_ready")
        empty_done, empty_kept, rest_done, rest_ready = (sem("empty_done"), sem("empty_kept"), sem("rest_done"),
                                                         sem("rest_ready"))
        pad_ready = sem("pad_ready")
        table_ready, padded = sem("table_ready"), sem("padded")
        tile_loaded = [sem(f"tile_loaded{r}") for r in range(RING)]
        tileT_done, tileT_kept = sem("tileT_done"), sem("tileT_kept")
        w1_ready, w2_ready, h_done, h_kept = sem("w1_ready"), sem("w2_ready"), sem("h_done"), sem("h_kept")
        y2_done, out_ready = sem("y2_done"), sem("out_ready")
        out_stored = [sem(f"out_stored{r}") for r in range(RING)]

        block = ctx.enter_context(nc.Block())

        @block.sync
        def _(sp):
            x_v = x.rearrange("b (t p) d -> p b t d", p=P)
            c_v = ctx_in[:, 0:S, :].rearrange("b (t p) d -> p b t d", p=P)
            x_d = x_nat[:, :, :].rearrange("p (b t) d -> p b t d", t=QT)
            c_d = ctx_nat[:, :, :].rearrange("p (b t) d -> p b t d", t=QT)
            sp.dma_start(x_d[:, 0], x_v[:, 0]).then_inc(ld_x[0], 16)
            sp.dma_start(c_d[:, 0], c_v[:, 0]).then_inc(ld_c[0], 16)
            sp.dma_start(wq_s[:, :], wq).then_inc(ld_wq, 16)
            sp.dma_start(wk_s[:, :], wk).then_inc(ld_wk, 16)
            for i, (b_, n) in enumerate(((bq, PAIRS), (bk, PAIRS), (bv, PAIRS))):
                sp.dma_start(bias_rows[i * PAIRS:i * PAIRS + n, :],
                             b_.rearrange("(n p) -> n p", p=P)).then_inc(ld_bias, 16)
            sp.dma_start(bias_rows[3 * PAIRS:NB, :], b1.rearrange("e (c p) -> (e c) p", p=P)).then_inc(ld_bias, 16)
            sp.dma_start(wv_s[:, :], wv).then_inc(ld_wv, 16)
            sp.dma_start(gates[:, 0:1], g_attn.partition_broadcast(P)).then_inc(ld_small, 16)
            sp.dma_start(gates[:, 1:2], g_ffn.partition_broadcast(P)).then_inc(ld_small, 16)
            sp.dma_start(bo_all[:, :], bo.partition_broadcast(P)).then_inc(ld_small, 16)
            sp.dma_start(br_all[:, :], br.partition_broadcast(P)).then_inc(ld_small, 16)
            sp.dma_start(wr_s[:, :], wr).then_inc(ld_small, 16)
            sp.dma_start(x_nat[:, QT:NT, :], x[1:B].rearrange("b (t p) d -> p (b t) d", p=P)).then_inc(ld_x[1], 16)
            for b in range(1, B):
                sp.dma_start(c_d[:, b], c_v[:, b]).then_inc(ld_c[1], 16)
            sp.dma_start(wo_s[:, :, :], wo.rearrange("(c p) d -> p c d", p=P)).then_inc(ld_wo, 16)
            sp.wait_ge(tails_zero, 1)
            for b in range(B):
                r = b % CTXR
                wait(sp, mean_done, b - CTXR + 1)
                sp.dma_start(ctx_ring[:, r], ctx_in[b, 0:FULL * P, :].rearrange("(p j) d -> p j d", p=P)
                             ).then_inc(ld_ring[r], 16)
                sp.dma_start(tail_ring[0:TAIL, r], ctx_in[b, FULL * P:SK, :]).then_inc(ld_ring[r], 16)
            sp.dma_start(w1_s, w1.rearrange("e d f -> d e f")).then_inc(ld_ffn, 16)
            for e in range(E):
                sp.dma_start(w2_s[:, e], w2[e].rearrange("(c p) d -> p c d", p=P)).then_inc(ld_ffn, 16)
            sp.dma_start(b2_s[:, :], b2).then_inc(ld_ffn, 16)

            sp.wait_ge(const_ready, CONSTS)
            sp.dma_start(sorted_rows[PADROW:PADROW + P, :], pad_rows[:, 0, :]).then_inc(padded, 16)
            sp.wait_ge(pad_ready, 1)
            for e in range(E):
                at = sp.value_load(pad_at[0:1, e:e + 1], min_val=0, max_val=PADROW - PADS * P)
                sp.dma_start(sorted_rows[bass.ds(at, PADS * P), :].rearrange("(t p) n -> p t n", p=P),
                             pad_rows[:, :, :]).then_inc(padded, 16)
            sp.wait_ge(table_ready, 1)
            for k in range(RING):
                at = sp.value_load(tile_row[0:1, k:k + 1], min_val=0, max_val=PADROW)
                if k == 0:
                    sp.wait_ge(scattered, 16 * NT)
                sp.dma_start(tile_in[:, k], sorted_rows[bass.ds(at, P), :]).then_inc(tile_loaded[k], 16)
            def load_again(i, r):
                at = sp.value_load(tile_row[0:1, bass.ds(i * RING + r, 1)], min_val=0, max_val=PADROW)
                sp.wait_ge(out_stored[r], i * 16)
                sp.dma_start(tile_in[:, r], sorted_rows[bass.ds(at, P), :]).then_inc(tile_loaded[r], 16)

            with sp.Fori(1, TURNS) as i:
                for r in range(RING):
                    load_again(i, r)
            for r in range(MT - TURNS * RING):
                load_again(TURNS, r)

        @block.gpsimd
        def _(pool):
            g = nc.gpsimd
            n = Count(pool, pool_chain)
            n.up(g.memset(ident[:, :], 0.0))
            n.wait()
            g.affine_select(out=ident[:, :], in_=ident[:, :], compare_op=ALU.not_equal, fill=1.0, base=0,
                            pattern=[[-1, P]], channel_multiplier=1).then_inc(ident_ready, 1)
            q_v = q_pad[:, :, :].rearrange("p (n two) s -> p n two s", two=2)
            pool.wait_ge(ident_ready, 1)
            g.memset(q_v[DK:P, :, 0, :], 0.0).then_inc(even_zero, 1)
            pool.wait_ge(even_zero, 1)
            n.up(g.memset(causal[:, :], 0.0))
            n.up(g.memset(ones_b[:, :], 1.0))
            n.up(g.memset(ones_f[:, :], 1.0))
            n.up(g.memset(eye[:, :, :], 0.0))
            n.up(g.memset(packs[:, :, SEL_AT:PACK], 0.0))
            n.wait()
            for c0 in (0, 2 * P):
                g.affine_select(out=causal[:, c0:c0 + P], in_=causal[:, c0:c0 + P], compare_op=ALU.is_ge,
                                fill=MASKED, base=0, pattern=[[-1, P]], channel_multiplier=1
                                ).then_inc(const_ready, 1)
            g.affine_select(out=before[:, :], in_=ones_b[:, :], compare_op=ALU.is_gt, fill=0.0, base=0,
                            pattern=[[1, P]], channel_multiplier=-1).then_inc(const_ready, 1)
            g.memset(mean_w[:, :], 1.0 / SK).then_inc(const_ready, 1)
            g.memset(ones_r[:, :], 1.0).then_inc(const_ready, 1)
            g.memset(relu_b1[:, :, :], 0.0).then_inc(const_ready, 1)
            n.up(g.iota(iota_i[:, :], pattern=[[1, 64]], base=0, channel_multiplier=0))
            g.iota(token_ids[:, :], pattern=[[P, NT]], base=0, channel_multiplier=1).then_inc(const_ready, 1)
            n.up(g.memset(pad_rows[:, :, :], 0.0))
            n.wait()
            g.memset(pad_rows[:, :, 2 * D:ROW].bitcast(i32), NOBODY).then_inc(const_ready, 1)
            g.tensor_scalar(e_less[:, :], iota_i[:, 0:E], -1000.0, None, ALU.add).then_inc(const_ready, 1)
            g.tensor_scalar(region[:, :], iota_i[:, 0:E], float(CAP), None, ALU.mult).then_inc(const_ready, 1)
            g.tensor_scalar(next_row[:, :], iota_i[:, 0:E], float(CAP), None, ALU.mult).then_inc(const_ready, 1)
            g.tensor_scalar(tile_f[:, :], iota_i[0:1, 0:NTILES], 1.0, None, ALU.mult).then_inc(const_ready, 1)
            g.tensor_scalar(steps_f[:, :], iota_i[0:1, 0:B * QT], float(P), None, ALU.mult
                            ).then_inc(const_ready, 1)
            g.affine_select(out=eye[:, :, :], in_=eye[:, :, :], compare_op=ALU.not_equal, fill=1.0, base=0,
                            pattern=[[1, E], [-1, E]], channel_multiplier=0).then_inc(const_ready, 1)
            g.affine_select(out=packs[:, :, SEL_AT:PACK], in_=packs[:, :, SEL_AT:PACK], compare_op=ALU.not_equal,
                            fill=1.0, base=0, pattern=[[-1, E], [0, P]], channel_multiplier=1
                            ).then_inc(const_ready, 1)
            g.affine_select(out=others_p[:, :], in_=ones_f[:, 0:E], compare_op=ALU.not_equal, fill=0.0, base=0,
                            pattern=[[-1, E]], channel_multiplier=1).then_inc(const_ready, 1)
            g.memset(tail_ring[:, :, :], 0.0).then_inc(tails_zero, 1)

            def normalise(p, h, slot):
                if h == 0:
                    pool.wait_ge(inv_ready, p + 1)
                g.tensor_tensor(prob[:, slot, 0:P], prob[:, slot, 0:P],
                                row_inv[:, slot, 0:1].to_broadcast([P, P]), ALU.mult).then_inc(prob_ready, 1)
                g.tensor_tensor(prob[:, slot, P:W3], prob[:, slot, P:W3],
                                row_inv[:, slot, 1:2].to_broadcast([P, S]), ALU.mult).then_inc(prob_ready, 1)

            def sum_context(b):
                r = b % CTXR
                pool.wait_ge(ld_ring[r], 32 * (b // CTXR + 1))
                n.up(g.tensor_tensor(ctx_ring[:, r, 0:6, :], ctx_ring[:, r, 0:6, :], ctx_ring[:, r, 6:12, :], ALU.add))
                n.wait()
                g.tensor_tensor(ctx_ring[:, r, 0:3, :], ctx_ring[:, r, 0:3, :], ctx_ring[:, r, 3:6, :], ALU.add
                                ).then_inc(csum_ready, 1)

            def residual_of(b):
                wait(pool, x2_ready, 2 * b)
                pool.wait_ge(ld_x[1], 16)
                g.tensor_tensor(residual[:, :, :], x_nat[:, bass.ds(b * QT, QT), :],
                                tg_bo[:, None, :].to_broadcast([P, QT, D]), ALU.add).then_inc(residual_ready, 1)

            def scatter(b):
                pool.wait_ge(slots_ready, b + 1)
                settle(pool)
                for t in range(QT):
                    g.indirect_dma_start(out=sorted_rows[:, :],
                                         out_offset=bass.IndirectOffsetOnAxis(ap=slot_i[:, t:t + 1], axis=0),
                                         in_=rows[:, t, :], in_offset=None).then_inc(scattered, 16)

            def batch(b, first=False, last=False):
                for j in range(PAIRS):
                    if not (last and j >= PAIRS - AHEAD):
                        for h in range(2):
                            normalise(8 * b + j + AHEAD, h, (2 * (j + AHEAD) + h) % SLOTS)
                    if j == 1:
                        if first:
                            pool.wait_ge(tgbo_ready, 1)
                        residual_of(b)
                    if j == 7 and not first:
                        scatter(b - 1)
                    if first and j + 2 < POOL_SUMS:
                        sum_context(j + 2)

            for j in range(AHEAD):
                for h in range(2):
                    normalise(j, h, 2 * j + h)
            pool.wait_ge(tg_ready, 1)
            g.tensor_scalar(tg_bo[:, :], bo_all[:, :], tg[:, 0:1], None, ALU.mult).then_inc(tgbo_ready, 1)
            sum_context(0)
            sum_context(1)
            batch(0, first=True)
            with pool.Fori(1, B - 1) as b:
                batch(b)
            batch(B - 1, last=True)
            pool.wait_ge(padded, 16 * (E + 1))
            scatter(B - 1)

            def store(i, r):
                pool.wait_ge(out_ready, i * RING + r + 1)
                settle(pool)
                g.indirect_dma_start(
                    out=out_rows, out_offset=bass.IndirectOffsetOnAxis(
                        ap=tile_in[:, r, 2 * D:ROW].bitcast(i32), axis=0),
                    in_=tile_out[:, r, :], in_offset=None, bounds_check=B * S - 1, oob_is_err=False
                ).then_inc(out_stored[r], 16)

            out_rows = out.rearrange("b s d -> (b s) d")
            with pool.Fori(0, TURNS) as i:
                for r in range(RING):
                    store(i, r)
            for r in range(MT - TURNS * RING):
                store(TURNS, r)
            for r in range(RING):
                pool.wait_ge(out_stored[r], 16 * (TURNS + (r < MT - TURNS * RING)))

        @block.scalar
        def _(act):
            s = nc.scalar
            act.dma_start(mask_all[:, :, :], mask[:, 0:S].partition_broadcast(P)).then_inc(ld_mask, 16)
            act.dma_start(mask_rows[:, :], mask[:, 0:S]).then_inc(ld_mask, 16)

            def context_now(b):
                act.wait_ge(ld_c[0], 16)
                if not isinstance(b, int) or b > 0:
                    act.wait_ge(ld_c[1], 16 * (B - 1))
                wait(act, inT_done, b)
                s.activation(ctx_now[:, :, :], ctx_nat[:, bass.ds(b * QT, QT), :], ACT.Copy
                             ).then_inc(ctxnow_ready, 1)

            def keep_inT(b):
                act.wait_ge(inT_done, b + 1)
                s.activation(in_T[:, :], ps_qk[:, :], ACT.Copy).then_inc(inT_ready, 1)

            def keep_qk(p, j, bank=ps_qk):
                act.wait_ge(qk_done, p + 1)
                s.activation(q_pad[0:DK, 2 * j, :], bank[0:DK, 0:S], ACT.Identity,
                             bias=bias_T[0:DK, j:j + 1]).then_inc(qk_kept, 1)
                act.wait_ge(qodd_kept, p + 1)
                s.activation(k_T[:, j, :], bank[:, S:2 * S], ACT.Identity,
                             bias=bias_T[:, PAIRS + j:PAIRS + j + 1]).then_inc(qk_kept, 1)

            def keep_oT(b, p, j):
                act.wait_ge(pv_done, p + 1)
                wait(act, wo_done, b)
                s.activation(o_T[:, j, :], ps_o[:, 0:S], ACT.Identity,
                             bias=bias_T[:, 2 * PAIRS + j:2 * PAIRS + j + 1]).then_inc(oT_kept, 1)

            def keep_v(p, j, bank=ps_v):
                act.wait_ge(v_done, p + 1)
                s.activation(v_nat[:, :, j * P:(j + 1) * P],
                             bank[:, 0:S].rearrange("p (t n) -> p t n", t=QT), ACT.Copy).then_inc(v_kept, 1)

            def exponential(p, h, slot):
                head = 2 * p + h
                act.wait_ge(max_ready, 2 * head + 2)
                wait(act, probT_done, head + 1 - SLOTS)
                for t, (lo, hi) in enumerate(((0, P), (P, W3))):
                    s.activation(prob[:, slot, lo:hi], masked[:, slot % 2, lo:hi], ACT.Exp,
                                 bias=neg_max[:, slot, t:t + 1], scale=-1.0,
                                 accum_out=row_sum[:, slot, t:t + 1]).then_inc(exp_done, 1)

            def keep_x2T(b):
                act.wait_ge(x2T_done, b + 1)
                s.activation(x2_T[:, :], ps_w[:, S:2 * S], ACT.Copy).then_inc(x2T_kept, 1)

            def batch(b, first=False, last=False):
                for j in range(PAIRS):
                    if j == 0 and not last:
                        context_now(b + 1)
                    if j == 4 and not first:
                        keep_x2T(b - 1)
                    if not (last and j >= PAIRS - AHEAD):
                        for h in range(2):
                            exponential(8 * b + j + AHEAD, h, (2 * (j + AHEAD) + h) % SLOTS)
                    if not last:
                        if j > 0:
                            keep_qk(8 * (b + 1) + j - 1, j - 1)
                            keep_v(8 * (b + 1) + j - 1, j - 1)
                    if first and j == 6:
                        act.wait_ge(u_done, 1)
                        s.activation(u_T[:, :, :], ps_u.rearrange("p (n b) -> p n b", b=B), ACT.Copy
                                     ).then_inc(u_kept, 1)
                    keep_oT(b, 8 * b + j, j)
                    if j == 0 and not last:
                        keep_inT(b + 1)
                    if first and j == 5:
                        act.wait_ge(mean_done, B)
                        s.activation(ctx_mean[:, :], ps_mean, ACT.Copy).then_inc(mean_kept, 1)
                if not last:
                    keep_qk(8 * (b + 1) + 7, 7)
                    keep_v(8 * (b + 1) + 7, 7)

            context_now(0)
            act.wait_ge(biasT_done, 1)
            s.activation(bias_T[:, :], ps_w[:, 0:NB], ACT.Copy).then_inc(biasT_ready, 1)
            keep_inT(0)
            act.wait_ge(biasT_ready, 1)
            act.wait_ge(even_zero, 1)
            act.wait_ge(odd_zero, 1)
            for j in range(PAIRS):
                keep_qk(j, j, qk_banks[j % 2])
                keep_v(j, j, v_banks[j % 2])
                if j == 1:
                    act.wait_ge(ld_small, 16 * 5)
                    s.activation(tg[:, :], gates[:, :], ACT.Tanh).then_inc(tg_ready, 1)
                if 2 <= j < 2 + AHEAD:
                    for h in range(2):
                        exponential(j - 2, h, 2 * (j - 2) + h)
            batch(0, first=True)
            with act.Fori(1, B - 1) as b:
                batch(b)
            batch(B - 1, last=True)
            keep_x2T(B - 1)

            def keep_tileT(tile, r):
                act.wait_ge(tileT_done, tile + 1)
                s.activation(tile_T[:, r % 2, :], ps_x[r % 2][:, 0:P], ACT.Copy).then_inc(tileT_kept, 1)

            def keep_hidden(tile, r):
                act.wait_ge(h_done, tile + 1)
                for c in range(FC):
                    s.activation(hidden[:, r % 2, c * P:(c + 1) * P], ps_h[r % 2][:, c * P:(c + 1) * P], ACT.Relu,
                                 bias=w1_now[:, r % 2, B1_AT + c:B1_AT + c + 1]).then_inc(h_kept, 1)

            keep_tileT(0, 0)
            with act.Fori(0, TURNS) as i:
                for r in range(RING):
                    keep_tileT(i * RING + r + 1, r + 1)
                    act.wait_ge(w1_ready, i * RING + r + 1)
                    keep_hidden(i * RING + r, r)
            for tile in range(TURNS * RING, MT):
                if tile < MT - 1:
                    keep_tileT(tile + 1, tile + 1)
                act.wait_ge(w1_ready, tile + 1)
                keep_hidden(tile, tile)

        @block.vector
        def _(dve):
            v = nc.vector
            n = Count(dve, dve_chain)

            def inverse_root_step(step, a, y, t, final):
                n.wait()
                if step == 0:
                    n.up(v.tensor_scalar(y.bitcast(i32), a.bitcast(i32), -0.5, RS_MAGIC, ALU.mult, ALU.add))
                elif step % 3 == 1:
                    n.up(v.tensor_tensor(t, y, y, ALU.mult))
                elif step % 3 == 2:
                    n.up(v.scalar_tensor_tensor(out=t, in0=t, scalar=-0.5, in1=a, op0=ALU.mult, op1=ALU.mult))
                else:
                    n.up(v.scalar_tensor_tensor(out=final if step == 9 else y, in0=t, scalar=1.5, in1=y,
                                                op0=ALU.add, op1=ALU.mult))

            def norm_stats(b):
                for t in range(b * QT, (b + 1) * QT):
                    n.up(v.bn_stats(stats[:, t, :], x_nat[:, t, :]))

            def norm_sums(b):
                n.wait()
                for t in range(b * QT, (b + 1) * QT):
                    n.up(v.bn_aggr(mv[:, t, :], stats[:, t, :]))

            def norm_scales(lo, hi, step):
                if step == 0:
                    n.wait()
                    n.up(v.tensor_scalar(rs_a[:, lo:hi], mv[:, lo:hi, 1], EPS, None, ALU.add))
                elif step < 11:
                    inverse_root_step(step - 1, rs_a[:, lo:hi], rs_y[:, lo:hi], rs_t[:, lo:hi], rstd[:, lo:hi])
                else:
                    n.wait()
                    n.up(v.scalar_tensor_tensor(out=nmr[:, lo:hi], in0=mv[:, lo:hi, 0], scalar=-1.0,
                                                in1=rstd[:, lo:hi], op0=ALU.mult, op1=ALU.mult))

            def normalise_x(b):
                wait(dve, inT_done, b)
                for t in range(QT):
                    i = b * QT + t
                    v.tensor_scalar(x_norm[:, t, :], x_nat[:, bass.ds(i, 1), :], rstd[:, bass.ds(i, 1)],
                                    nmr[:, bass.ds(i, 1)], ALU.mult, ALU.add).then_inc(xnorm_ready, 1)

            def mask_of(b):
                for lo, hi, keys in ((0, P, P), (P, W3, S)):
                    n.up(v.scalar_tensor_tensor(out=mask_now[:, lo:hi], in0=mask_all[:, bass.ds(b, 1), 0:keys],
                                                scalar=MASKED, in1=causal[:, lo:hi], op0=ALU.mult, op1=ALU.add))
                n.wait()

            def maximum(p, h, slot):
                head = 2 * p + h
                dve.wait_ge(scores_done, head + 1)
                wait(dve, exp_done, 2 * (head - 1))
                settle(dve)
                for t, (lo, hi) in enumerate(((0, P), (P, W3))):
                    v.tensor_tensor_reduce(out=masked[:, slot % 2, lo:hi], in0=ps_s[slot % 2][:, lo:hi],
                                           in1=mask_now[:, lo:hi], scale=-SCALE, scalar=FLOOR, op0=ALU.add,
                                           op1=ALU.min, accum_out=neg_max[:, slot, t:t + 1]).then_inc(max_ready, 1)

            def fix_sums(p, slot):
                dve.wait_ge(exp_done, 4 * p + 4)
                n.up(v.tensor_scalar(row_fix[:, slot:slot + 2, :], row_sum[:, slot:slot + 2, :], 1e-30, None,
                                     ALU.max))

            def invert_sums(p, slot):
                wait(dve, prob_ready, 4 * (p + 1) - 2 * SLOTS)
                n.wait()
                v.reciprocal(row_inv[:, slot:slot + 2, :], row_fix[:, slot:slot + 2, :]).then_inc(inv_ready, 1)

            def keep_probT(p, h, slot):
                head = 2 * p + h
                dve.wait_ge(probT_done, head + 1)
                wait(dve, pv_done, p - 1)
                v.tensor_copy(prob_T[:, slot % TSLOTS, :], ps_t[slot % 2][:, 0:W3]).then_inc(probT_kept, 1)

            def keep_qodd(p, j, bank=ps_qk):
                dve.wait_ge(qk_done, p + 1)
                v.tensor_scalar(q_pad[DK:P, 2 * j + 1, :], bank[DK:P, 0:S], bias_T[DK:P, j:j + 1], None, ALU.add
                                ).then_inc(qodd_kept, 1)

            def second_norm(b, step, bank=ps_w):
                a, y, t_ = rs_a[:, 0:QT], rs_y[:, 0:QT], rs_t[:, 0:QT]
                if step == 0:
                    dve.wait_ge(wo_done, b + 1)
                    dve.wait_ge(residual_ready, b + 1)
                    wait(dve, scattered, 16 * QT * b)
                    for t in range(QT):
                        v.scalar_tensor_tensor(out=rows[:, t, 0:D], in0=bank[:, t * D:(t + 1) * D],
                                               scalar=tg[:, 0:1], in1=residual[:, t, :], op0=ALU.mult, op1=ALU.add
                                               ).then_inc(x2_ready, 1)
                    n.up(v.tensor_copy(rows[:, :, 2 * D].bitcast(i32), token_ids[:, bass.ds(b * QT, QT)]))
                elif step == 1:
                    dve.wait_ge(x2_ready, 2 * (b + 1))
                    for t in range(QT):
                        n.up(v.bn_stats(stats2[:, t, :], rows[:, t, 0:D]))
                elif step == 2:
                    n.wait()
                    settle(dve)
                    for t in range(QT):
                        n.up(v.bn_aggr(mv2[:, t, :], stats2[:, t, :]))
                elif step == 3:
                    n.wait()
                    n.up(v.tensor_scalar(a, mv2[:, :, 1], EPS, None, ALU.add))
                elif step < 14:
                    inverse_root_step(step - 4, a, y, t_, rstd2[:, :])
                elif step == 14:
                    n.wait()
                    n.up(v.scalar_tensor_tensor(out=nmr2[:, :], in0=mv2[:, :, 0], scalar=-1.0, in1=rstd2[:, :],
                                                op0=ALU.mult, op1=ALU.mult))
                elif step == 15:
                    n.wait()
                    for t in range(QT):
                        v.tensor_scalar(rows[:, t, D:2 * D], rows[:, t, 0:D], rstd2[:, t:t + 1], nmr2[:, t:t + 1],
                                        ALU.mult, ALU.add).then_inc(rows_ready, 1)

            def choose(b, step):
                number = e_less[:, None, :].to_broadcast([P, QT, E])
                if step == 0:
                    dve.wait_ge(logits_done, b + 1)
                    n.up(v.tensor_tensor(logits[:, :, :], ps_lg, br_all[:, None, :].to_broadcast([P, QT, E]), ALU.add))
                elif step == 1:
                    n.wait()
                    n.up(v.reduce_max(best[:, :], logits[:, :, :], AX.X))
                elif step == 2:
                    n.wait()
                    n.up(v.tensor_tensor(hit[:, :, :], logits[:, :, :], best[:, :, None].to_broadcast([P, QT, E]),
                                         ALU.is_equal))
                elif step == 3:
                    n.wait()
                    n.up(v.tensor_tensor(hit[:, :, :], hit[:, :, :], number, ALU.mult))
                elif step == 4:
                    n.wait()
                    n.up(v.tensor_reduce(pick[:, :], hit[:, :, :], AX.X, ALU.min))
                elif step == 5:
                    n.wait()
                    mine = pick[:, :, None].to_broadcast([P, QT, E])
                    v.tensor_tensor(choice_b[:, :, :], number, mine, ALU.is_equal).then_inc(choice_ready, 1)
                    n.up(v.tensor_tensor(choice[:, :, :], number, mine, ALU.is_equal))

            def place(b, step):
                if step == 0:
                    dve.wait_ge(rank_done, b + 1)
                    n.wait()
                    n.up(v.tensor_tensor(rank[:, :, :], ps_rk, next_row[:, None, :].to_broadcast([P, QT, E]), ALU.add))
                elif step == 1:
                    n.wait()
                    n.up(v.tensor_tensor(rank[:, :, :], rank[:, :, :], choice[:, :, :], ALU.mult))
                    n.up(v.tensor_tensor(next_row[:, :], next_row[:, :], ps_ct, ALU.add))
                elif step == 2:
                    n.wait()
                    n.up(v.reduce_sum(slot_f[:, :], rank[:, :, :], AX.X))
                elif step == 3:
                    n.wait()
                    v.tensor_copy(slot_i[:, :], slot_f[:, :]).then_inc(slots_ready, 1)

            def sum_context(b, step):
                r = b % CTXR
                if step == 0:
                    dve.wait_ge(ld_ring[r], 32 * (b // CTXR + 1))
                    n.up(v.tensor_tensor(ctx_ring[:, r, 0:6, :], ctx_ring[:, r, 0:6, :], ctx_ring[:, r, 6:12, :],
                                         ALU.add))
                else:
                    n.wait()
                    v.tensor_tensor(ctx_ring[:, r, 0:3, :], ctx_ring[:, r, 0:3, :], ctx_ring[:, r, 3:6, :], ALU.add
                                    ).then_inc(late_csum_ready, 1)

            def bias_columns(step):
                b1_T = bias_T[:, 3 * PAIRS:NB].rearrange("p (e c) -> p e c", e=E)
                if step == 0:
                    n.up(v.tensor_scalar(relu_b1[:, :, :], b1_T, 0.0, None, ALU.max))
                    v.tensor_copy(packs[:, :, B1_AT:W2_AT], b1_T).then_inc(b1_ready, 1)
                else:
                    n.wait()
                    v.tensor_tensor(relu_col[:, :, :, :], relu_b1[:, :, :, None].to_broadcast([P, E, FC, E]),
                                    eye[:, :, None, :].to_broadcast([P, E, FC, E]), ALU.mult).then_inc(col_ready, 1)

            def between(b, j, at, first):
                here = 6 * j + at
                if first:
                    if 2 <= here < 14:
                        norm_scales(2 * QT, NT, here - 2)
                    if 18 <= here < 20:
                        bias_columns(here - 18)
                    if 26 <= here < 26 + 2 * (B - POOL_SUMS):
                        sum_context(POOL_SUMS + (here - 26) // 2, here % 2)
                    return
                if 4 <= here < 20:
                    second_norm(b - 1, here - 4)
                if 30 <= here < 36:
                    choose(b - 1, here - 30)
                if 38 <= here < 42:
                    place(b - 1, here - 38)

            def batch(b, first=False, last=False):
                for j in range(PAIRS):
                    p = 8 * b + j
                    ahead = not (last and j >= PAIRS - AHEAD)
                    if j == 0 and not last:
                        normalise_x(b + 1)
                    for h in range(2):
                        if ahead:
                            maximum(p + AHEAD, h, (2 * (j + AHEAD) + h) % SLOTS)
                        between(b, j, 2 * h, first)
                        if not (last and j == PAIRS - 1):
                            keep_probT(p + 1, h, (2 * j + 2 + h) % SLOTS)
                        between(b, j, 2 * h + 1, first)
                    if not last and j > 0:
                        keep_qodd(8 * (b + 1) + j - 1, j - 1)
                    if ahead:
                        fix_sums(p + AHEAD, 2 * (j + AHEAD) % SLOTS)
                    between(b, j, 4, first)
                    if ahead:
                        invert_sums(p + AHEAD, 2 * (j + AHEAD) % SLOTS)
                    between(b, j, 5, first)
                    if j == PAIRS - AHEAD - 1 and not last:
                        dve.wait_ge(max_ready, 4 * 8 * (b + 1))
                        mask_of(b + 1)
                    if first:
                        if j == 5:
                            n.up(v.tensor_copy(mask_f[:, :], mask_rows[:, :]))
                            n.wait()
                            v.tensor_tensor_scan(blind[:, :], mask_f[:, :], mask_f[:, :], 1.0, ALU.min, ALU.min
                                                 ).then_inc(y_kept, 1)
                        if j == 7:
                            dve.wait_ge(y_done, 1)
                            n.up(v.tensor_copy(mean_y[:, :], ps_y))
                            n.wait()
                            v.tensor_tensor(mean_rows[:, :, :], mean_y[:, None, :].to_broadcast([B, B, D]),
                                            ident[0:B, 0:B, None].to_broadcast([B, B, D]), ALU.mult
                                            ).then_inc(y_kept, 1)
                if not last:
                    keep_qodd(8 * (b + 1) + 7, 7)

            q_v = q_pad[:, :, :].rearrange("p (n two) s -> p n two s", two=2)
            v.memset(q_v[0:DK, :, 1, :], 0.0).then_inc(odd_zero, 1)
            dve.wait_ge(ld_x[0], 16)
            norm_stats(0)
            norm_sums(0)
            for step in range(12):
                norm_scales(0, QT, step)
            n.wait()
            normalise_x(0)
            dve.wait_ge(ld_mask, 16 * 2)
            dve.wait_ge(const_ready, CONSTS)
            mask_of(0)
            dve.wait_ge(biasT_ready, 1)
            for j in range(PAIRS):
                keep_qodd(j, j, qk_banks[j % 2])
                if j > 2:
                    norm_scales(QT, 2 * QT, 2 * j - 6)
                if 2 <= j < 2 + AHEAD:
                    for h in range(2):
                        maximum(j - 2, h, 2 * (j - 2) + h)
                if j > 2:
                    norm_scales(QT, 2 * QT, 2 * j - 5)
                if 3 <= j < 3 + AHEAD:
                    fix_sums(j - 3, 2 * (j - 3))
                    invert_sums(j - 3, 2 * (j - 3))
                if j == 1:
                    dve.wait_ge(ld_x[1], 16)
                    norm_stats(1)
                if j > 1:
                    norm_sums(j - 1)
                    norm_stats(j)
            norm_sums(PAIRS - 1)
            for h in range(2):
                norm_scales(QT, 2 * QT, 10 + h)
                keep_probT(0, h, h)
            n.wait()
            batch(0, first=True)
            dve.wait_ge(ld_small, 16 * 5)
            dve.wait_ge(const_ready, CONSTS)
            with dve.Fori(1, B - 1) as b:
                n.enter(b - 1, PER_BATCH)
                batch(b)
                n.leave(B - 2)
            batch(B - 1, last=True)
            v.tensor_copy(pad_at[:, :], next_row[0:1, :]).then_inc(pad_ready, 1)
            dve.wait_ge(empty_done, 1)
            n.up(v.tensor_copy(empty[:, :], ps_c))
            n.wait()
            v.tensor_tensor(empty[:, :], empty[:, :], b2_s[:, :], ALU.add).then_inc(empty_kept, 1)
            for step in range(16):
                second_norm(B - 1, step, ps_qk)
            dve.wait_ge(rest_done, 1)
            v.tensor_tensor(rest[:, :], ps_rest, b2_s[:, :], ALU.add).then_inc(rest_ready, 1)
            for step in range(6):
                choose(B - 1, step)
            for step in range(4):
                place(B - 1, step)

            n.up(v.tensor_tensor(count_1[:, :], next_row[0:1, :], region[0:1, :], ALU.subtract))
            n.wait()
            n.up(v.tensor_tensor(full_c[:, :, :], count_1[:, :, None].to_broadcast([1, E, B * QT]),
                                 steps_f[:, None, :].to_broadcast([1, E, B * QT]), ALU.is_gt))
            n.wait()
            n.up(v.reduce_sum(tiles_e[:, :], full_c[:, :, :], AX.X))
            n.wait()
            n.up(v.tensor_tensor_scan(tiles_to[:, :], ones_r[0:1, 0:E], tiles_e[:, :], 0.0, ALU.mult, ALU.add))
            n.up(v.tensor_scalar(jump[:, :], tiles_e[:, :], -float(P), float(CAP), ALU.mult, ALU.add))
            n.wait()
            n.up(v.tensor_tensor(passed[:, :, :], tile_f[:, :, None].to_broadcast([1, NTILES, E]),
                                 tiles_to[:, None, :].to_broadcast([1, NTILES, E]), ALU.is_ge))
            n.wait()
            n.up(v.reduce_sum(tab_f[:, 0, :], passed[:, :, :], AX.X))
            n.up(v.tensor_tensor(jumped[:, :, :], passed[:, :, :], jump[:, None, :].to_broadcast([1, NTILES, E]),
                                 ALU.mult))
            n.wait()
            n.up(v.reduce_sum(tab_f[:, 1, :], jumped[:, :, :], AX.X))
            n.up(v.tensor_scalar(tile_expert[:, :], tab_f[:, 0, :], float(E - 1), None, ALU.min))
            n.wait()
            n.up(v.scalar_tensor_tensor(out=tab_f[:, 1, :], in0=tile_f[:, :], scalar=float(P), in1=tab_f[:, 1, :],
                                        op0=ALU.mult, op1=ALU.add))
            n.wait()
            n.up(v.tensor_scalar(tile_row[:, :], tab_f[:, 1, :], float(PADROW), None, ALU.min))
            n.wait()
            v.engine_nop().then_inc(table_ready, 1)

            def weights_of(tile, r, part):
                if part == 0:
                    wait(dve, h_kept, FC * (tile - 1))
                    v.tensor_copy(w1_now[:, r % 2, :], packs[:, bass.ds(expert, 1), 0:W2_AT]).then_inc(w1_ready, 1)
                else:
                    wait(dve, y2_done, tile - W2R + 1)
                    v.tensor_copy(w2_now[:, r % W2R, :], packs[:, bass.ds(expert, 1), W2_AT:PACK]
                                  ).then_inc(w2_ready, 1)

            def finish(tile, r):
                dve.wait_ge(y2_done, tile + 1)
                v.scalar_tensor_tensor(out=tile_out[:, r, :], in0=ps_out[r % 2][:, 0:D], scalar=tg[:, 1:2],
                                       in1=tile_in[:, r, 0:D], op0=ALU.mult, op1=ALU.add).then_inc(out_ready, 1)

            def expert_of(tile):
                return dve.value_load(tile_expert[0:1, bass.ds(tile, 1)], min_val=0, max_val=E - 1)

            dve.wait_ge(ld_ffn, 16 * (E + 2))
            expert = expert_of(0)
            weights_of(0, 0, 0)
            weights_of(0, 0, 1)
            for tile in range(RING):
                expert = expert_of(tile + 1)
                weights_of(tile + 1, tile + 1, 0)
                if tile >= 2:
                    finish(tile - 2, tile - 2)
                weights_of(tile + 1, tile + 1, 1)
            with dve.Fori(1, TURNS) as i:
                for r in range(RING):
                    tile = i * RING + r
                    expert = expert_of(tile + 1)
                    weights_of(tile + 1, r + 1, 0)
                    finish(tile - 2, (r - 2) % RING)
                    weights_of(tile + 1, r + 1, 1)
            for tile in range(TURNS * RING, MT):
                if tile < MT - 1:
                    expert = expert_of(tile + 1)
                    weights_of(tile + 1, tile + 1, 0)
                finish(tile - 2, (tile - 2) % RING)
                if tile < MT - 1:
                    weights_of(tile + 1, tile + 1, 1)
            for tile in range(MT - 2, MT):
                finish(tile, tile % RING)

        @block.tensor
        def _(pe):
            t_ = nc.tensor

            def mm(out_, lhsT, rhs, start=True, stop=True, loose=False):
                return t_.matmul(out_, lhsT, rhs, start=start, stop=stop, skip_group_check=loose)

            def input_transposes(b):
                pe.wait_ge(xnorm_ready, 2 * b + 2)
                pe.wait_ge(ctxnow_ready, b + 1)
                wait(pe, qk_kept, 16 * b)
                wait(pe, qodd_kept, 8 * b)
                for t in range(QT):
                    t_.transpose(ps_qk[:, t * P:(t + 1) * P], x_norm[:, t, :], ident[:, :])
                for t in range(QT):
                    last = t_.transpose(ps_qk[:, S + t * P:S + (t + 1) * P], ctx_now[:, t, :], ident[:, :])
                last.then_inc(inT_done, 1)

            def project_qk(b, j, bank=ps_qk, free=None):
                p = 8 * b + j
                if j == 0:
                    pe.wait_ge(inT_ready, b + 1)
                free = p if free is None else free
                wait(pe, qk_kept, 2 * free)
                wait(pe, qodd_kept, free)
                mm(bank[:, 0:S], wq_s[:, j * P:(j + 1) * P], xT)
                mm(bank[:, S:2 * S], wk_s[:, j * P:(j + 1) * P], cT).then_inc(qk_done, 1)

            def project_v(b, j, bank=ps_v, free=None):
                p = 8 * b + j
                wait(pe, v_kept, p if free is None else free)
                for t in range(QT):
                    last = mm(bank[:, t * P:(t + 1) * P], cT[:, t * P:(t + 1) * P], wv_s[:, j * P:(j + 1) * P])
                last.then_inc(v_done, 1)

            def scores(p, j, h):
                head = 2 * p + h
                pe.wait_ge(qk_kept, 2 * p + 2)
                if h == 1:
                    pe.wait_ge(qodd_kept, p + 1)
                wait(pe, max_ready, 2 * (head - 1))
                mm(ps_s[h][:, 0:P], q_pad[:, 2 * j + h, 0:P], k_T[:, j, 0:P])
                mm(ps_s[h][:, P:W3], q_pad[:, 2 * j + h, P:S], k_T[:, j, :]).then_inc(scores_done, 1)

            def transpose_probs(p, h, slot):
                head = 2 * p + h
                pe.wait_ge(prob_ready, 2 * head + 2)
                wait(pe, probT_kept, head - 1)
                for i in range(3):
                    last = t_.transpose(ps_t[slot % 2][:, i * P:(i + 1) * P], prob[:, slot, i * P:(i + 1) * P],
                                        ident[:, :])
                last.then_inc(probT_done, 1)

            def values(p, j):
                pe.wait_ge(probT_kept, 2 * p + 2)
                pe.wait_ge(v_kept, p + 1)
                wait(pe, oT_kept, p)
                for t in range(QT):
                    for h in range(2):
                        slot = (2 * j + h) % TSLOTS
                        last = mm(ps_o[h * DK:(h + 1) * DK, t * P:S],
                                  v_nat[:, t, (2 * j + h) * DK:(2 * j + h + 1) * DK],
                                  prob_T[:, slot, t * S:t * S + S - t * P], start=t == 0, stop=t == QT - 1)
                last.then_inc(pv_done, 1)

            def output_projection(b):
                wait(pe, slots_ready, b)
                for t in range(QT):
                    for c in range(PAIRS):
                        if t == 0 and c >= PAIRS - 2:
                            pe.wait_ge(oT_kept, 8 * b + c + 1)
                        mm(ps_w[:, t * P:(t + 1) * P], o_T[:, c, t * P:(t + 1) * P], wo_s[:, c, :],
                           start=c == 0, stop=False)
                    last = mm(ps_w[:, t * P:(t + 1) * P], blind[:, t * P:(t + 1) * P],
                              mean_rows[:, bass.ds(b, 1), :], start=False, stop=True)
                last.then_inc(wo_done, 1)

            def norm_transposes(b):
                pe.wait_ge(rows_ready, 2 * b + 2)
                for t in range(QT):
                    last = t_.transpose(ps_w[:, S + t * P:S + (t + 1) * P], rows[:, t, D:2 * D], ident[:, :])
                last.then_inc(x2T_done, 1)

            def router(b):
                pe.wait_ge(x2T_kept, b + 1)
                for t in range(QT):
                    last = mm(ps_lg[:, t, :], x2_T[:, t * P:(t + 1) * P], wr_s[:, :])
                last.then_inc(logits_done, 1)

            def ranks(b):
                pe.wait_ge(choice_ready, b + 1)
                mm(ps_rk[:, 0, :], before[:, :], choice_b[:, 0, :])
                mm(ps_rk[:, 1, :], before[:, :], choice_b[:, 1, :], stop=False)
                mm(ps_rk[:, 1, :], ones_b[:, :], choice_b[:, 0, :], start=False)
                mm(ps_ct, ones_b[:, :], choice_b[:, 0, :], stop=False)
                mm(ps_ct, ones_b[:, :], choice_b[:, 1, :], start=False).then_inc(rank_done, 1)

            def mean_of(b):
                r = b % CTXR
                if b < POOL_SUMS:
                    pe.wait_ge(csum_ready, b + 1)
                else:
                    pe.wait_ge(late_csum_ready, b + 1 - POOL_SUMS)
                for i in range(3):
                    mm(ps_mean[:, b:b + 1], ctx_ring[:, r, i, :], mean_w[:, :], start=i == 0, stop=False)
                mm(ps_mean[:, b:b + 1], tail_ring[:, r, :], mean_w[:, :], start=False).then_inc(mean_done, 1)

            def means_through_wv():
                pe.wait_ge(mean_kept, 1)
                for c in range(PAIRS):
                    last = mm(ps_u[:, c * B:(c + 1) * B], wv_s[:, c * P:(c + 1) * P], ctx_mean[:, :])
                last.then_inc(u_done, 1)

            def means_through_wo():
                pe.wait_ge(u_kept, 1)
                for c in range(PAIRS):
                    last = mm(ps_y, u_T[:, c, :], wo_s[:, c, :], start=c == 0, stop=c == PAIRS - 1)
                last.then_inc(y_done, 1)

            def last_projection(c):
                b = B - 1
                if c == 0:
                    pe.wait_ge(qk_kept, 16 * B)
                    pe.wait_ge(qodd_kept, 8 * B)
                    for t in range(QT):
                        mm(ps_qk[:, t * P:(t + 1) * P], blind[:, t * P:(t + 1) * P], mean_rows[:, b, :], stop=False,
                           loose=True)
                pe.wait_ge(oT_kept, 8 * b + c + 1)
                for t in range(QT):
                    last = mm(ps_qk[:, t * P:(t + 1) * P], o_T[:, c, t * P:(t + 1) * P], wo_s[:, c, :],
                              start=False, stop=c == PAIRS - 1, loose=True)
                if c == PAIRS - 1:
                    last.then_inc(wo_done, 1)

            def empty_product(e):
                if e == 0:
                    pe.wait_ge(b1_ready, 1)
                    pe.wait_ge(col_ready, 1)
                    pe.wait_ge(ld_ffn, 16 * (E + 2))
                    pe.wait_ge(v_kept, 8 * B)
                for c in range(FC):
                    last = mm(ps_c, relu_col[:, e, c, :], w2_s[:, e, c, :], start=e + c == 0,
                              stop=e + c == E + FC - 2)
                if e == E - 1:
                    last.then_inc(empty_done, 1)

            def batch(b, first=False, last=False):
                for j in range(PAIRS):
                    p = 8 * b + j
                    for h in range(2):
                        if not (last and j >= PAIRS - AHEAD):
                            scores(p + AHEAD, (j + AHEAD) % PAIRS, h)
                        if not (last and j == PAIRS - 1):
                            transpose_probs(p + 1, h, (2 * j + 2 + h) % SLOTS)
                    if not last and j > 0:
                        project_qk(b + 1, j - 1)
                        project_v(b + 1, j - 1)
                    if first and j == 0:
                        pe.wait_ge(ld_wo, 16)
                    if first and j < 5:
                        mean_of(j)
                    if first and j == 5:
                        for late in range(5, B):
                            mean_of(late)
                    if first and j == 6:
                        means_through_wv()
                    if first and j == 7:
                        means_through_wo()
                    if j == 6 and not first:
                        ranks(b - 1)
                    if last:
                        empty_product(j)
                    values(p, j)
                    if last and j > 0:
                        last_projection(j - 1)
                    if j == 0 and not last:
                        input_transposes(b + 1)
                    if j == 3 and not first:
                        norm_transposes(b - 1)
                    if j == 4 and not first:
                        router(b - 1)
                if last:
                    last_projection(PAIRS - 1)
                else:
                    if first:
                        pe.wait_ge(y_kept, 2)
                    output_projection(b)
                    project_qk(b + 1, 7)
                    project_v(b + 1, 7)

            pe.wait_ge(ident_ready, 1)
            input_transposes(0)
            pe.wait_ge(ld_bias, 16 * 4)
            t_.transpose(ps_w[:, 0:NB], bias_rows[:, :], ident[0:NB, 0:NB]).then_inc(biasT_done, 1)
            pe.wait_ge(ld_wq, 16)
            pe.wait_ge(ld_wk, 16)
            pe.wait_ge(ld_wv, 16)
            for j in range(PAIRS):
                project_qk(0, j, qk_banks[j % 2], j - 1)
                project_v(0, j, v_banks[j % 2], j - 1)
                if 1 <= j < 1 + AHEAD:
                    for h in range(2):
                        scores(j - 1, j - 1, h)
            pe.wait_ge(const_ready, CONSTS)
            pe.wait_ge(qk_kept, 2 * (PAIRS - 1))
            pe.wait_ge(qodd_kept, PAIRS - 1)
            pe.wait_ge(v_kept, PAIRS - 1)
            for h in range(2):
                transpose_probs(0, h, h)
            batch(0, first=True)
            pe.wait_ge(ld_small, 16 * 5)
            with pe.Fori(1, B - 1) as b:
                batch(b)
            batch(B - 1, last=True)
            pe.wait_ge(empty_kept, 1)
            norm_transposes(B - 1)
            mm(ps_rest, others_p[0:E, :], empty[:, :]).then_inc(rest_done, 1)
            router(B - 1)
            ranks(B - 1)

            def tile_transpose(tile, r, turn):
                pe.wait_ge(tile_loaded[r], 16 * turn + 16)
                wait(pe, tileT_kept, tile - 1)
                t_.transpose(ps_x[r % 2][:, 0:P], tile_in[:, r, D:2 * D], ident[:, :]).then_inc(tileT_done, 1)

            def first_product(tile, r):
                pe.wait_ge(tileT_kept, tile + 1)
                pe.wait_ge(w1_ready, tile + 1)
                wait(pe, h_kept, FC * (tile - 1))
                for c in range(FC):
                    last = mm(ps_h[r % 2][:, c * P:(c + 1) * P], w1_now[:, r % 2, c * P:(c + 1) * P],
                              tile_T[:, r % 2, :])
                last.then_inc(h_done, 1)

            def second_product(tile, r):
                wait(pe, out_ready, tile - 1)
                pe.wait_ge(w2_ready, tile + 1)
                mm(ps_out[r % 2][:, 0:D], w2_now[0:E, r % W2R, SEL_AT - W2_AT:PACK - W2_AT], rest[:, :], stop=False)
                for c in range(FC):
                    pe.wait_ge(h_kept, FC * tile + c + 1)
                    last = mm(ps_out[r % 2][:, 0:D], hidden[:, r % 2, c * P:(c + 1) * P],
                              w2_now[:, r % W2R, c * D:(c + 1) * D], start=False, stop=c == FC - 1)
                last.then_inc(y2_done, 1)

            pe.wait_ge(table_ready, 1)
            pe.wait_ge(rest_ready, 1)
            tile_transpose(0, 0, 0)
            first_product(0, 0)
            tile_transpose(1, 1, 0)
            for r in range(1, RING):
                first_product(r, r)
                tile_transpose(r + 1, (r + 1) % RING, (r + 1) // RING)
                second_product(r - 1, r - 1)
            with pe.Fori(1, TURNS) as i:
                for r in range(RING):
                    tile = i * RING + r
                    first_product(tile, r)
                    tile_transpose(tile + 1, (r + 1) % RING, i + (r + 1) // RING)
                    second_product(tile - 1, (r - 1) % RING)
            for tile in range(TURNS * RING, MT):
                first_product(tile, tile % RING)
                if tile < MT - 1:
                    tile_transpose(tile + 1, (tile + 1) % RING, (tile + 1) // RING)
                second_product(tile - 1, (tile - 1) % RING)
            second_product(MT - 1, (MT - 1) % RING)


CONSTS = 16
PER_BATCH = 37

_INS = ['x', 'ctx_1024', 'mask_BxS2_bf0', 'g_xattn', 'g_ffn', 'L0_xattn_Wq', 'L0_xattn_bq', 'L0_xattn_Wk', 'L0_xattn_bk',
        'L0_xattn_Wv', 'L0_xattn_bv', 'L0_xattn_Wo', 'L0_xattn_bo', 'L0_ffn_W1', 'L0_ffn_b1', 'L0_ffn_W2', 'L0_ffn_b2',
        'L0_ffn_Wr', 'L0_ffn_br']


def kernel(**inputs):
    import numpy as np
    import concourse.bacc as bacc
    from concourse.bass_utils import run_bass_kernel_spmd

    nc = bacc.Bacc("TRN2", target_bir_lowering=False, num_devices=1)
    arrays, args = {}, []
    for name in _INS:
        a = np.ascontiguousarray(inputs[name])
        arrays[f"in_{name}"] = a
        args.append(nc.dram_tensor(f"in_{name}", a.shape, mybir.dt.from_np(a.dtype), kind="ExternalInput").ap())
    result = nc.dram_tensor("out_0", (B, S, D), fp32, kind="ExternalOutput").ap()
    flamingo_layer(nc, *args, result)
    r = run_bass_kernel_spmd(nc, [arrays], core_ids=[0])
    return r.results[0]["out_0"]
```

```python
import concourse.bass as bass
from concourse import mybir
from contextlib import ExitStack

fp32 = mybir.dt.float32
bf16 = mybir.dt.bfloat16
i32 = mybir.dt.int32
u8 = mybir.dt.uint8
ALU = mybir.AluOpType
ACT = mybir.ActivationFunctionType
AX = mybir.AxisListType

P = 128
B, S, D = 8, 256, 128
SK = 1601
H, DK = 16, 64
E, F = 8, 512
QT = S // P
NT = B * QT
PAIRS = H // 2
FC = F // P
W3 = 3 * P
AHEAD = 3
SLOTS = 8
TSLOTS = 4
SCALE = DK ** -0.5
MASKED = -1e30 / SCALE
FLOOR = 5e29
EPS = 1e-5
RS_MAGIC = float(0x5F3759DF)
TAIL = SK - (SK // P) * P
FULL = SK // P
CAP = B * S + (QT + 1) * P
PADS = QT + 1
PADROW = E * CAP
ROW = 2 * D + 1
MT = (B * S + E * (P - 1)) // P
RING = 8
EARLY = ((B - 1) * S - E * (P - 1) + P - 1) // P
TURNS = (MT - EARLY) // RING
NTILES = MT + 1
assert (MT - EARLY) % RING == 0 and NTILES % RING == 0
SP_PADS = 2
POOL_SUMS = (0, 1, 2, 3, 4, 6)
SUM_AT = (0, 10, 16, 22, 28, 29, 32, 33)
NOBODY = 1 << 20


class Count:

    def __init__(self, engine, sem):
        self.engine, self.sem, self.base, self.n = engine, sem, 0, 0

    def up(self, instruction):
        instruction.then_inc(self.sem, 1)
        self.n += 1

    def wait(self):
        self.engine.wait_ge(self.sem, self.base + self.n)

    def enter(self, turn, each):
        self.fixed, self.base, self.n, self.each = self.base + self.n, self.base + self.n + turn * each, 0, each

    def leave(self, turns):
        assert self.n == self.each, (self.n, self.each)
        self.base, self.n = self.fixed + turns * self.each, 0


def settle(engine):
    engine.nop(nofuse=True)


def wait(engine, sem, value):
    if not isinstance(value, int) or value > 0:
        engine.wait_ge(sem, value)


def flamingo_layer(nc, x, ctx_in, mask, g_attn, g_ffn, wq, bq, wk, bk, wv, bv, wo, bo, w1, b1, w2, b2, wr, br, out):
    ctx = ExitStack()
    with ctx:
        def sb(name, shape, dt=fp32):
            return ctx.enter_context(nc.sbuf_tensor(name, shape, dt))

        def pb(name):
            return ctx.enter_context(nc.psum_tensor(name, [P, 512], fp32))

        def sem(name):
            return ctx.enter_context(nc.semaphore(name))

        sorted_rows = nc.dram_tensor("sorted_rows", (PADROW + P, ROW), fp32, kind="Internal").ap()

        x_nat = sb("x_nat", [P, NT, D])
        ctx_nat = sb("ctx_nat", [P, NT, D])
        x_norm = sb("x_norm", [P, QT, D])
        ctx_now = sb("ctx_now", [P, QT, D])
        in_T = sb("in_T", [P, 2 * S])
        xT, cT = in_T[:, 0:S], in_T[:, S:2 * S]
        q_pad = sb("q_pad", [P, H, S])
        k_T = sb("k_T", [P, PAIRS, S])
        v_nat = sb("v_nat", [P, QT, H * DK])
        o_T = sb("o_T", [P, PAIRS, S])
        masked = sb("masked", [P, 2, W3])
        prob = sb("prob", [P, SLOTS, W3])
        prob_T = sb("prob_T", [P, TSLOTS, W3])
        neg_max = sb("neg_max", [P, SLOTS, QT])
        row_sum = sb("row_sum", [P, SLOTS, QT])
        row_fix = sb("row_fix", [P, SLOTS, QT])
        row_inv = sb("row_inv", [P, SLOTS, QT])
        causal = sb("causal", [P, W3])
        mask_now = sb("mask_now", [P, W3])
        mask_all = sb("mask_all", [P, B, S], u8)
        mask_rows = sb("mask_rows", [B, S], u8)
        mask_f = sb("mask_f", [B, S])
        blind = sb("blind", [B, S])
        mean_rows = sb("mean_rows", [B, B, D])
        mean_y = sb("mean_y", [B, D])
        wq_s = sb("wq_s", [P, H * DK])
        wk_s = sb("wk_s", [P, H * DK])
        wv_s = sb("wv_s", [P, H * DK])
        wo_s = sb("wo_s", [P, PAIRS, D])
        B1_AT, W2_AT = F, F + FC
        SEL_AT = W2_AT + FC * D
        PACK = SEL_AT + P
        packs = sb("packs", [P, E, PACK])
        w1_s = packs[:, :, 0:F]
        w2_s = packs[:, :, W2_AT:SEL_AT].rearrange("p e (c d) -> p e c d", c=FC)
        wr_s = sb("wr_s", [P, E])
        NB = 3 * PAIRS + E * FC
        bias_rows = sb("bias_rows", [NB, P])
        bias_T = sb("bias_T", [P, NB])
        relu_b1 = sb("relu_b1", [P, E, FC])
        relu_col = sb("relu_col", [P, E, FC, E])
        others_p = sb("others_p", [P, E])
        ones_f = sb("ones_f", [P, E])
        eye = sb("eye", [P, E, E])
        br_all = sb("br_all", [P, E])
        bo_all = sb("bo_all", [P, D])
        tg_bo = sb("tg_bo", [P, D])
        gates = sb("gates", [P, 2])
        tg = sb("tg", [P, 2])
        ident = sb("ident", [P, P])
        before = sb("before", [P, P], bf16)
        ones_b = sb("ones_b", [P, P], bf16)
        ones_r = sb("ones_r", [1, P])
        mean_w = sb("mean_w", [P, 1])
        CTXR = 4
        ctx_ring = sb("ctx_ring", [P, CTXR, FULL + 1, D])
        tail_ring = ctx_ring[:, :, FULL, :]
        ctx_sum = sb("ctx_sum", [P, B, D])
        ctx_mean = sb("ctx_mean", [P, B])
        u_T = sb("u_T", [P, PAIRS, B])
        stats = sb("stats", [P, NT, 6])
        mv = sb("mv", [P, NT, 2])
        rs_a = sb("rs_a", [P, NT])
        rs_y = sb("rs_y", [P, NT])
        rs_t = sb("rs_t", [P, NT])
        rstd = sb("rstd", [P, NT])
        nmr = sb("nmr", [P, NT])
        stats2 = sb("stats2", [P, QT, 6])
        mv2 = sb("mv2", [P, QT, 2])
        rstd2 = sb("rstd2", [P, QT])
        nmr2 = sb("nmr2", [P, QT])
        residual = sb("residual", [P, QT, D])
        rows = sb("rows", [P, QT, ROW])
        token_ids = sb("token_ids", [P, NT], i32)
        x2_T = sb("x2_T", [P, S])
        logits = sb("logits", [P, QT, E])
        best = sb("best", [P, QT])
        hit = sb("hit", [P, QT, E])
        pick = sb("pick", [P, QT])
        choice = sb("choice", [P, QT, E])
        choice_b = sb("choice_b", [P, QT, E], bf16)
        rank = sb("rank", [P, QT, E])
        slot_f = sb("slot_f", [P, QT])
        slot_i = sb("slot_i", [P, QT], i32)
        iota_i = sb("iota_i", [P, 64], i32)
        e_less = sb("e_less", [P, E])
        next_row = sb("next_row", [P, E])
        region = sb("region", [P, E])
        pad_rows = sb("pad_rows", [P, PADS, ROW])
        steps_f = sb("steps_f", [1, B * QT])
        tile_f = sb("tile_f", [1, NTILES])
        early_e = sb("early_e", [1, E + 1])
        before_e = sb("before_e", [1, E])
        jump_late = sb("jump_late", [1, E])
        start_late = sb("start_late", [1, 1])
        count_1 = sb("count_1", [1, E])
        full_c = sb("full_c", [1, E, B * QT])
        tiles_e = sb("tiles_e", [1, E])
        tiles_to = sb("tiles_to", [1, E])
        jump = sb("jump", [1, E])
        passed = sb("passed", [1, NTILES, E])
        jumped = sb("jumped", [1, NTILES, E])
        tab_f = sb("tab_f", [1, 2, NTILES])
        tile_expert = sb("tile_expert", [1, NTILES], i32)
        tile_row = sb("tile_row", [1, NTILES], i32)
        pad_at = sb("pad_at", [1, E], i32)
        b2_s = sb("b2_s", [E, D])
        empty = sb("empty", [E, D])
        rest = sb("rest", [E, D])
        room = ctx_ring[:, :, :, :].rearrange("p r j d -> p (r j d)")
        tile_in = room[:, 0:RING * ROW].rearrange("p (r n) -> p r n", r=RING)
        tile_out = room[:, RING * ROW:RING * (ROW + D)].rearrange("p (r n) -> p r n", r=RING)
        tile_T = sb("tile_T", [P, 2, P])
        w1_now = sb("w1_now", [P, 2, W2_AT])
        W2R = 4
        w2_now = q_pad[:, :, :].rearrange("p h s -> p (h s)")[:, 0:W2R * (PACK - W2_AT)].rearrange(
            "p (r n) -> p r n", r=W2R)
        hidden = sb("hidden", [P, 2, F])

        ps_s = [pb("ps_s0"), pb("ps_s1")]
        ps_t = [pb("ps_t0"), pb("ps_t1")]
        ps_o = pb("ps_o")
        ps_qk = pb("ps_qk")
        ps_v = pb("ps_v")
        ps_w = pb("ps_w")
        ps_lg = ps_w[:, 0:QT * E].rearrange("p (t e) -> p t e", e=E)
        ps_rk = ps_w[:, 0:QT * E].rearrange("p (t e) -> p t e", e=E)
        ps_ct = ps_w[:, QT * E:QT * E + E]
        ps_mean = ps_w[:, 0:B]
        ps_u = ps_w[:, 0:PAIRS * B]
        ps_y = ps_w[0:B, S:S + D]
        kv_banks, q_banks = [ps_t[0], ps_t[1], ps_o], [ps_qk, ps_v, ps_w]
        ps_x = ps_s
        ps_h = ps_t
        ps_out = [ps_o, ps_v]
        ps_c = ps_v[0:E, 0:D]
        ps_rest = ps_v[0:E, D:2 * D]

        ld_x = [sem(f"ld_x{b}") for b in range(2)]
        ld_c = [sem(f"ld_c{b}") for b in range(2)]
        ld_wq, ld_wk, ld_wv, ld_wo = sem("ld_wq"), sem("ld_wk"), sem("ld_wv"), sem("ld_wo")
        ld_bias, ld_small, ld_mask, ld_ffn = sem("ld_bias"), sem("ld_small"), sem("ld_mask"), sem("ld_ffn")
        ld_ring = [sem(f"ld_ring{r}") for r in range(CTXR)]
        ident_ready, const_ready = sem("ident_ready"), sem("const_ready")
        even_zero, odd_zero, tails_zero = sem("even_zero"), sem("odd_zero"), sem("tails_zero")
        pool_chain, dve_chain = sem("pool_chain"), sem("dve_chain")
        biasT_done, biasT_ready = sem("biasT_done"), sem("biasT_ready")
        tg_ready, tgbo_ready = sem("tg_ready"), sem("tgbo_ready")
        xnorm_ready, ctxnow_ready = sem("xnorm_ready"), sem("ctxnow_ready")
        inT_done, inT_ready = sem("inT_done"), sem("inT_ready")
        first_cT_done, first_cT_ready = sem("first_cT_done"), sem("first_cT_ready")
        qk_done, v_done = sem("qk_done"), sem("v_done")
        qk_kept, qodd_kept, v_kept = sem("qk_kept"), sem("qodd_kept"), sem("v_kept")
        scores_done, max_ready, exp_done = sem("scores_done"), sem("max_ready"), sem("exp_done")
        inv_ready, prob_ready = sem("inv_ready"), sem("prob_ready")
        probT_done, probT_kept = sem("probT_done"), sem("probT_kept")
        pv_done, oT_kept = sem("pv_done"), sem("oT_kept")
        wo_done, x2_ready = sem("wo_done"), sem("x2_ready")
        residual_ready = sem("residual_ready")
        rows_ready, x2T_done, x2T_kept = sem("rows_ready"), sem("x2T_done"), sem("x2T_kept")
        logits_done, choice_ready, rank_done, slots_ready = (sem("logits_done"), sem("choice_ready"),
                                                             sem("rank_done"), sem("slots_ready"))
        scattered = sem("scattered")
        csum_ready, ctx_sum_ready, mean_done, mean_kept = (sem("csum_ready"), sem("ctx_sum_ready"), sem("mean_done"),
                                                               sem("mean_kept"))
        u_done, u_kept, y_done, y_kept = sem("u_done"), sem("u_kept"), sem("y_done"), sem("y_kept")
        b1_ready, col_ready = sem("b1_ready"), sem("col_ready")
        empty_done, empty_kept, rest_done, rest_ready = (sem("empty_done"), sem("empty_kept"), sem("rest_done"),
                                                         sem("rest_ready"))
        pad_ready = sem("pad_ready")
        early_table_ready, table_ready = sem("early_table_ready"), sem("table_ready")
        padded, pool_padded = sem("padded"), sem("pool_padded")
        tile_loaded = [sem(f"tile_loaded{r}") for r in range(RING)]
        tileT_done, tileT_kept = sem("tileT_done"), sem("tileT_kept")
        w1_early = sem("w1_early")
        w1_ready, w2_ready, h_done, h_kept = sem("w1_ready"), sem("w2_ready"), sem("h_done"), sem("h_kept")
        y2_done, out_ready = sem("y2_done"), sem("out_ready")
        out_stored = [sem(f"out_stored{r}") for r in range(RING)]

        block = ctx.enter_context(nc.Block())

        @block.sync
        def _(sp):
            x_v = x.rearrange("b (t p) d -> p b t d", p=P)
            c_v = ctx_in[:, 0:S, :].rearrange("b (t p) d -> p b t d", p=P)
            x_d = x_nat[:, :, :].rearrange("p (b t) d -> p b t d", t=QT)
            c_d = ctx_nat[:, :, :].rearrange("p (b t) d -> p b t d", t=QT)
            sp.dma_start(x_d[:, 0], x_v[:, 0]).then_inc(ld_x[0], 16)
            sp.dma_start(c_d[:, 0], c_v[:, 0]).then_inc(ld_c[0], 16)
            sp.dma_start(wk_s[:, :], wk).then_inc(ld_wk, 16)
            for i, (b_, n) in enumerate(((bq, PAIRS), (bk, PAIRS), (bv, PAIRS))):
                sp.dma_start(bias_rows[i * PAIRS:i * PAIRS + n, :],
                             b_.rearrange("(n p) -> n p", p=P)).then_inc(ld_bias, 16)
            sp.dma_start(bias_rows[3 * PAIRS:NB, :], b1.rearrange("e (c p) -> (e c) p", p=P)).then_inc(ld_bias, 16)
            sp.dma_start(wv_s[:, :], wv).then_inc(ld_wv, 16)
            sp.dma_start(wq_s[:, :], wq).then_inc(ld_wq, 16)
            sp.dma_start(mask_all[:, :, :], mask[:, 0:S].partition_broadcast(P)).then_inc(ld_mask, 16)
            sp.dma_start(mask_rows[:, :], mask[:, 0:S]).then_inc(ld_mask, 16)
            sp.dma_start(gates[:, 0:1], g_attn.partition_broadcast(P)).then_inc(ld_small, 16)
            sp.dma_start(gates[:, 1:2], g_ffn.partition_broadcast(P)).then_inc(ld_small, 16)
            sp.dma_start(bo_all[:, :], bo.partition_broadcast(P)).then_inc(ld_small, 16)
            sp.dma_start(br_all[:, :], br.partition_broadcast(P)).then_inc(ld_small, 16)
            sp.dma_start(wr_s[:, :], wr).then_inc(ld_small, 16)
            sp.dma_start(x_nat[:, QT:NT, :], x[1:B].rearrange("b (t p) d -> p (b t) d", p=P)).then_inc(ld_x[1], 16)
            for b in range(1, B):
                sp.dma_start(c_d[:, b], c_v[:, b]).then_inc(ld_c[1], 16)
            sp.dma_start(wo_s[:, :, :], wo.rearrange("(c p) d -> p c d", p=P)).then_inc(ld_wo, 16)
            sp.wait_ge(tails_zero, 1)
            for b in range(B):
                r = b % CTXR
                wait(sp, ctx_sum_ready, b - CTXR + 1)
                sp.dma_start(ctx_ring[:, r, 0:FULL], ctx_in[b, 0:FULL * P, :].rearrange("(p j) d -> p j d", p=P)
                             ).then_inc(ld_ring[r], 16)
                sp.dma_start(tail_ring[0:TAIL, r], ctx_in[b, FULL * P:SK, :]).then_inc(ld_ring[r], 16)
            sp.dma_start(w1_s, w1.rearrange("e d f -> d e f")).then_inc(ld_ffn, 16)
            for e in range(E):
                sp.dma_start(w2_s[:, e], w2[e].rearrange("(c p) d -> p c d", p=P)).then_inc(ld_ffn, 16)
            sp.dma_start(b2_s[:, :], b2).then_inc(ld_ffn, 16)

            sp.wait_ge(const_ready, CONSTS)
            sp.dma_start(sorted_rows[PADROW:PADROW + P, :], pad_rows[:, 0, :]).then_inc(padded, 16)
            sp.wait_ge(pad_ready, 1)
            for e in range(SP_PADS):
                at = sp.value_load(pad_at[0:1, e:e + 1], min_val=0, max_val=PADROW - PADS * P)
                sp.dma_start(sorted_rows[bass.ds(at, PADS * P), :].rearrange("(p t) n -> p t n", p=P),
                             pad_rows[:, :, :]).then_inc(padded, 16)
            sp.wait_ge(early_table_ready, 1)
            for k in range(EARLY):
                at = sp.value_load(tile_row[0:1, k:k + 1], min_val=0, max_val=PADROW)
                if k == 0:
                    sp.wait_ge(scattered, 16 * (NT - QT))
                sp.dma_start(tile_in[:, k], sorted_rows[bass.ds(at, P), :]).then_inc(tile_loaded[k], 16)
            sp.wait_ge(table_ready, 1)
            for k in range(EARLY, RING):
                at = sp.value_load(tile_row[0:1, k:k + 1], min_val=0, max_val=PADROW)
                if k == EARLY:
                    sp.wait_ge(scattered, 16 * NT)
                sp.dma_start(tile_in[:, k], sorted_rows[bass.ds(at, P), :]).then_inc(tile_loaded[k], 16)
            with sp.Fori(1, NTILES // RING) as i:
                for r in range(RING):
                    at = sp.value_load(tile_row[0:1, bass.ds(i * RING + r, 1)], min_val=0, max_val=PADROW)
                    sp.wait_ge(out_stored[r], i * 16)
                    sp.dma_start(tile_in[:, r], sorted_rows[bass.ds(at, P), :]).then_inc(tile_loaded[r], 16)

        @block.gpsimd
        def _(pool):
            g = nc.gpsimd
            n = Count(pool, pool_chain)
            n.up(g.memset(ident[:, :], 0.0))
            n.wait()
            g.affine_select(out=ident[:, :], in_=ident[:, :], compare_op=ALU.not_equal, fill=1.0, base=0,
                            pattern=[[-1, P]], channel_multiplier=1).then_inc(ident_ready, 1)
            q_v = q_pad[:, :, :].rearrange("p (n two) s -> p n two s", two=2)
            pool.wait_ge(ident_ready, 1)
            g.memset(q_v[DK:P, :, 0, :], 0.0).then_inc(even_zero, 1)
            pool.wait_ge(even_zero, 1)
            n.up(g.memset(causal[:, :], 0.0))
            n.up(g.memset(ones_b[:, :], 1.0))
            n.up(g.memset(ones_f[:, :], 1.0))
            n.up(g.memset(eye[:, :, :], 0.0))
            n.up(g.memset(packs[:, :, SEL_AT:PACK], 0.0))
            n.wait()
            for c0 in (0, 2 * P):
                g.affine_select(out=causal[:, c0:c0 + P], in_=causal[:, c0:c0 + P], compare_op=ALU.is_ge,
                                fill=MASKED, base=0, pattern=[[-1, P]], channel_multiplier=1
                                ).then_inc(const_ready, 1)
            g.affine_select(out=before[:, :], in_=ones_b[:, :], compare_op=ALU.is_gt, fill=0.0, base=0,
                            pattern=[[1, P]], channel_multiplier=-1).then_inc(const_ready, 1)
            g.memset(mean_w[:, :], 1.0 / SK).then_inc(const_ready, 1)
            g.memset(ones_r[:, :], 1.0).then_inc(const_ready, 1)
            g.memset(relu_b1[:, :, :], 0.0).then_inc(const_ready, 1)
            n.up(g.iota(iota_i[:, :], pattern=[[1, 64]], base=0, channel_multiplier=0))
            g.iota(token_ids[:, :], pattern=[[P, NT]], base=0, channel_multiplier=1).then_inc(const_ready, 1)
            g.memset(early_e[:, :], 0.0).then_inc(const_ready, 1)
            n.up(g.memset(pad_rows[:, :, :], 0.0))
            n.wait()
            g.memset(pad_rows[:, :, 2 * D:ROW].bitcast(i32), NOBODY).then_inc(const_ready, 1)
            g.tensor_scalar(e_less[:, :], iota_i[:, 0:E], -1000.0, None, ALU.add).then_inc(const_ready, 1)
            g.tensor_scalar(region[:, :], iota_i[:, 0:E], float(CAP), None, ALU.mult).then_inc(const_ready, 1)
            g.tensor_scalar(next_row[:, :], iota_i[:, 0:E], float(CAP), None, ALU.mult).then_inc(const_ready, 1)
            g.tensor_scalar(tile_f[:, :], iota_i[0:1, 0:NTILES], 1.0, None, ALU.mult).then_inc(const_ready, 1)
            g.tensor_scalar(steps_f[:, :], iota_i[0:1, 0:B * QT], float(P), None, ALU.mult
                            ).then_inc(const_ready, 1)
            g.affine_select(out=eye[:, :, :], in_=eye[:, :, :], compare_op=ALU.not_equal, fill=1.0, base=0,
                            pattern=[[1, E], [-1, E]], channel_multiplier=0).then_inc(const_ready, 1)
            g.affine_select(out=packs[:, :, SEL_AT:PACK], in_=packs[:, :, SEL_AT:PACK], compare_op=ALU.not_equal,
                            fill=1.0, base=0, pattern=[[-1, E], [0, P]], channel_multiplier=1
                            ).then_inc(const_ready, 1)
            g.affine_select(out=others_p[:, :], in_=ones_f[:, 0:E], compare_op=ALU.not_equal, fill=0.0, base=0,
                            pattern=[[-1, E]], channel_multiplier=1).then_inc(const_ready, 1)
            g.memset(tail_ring[:, :, :], 0.0).then_inc(tails_zero, 1)

            def normalise(p, h, slot):
                if h == 0:
                    pool.wait_ge(inv_ready, p + 1)
                g.tensor_tensor(prob[:, slot, 0:P], prob[:, slot, 0:P],
                                row_inv[:, slot, 0:1].to_broadcast([P, P]), ALU.mult).then_inc(prob_ready, 1)
                g.tensor_tensor(prob[:, slot, P:W3], prob[:, slot, P:W3],
                                row_inv[:, slot, 1:2].to_broadcast([P, S]), ALU.mult).then_inc(prob_ready, 1)

            def sum_context(b):
                r = b % CTXR
                pool.wait_ge(ld_ring[r], 32 * (b // CTXR + 1))
                n.up(g.tensor_tensor(ctx_ring[:, r, 0:6, :], ctx_ring[:, r, 0:6, :], ctx_ring[:, r, 6:12, :], ALU.add))
                n.wait()
                g.tensor_tensor(ctx_ring[:, r, 9:12, :], ctx_ring[:, r, 0:3, :], ctx_ring[:, r, 3:6, :], ALU.add
                                ).then_inc(csum_ready, 1)

            def residual_of(b):
                wait(pool, x2_ready, 2 * b)
                pool.wait_ge(ld_x[1], 16)
                g.tensor_tensor(residual[:, :, :], x_nat[:, bass.ds(b * QT, QT), :],
                                tg_bo[:, None, :].to_broadcast([P, QT, D]), ALU.add).then_inc(residual_ready, 1)

            def scatter(b):
                pool.wait_ge(slots_ready, b + 1)
                settle(pool)
                for t in range(QT):
                    g.indirect_dma_start(out=sorted_rows[:, :],
                                         out_offset=bass.IndirectOffsetOnAxis(ap=slot_i[:, t:t + 1], axis=0),
                                         in_=rows[:, t, :], in_offset=None).then_inc(scattered, 16)

            def batch(b, first=False, last=False):
                for j in range(PAIRS):
                    if not (last and j >= PAIRS - AHEAD):
                        for h in range(2):
                            normalise(8 * b + j + AHEAD, h, (2 * (j + AHEAD) + h) % SLOTS)
                    if j == 1:
                        if first:
                            pool.wait_ge(tgbo_ready, 1)
                        residual_of(b)
                    if j == 7 and not first:
                        scatter(b - 1)
                    if first and j + 1 < len(POOL_SUMS):
                        sum_context(POOL_SUMS[j + 1])

            sum_context(0)
            for j in range(AHEAD):
                for h in range(2):
                    normalise(j, h, 2 * j + h)
            pool.wait_ge(tg_ready, 1)
            g.tensor_scalar(tg_bo[:, :], bo_all[:, :], tg[:, 0:1], None, ALU.mult).then_inc(tgbo_ready, 1)
            batch(0, first=True)
            with pool.Fori(1, B - 1) as b:
                batch(b)
            batch(B - 1, last=True)

            pool.wait_ge(pad_ready, 1)
            pool.wait_ge(tile_loaded[0], 16)
            for e in range(SP_PADS, E):
                at = pool.value_load(pad_at[0:1, e:e + 1], min_val=0, max_val=PADROW - PADS * P)
                pool.dma_start(sorted_rows[bass.ds(at, PADS * P), :].rearrange("(p t) n -> p t n", p=P),
                               pad_rows[:, :, :]).then_inc(pool_padded, 16)

            out_rows = out.rearrange("b s d -> (b s) d")

            def store(tile, r):
                pool.wait_ge(out_ready, tile + 1)
                settle(pool)
                g.indirect_dma_start(
                    out=out_rows, out_offset=bass.IndirectOffsetOnAxis(
                        ap=tile_in[:, r, 2 * D:ROW].bitcast(i32), axis=0),
                    in_=tile_out[:, r, :], in_offset=None, bounds_check=B * S - 1, oob_is_err=False
                ).then_inc(out_stored[r], 16)

            pool.wait_ge(padded, 16 * (SP_PADS + 1))
            pool.wait_ge(pool_padded, 16 * (E - SP_PADS))
            scatter(B - 1)
            for tile in range(EARLY):
                store(tile, tile)
            with pool.Fori(0, TURNS) as i:
                for r in range(RING):
                    store(i * RING + EARLY + r, (EARLY + r) % RING)
            for r in range(RING):
                pool.wait_ge(out_stored[r], 16 * (TURNS + (r < EARLY)))

        @block.scalar
        def _(act):
            s = nc.scalar

            def context_now(b):
                act.wait_ge(ld_c[1], 16 * (B - 1))
                wait(act, inT_done, b)
                s.activation(ctx_now[:, :, :], ctx_nat[:, bass.ds(b * QT, QT), :], ACT.Copy
                             ).then_inc(ctxnow_ready, 1)

            def keep_inT(b):
                act.wait_ge(inT_done, b + 1)
                s.activation(in_T[:, :], ps_qk[:, :], ACT.Copy).then_inc(inT_ready, 1)

            def keep_q(p, j, bank):
                act.wait_ge(qk_done, p + 1)
                s.activation(q_pad[0:DK, 2 * j, :], bank[0:DK, 0:S], ACT.Identity,
                             bias=bias_T[0:DK, j:j + 1]).then_inc(qk_kept, 1)

            def keep_k(j, keys):
                s.activation(k_T[:, j, :], keys, ACT.Identity,
                             bias=bias_T[:, PAIRS + j:PAIRS + j + 1]).then_inc(qk_kept, 1)

            def keep_qk(p, j):
                keep_q(p, j, ps_qk)
                act.wait_ge(qodd_kept, p + 1)
                keep_k(j, ps_qk[:, S:2 * S])

            def keep_oT(b, p, j):
                act.wait_ge(pv_done, p + 1)
                wait(act, wo_done, b)
                s.activation(o_T[:, j, :], ps_o[:, 0:S], ACT.Identity,
                             bias=bias_T[:, 2 * PAIRS + j:2 * PAIRS + j + 1]).then_inc(oT_kept, 1)

            def keep_v(p, j, values=ps_v[:, 0:S]):
                act.wait_ge(v_done, p + 1)
                s.activation(v_nat[:, :, j * P:(j + 1) * P],
                             values.rearrange("p (t n) -> p t n", t=QT), ACT.Copy).then_inc(v_kept, 1)

            def exponential(p, h, slot):
                head = 2 * p + h
                act.wait_ge(max_ready, 2 * head + 2)
                wait(act, probT_done, head + 1 - SLOTS)
                for t, (lo, hi) in enumerate(((0, P), (P, W3))):
                    s.activation(prob[:, slot, lo:hi], masked[:, slot % 2, lo:hi], ACT.Exp,
                                 bias=neg_max[:, slot, t:t + 1], scale=-1.0,
                                 accum_out=row_sum[:, slot, t:t + 1]).then_inc(exp_done, 1)

            def keep_x2T(b):
                act.wait_ge(x2T_done, b + 1)
                s.activation(x2_T[:, :], ps_w[:, S:2 * S], ACT.Copy).then_inc(x2T_kept, 1)

            def batch(b, first=False, last=False):
                for j in range(PAIRS):
                    if j == 0 and not last:
                        context_now(b + 1)
                    if j == 4 and not first:
                        keep_x2T(b - 1)
                    if first and j == 6:
                        act.wait_ge(mean_done, B)
                        s.activation(ctx_mean[:, :], ps_mean, ACT.Copy).then_inc(mean_kept, 1)
                    if not (last and j >= PAIRS - AHEAD):
                        for h in range(2):
                            exponential(8 * b + j + AHEAD, h, (2 * (j + AHEAD) + h) % SLOTS)
                    if not last:
                        if j > 0:
                            keep_qk(8 * (b + 1) + j - 1, j - 1)
                            keep_v(8 * (b + 1) + j - 1, j - 1)
                    if first and j == 7:
                        act.wait_ge(u_done, 2)
                        s.activation(u_T[:, :, :], ps_u.rearrange("p (n b) -> p n b", b=B), ACT.Copy
                                     ).then_inc(u_kept, 1)
                    keep_oT(b, 8 * b + j, j)
                    if j == 0 and not last:
                        keep_inT(b + 1)
                if not last:
                    keep_qk(8 * (b + 1) + 7, 7)
                    keep_v(8 * (b + 1) + 7, 7)

            act.wait_ge(first_cT_done, 1)
            s.activation(cT, ps_s[0][:, 0:S], ACT.Copy).then_inc(first_cT_ready, 1)
            act.wait_ge(biasT_done, 1)
            s.activation(bias_T[:, :], ps_w[:, 0:NB], ACT.Copy).then_inc(biasT_ready, 1)
            act.wait_ge(biasT_ready, 1)
            for j in range(PAIRS):
                if j == X_AT:
                    act.wait_ge(inT_done, 1)
                    s.activation(xT, ps_s[1][:, 0:S], ACT.Copy).then_inc(inT_ready, 1)
                act.wait_ge(v_done, j + 1)
                keep_k(j, kv_banks[j % 3][:, 0:S])
                keep_v(j, j, kv_banks[j % 3][:, S:2 * S])
            act.wait_ge(ld_small, 16 * 5)
            s.activation(tg[:, :], gates[:, :], ACT.Tanh).then_inc(tg_ready, 1)
            act.wait_ge(even_zero, 1)
            act.wait_ge(odd_zero, 1)
            for j in range(PAIRS):
                if 3 <= j < 3 + AHEAD:
                    for h in range(2):
                        exponential(j - 3, h, 2 * (j - 3) + h)
                keep_q(j, j, q_banks[j % 3])
            batch(0, first=True)
            with act.Fori(1, B - 1) as b:
                batch(b)
            batch(B - 1, last=True)

            def keep_tileT(tile, r):
                act.wait_ge(tileT_done, tile + 1)
                s.activation(tile_T[:, r % 2, :], ps_x[r % 2][:, 0:P], ACT.Copy).then_inc(tileT_kept, 1)

            def keep_hidden(tile, r):
                act.wait_ge(h_done, tile + 1)
                for c in range(FC):
                    s.activation(hidden[:, r % 2, c * P:(c + 1) * P], ps_h[r % 2][:, c * P:(c + 1) * P], ACT.Relu,
                                 bias=w1_now[:, r % 2, B1_AT + c:B1_AT + c + 1]).then_inc(h_kept, 1)

            def expert_of(tile):
                return act.value_load(tile_expert[0:1, tile:tile + 1], min_val=0, max_val=E - 1)

            def early_w1(tile, expert):
                wait(act, h_kept, FC * (tile - 1))
                s.activation(w1_now[:, tile % 2, :], packs[:, bass.ds(expert, 1), 0:W2_AT], ACT.Copy
                             ).then_inc(w1_early, 1)

            act.wait_ge(early_table_ready, 1)
            act.wait_ge(ld_ffn, 16 * (E + 2))
            early_w1(0, expert_of(0))
            expert = expert_of(1)
            keep_tileT(0, 0)
            for tile in range(EARLY):
                if tile < EARLY - 1:
                    keep_tileT(tile + 1, tile + 1)
                    early_w1(tile + 1, expert)
                if tile < EARLY - 2:
                    expert = expert_of(tile + 2)
                act.wait_ge(w1_early, tile + 1)
                keep_hidden(tile, tile)
                if tile == LN_AT - 1:
                    keep_x2T(B - 1)
            keep_tileT(EARLY, EARLY % RING)
            with act.Fori(0, TURNS) as i:
                for r in range(RING):
                    tile = i * RING + EARLY + r
                    keep_tileT(tile + 1, (EARLY + r + 1) % RING)
                    act.wait_ge(w1_ready, i * RING + r + 1)
                    keep_hidden(tile, (EARLY + r) % RING)

        @block.vector
        def _(dve):
            v = nc.vector
            n = Count(dve, dve_chain)

            def inverse_root_step(step, a, y, t, final):
                n.wait()
                if step == 0:
                    n.up(v.tensor_scalar(y.bitcast(i32), a.bitcast(i32), -0.5, RS_MAGIC, ALU.mult, ALU.add))
                elif step % 3 == 1:
                    n.up(v.tensor_tensor(t, y, y, ALU.mult))
                elif step % 3 == 2:
                    n.up(v.scalar_tensor_tensor(out=t, in0=t, scalar=-0.5, in1=a, op0=ALU.mult, op1=ALU.mult))
                else:
                    n.up(v.scalar_tensor_tensor(out=final if step == 9 else y, in0=t, scalar=1.5, in1=y,
                                                op0=ALU.add, op1=ALU.mult))

            def norm_stats(b):
                for t in range(b * QT, (b + 1) * QT):
                    n.up(v.bn_stats(stats[:, t, :], x_nat[:, t, :]))

            def norm_sums(b):
                n.wait()
                for t in range(b * QT, (b + 1) * QT):
                    n.up(v.bn_aggr(mv[:, t, :], stats[:, t, :]))

            def norm_scales(lo, hi, step):
                if step == 0:
                    n.wait()
                    n.up(v.tensor_scalar(rs_a[:, lo:hi], mv[:, lo:hi, 1], EPS, None, ALU.add))
                elif step < 11:
                    inverse_root_step(step - 1, rs_a[:, lo:hi], rs_y[:, lo:hi], rs_t[:, lo:hi], rstd[:, lo:hi])
                else:
                    n.wait()
                    n.up(v.scalar_tensor_tensor(out=nmr[:, lo:hi], in0=mv[:, lo:hi, 0], scalar=-1.0,
                                                in1=rstd[:, lo:hi], op0=ALU.mult, op1=ALU.mult))

            def normalise_x(b):
                wait(dve, inT_done, b)
                for t in range(QT):
                    i = b * QT + t
                    v.tensor_scalar(x_norm[:, t, :], x_nat[:, bass.ds(i, 1), :], rstd[:, bass.ds(i, 1)],
                                    nmr[:, bass.ds(i, 1)], ALU.mult, ALU.add).then_inc(xnorm_ready, 1)

            def mask_of(b):
                for lo, hi, keys in ((0, P, P), (P, W3, S)):
                    n.up(v.scalar_tensor_tensor(out=mask_now[:, lo:hi], in0=mask_all[:, bass.ds(b, 1), 0:keys],
                                                scalar=MASKED, in1=causal[:, lo:hi], op0=ALU.mult, op1=ALU.add))
                n.wait()

            def maximum(p, h, slot):
                head = 2 * p + h
                dve.wait_ge(scores_done, head + 1)
                wait(dve, exp_done, 2 * (head - 1))
                settle(dve)
                for t, (lo, hi) in enumerate(((0, P), (P, W3))):
                    v.tensor_tensor_reduce(out=masked[:, slot % 2, lo:hi], in0=ps_s[slot % 2][:, lo:hi],
                                           in1=mask_now[:, lo:hi], scale=-SCALE, scalar=FLOOR, op0=ALU.add,
                                           op1=ALU.min, accum_out=neg_max[:, slot, t:t + 1]).then_inc(max_ready, 1)

            def fix_sums(p, slot):
                dve.wait_ge(exp_done, 4 * p + 4)
                n.up(v.tensor_scalar(row_fix[:, slot:slot + 2, :], row_sum[:, slot:slot + 2, :], 1e-30, None,
                                     ALU.max))

            def invert_sums(p, slot):
                wait(dve, prob_ready, 4 * (p + 1) - 2 * SLOTS)
                n.wait()
                v.reciprocal(row_inv[:, slot:slot + 2, :], row_fix[:, slot:slot + 2, :]).then_inc(inv_ready, 1)

            def keep_probT(p, h, slot):
                head = 2 * p + h
                dve.wait_ge(probT_done, head + 1)
                wait(dve, pv_done, p - 1)
                v.tensor_copy(prob_T[:, slot % TSLOTS, :], ps_t[slot % 2][:, 0:W3]).then_inc(probT_kept, 1)

            def keep_qodd(p, j, bank=ps_qk):
                dve.wait_ge(qk_done, p + 1)
                v.tensor_scalar(q_pad[DK:P, 2 * j + 1, :], bank[DK:P, 0:S], bias_T[DK:P, j:j + 1], None, ALU.add
                                ).then_inc(qodd_kept, 1)

            def second_norm(b, step, bank=ps_w):
                a, y, t_ = rs_a[:, 0:QT], rs_y[:, 0:QT], rs_t[:, 0:QT]
                if step == 0:
                    dve.wait_ge(wo_done, b + 1)
                    dve.wait_ge(residual_ready, b + 1)
                    wait(dve, scattered, 16 * QT * b)
                    for t in range(QT):
                        v.scalar_tensor_tensor(out=rows[:, t, 0:D], in0=bank[:, t * D:(t + 1) * D],
                                               scalar=tg[:, 0:1], in1=residual[:, t, :], op0=ALU.mult, op1=ALU.add
                                               ).then_inc(x2_ready, 1)
                    n.up(v.tensor_copy(rows[:, :, 2 * D].bitcast(i32), token_ids[:, bass.ds(b * QT, QT)]))
                elif step == 1:
                    dve.wait_ge(x2_ready, 2 * (b + 1))
                    for t in range(QT):
                        n.up(v.bn_stats(stats2[:, t, :], rows[:, t, 0:D]))
                elif step == 2:
                    n.wait()
                    settle(dve)
                    for t in range(QT):
                        n.up(v.bn_aggr(mv2[:, t, :], stats2[:, t, :]))
                elif step == 3:
                    n.wait()
                    n.up(v.tensor_scalar(a, mv2[:, :, 1], EPS, None, ALU.add))
                elif step < 14:
                    inverse_root_step(step - 4, a, y, t_, rstd2[:, :])
                elif step == 14:
                    n.wait()
                    n.up(v.scalar_tensor_tensor(out=nmr2[:, :], in0=mv2[:, :, 0], scalar=-1.0, in1=rstd2[:, :],
                                                op0=ALU.mult, op1=ALU.mult))
                elif step == 15:
                    n.wait()
                    for t in range(QT):
                        v.tensor_scalar(rows[:, t, D:2 * D], rows[:, t, 0:D], rstd2[:, t:t + 1], nmr2[:, t:t + 1],
                                        ALU.mult, ALU.add).then_inc(rows_ready, 1)

            def choose(b, step):
                number = e_less[:, None, :].to_broadcast([P, QT, E])
                if step == 0:
                    dve.wait_ge(logits_done, b + 1)
                    n.up(v.tensor_tensor(logits[:, :, :], ps_lg, br_all[:, None, :].to_broadcast([P, QT, E]), ALU.add))
                elif step == 1:
                    n.wait()
                    n.up(v.reduce_max(best[:, :], logits[:, :, :], AX.X))
                elif step == 2:
                    n.wait()
                    n.up(v.tensor_tensor(hit[:, :, :], logits[:, :, :], best[:, :, None].to_broadcast([P, QT, E]),
                                         ALU.is_equal))
                elif step == 3:
                    n.wait()
                    n.up(v.tensor_tensor(hit[:, :, :], hit[:, :, :], number, ALU.mult))
                elif step == 4:
                    n.wait()
                    n.up(v.tensor_reduce(pick[:, :], hit[:, :, :], AX.X, ALU.min))
                elif step == 5:
                    n.wait()
                    mine = pick[:, :, None].to_broadcast([P, QT, E])
                    v.tensor_tensor(choice_b[:, :, :], number, mine, ALU.is_equal).then_inc(choice_ready, 1)
                    n.up(v.tensor_tensor(choice[:, :, :], number, mine, ALU.is_equal))

            def place(b, step):
                if step == 0:
                    dve.wait_ge(rank_done, b + 1)
                    n.wait()
                    n.up(v.tensor_tensor(rank[:, :, :], ps_rk, next_row[:, None, :].to_broadcast([P, QT, E]), ALU.add))
                elif step == 1:
                    n.wait()
                    n.up(v.tensor_tensor(rank[:, :, :], rank[:, :, :], choice[:, :, :], ALU.mult))
                    n.up(v.tensor_tensor(next_row[:, :], next_row[:, :], ps_ct, ALU.add))
                elif step == 2:
                    n.wait()
                    n.up(v.reduce_sum(slot_f[:, :], rank[:, :, :], AX.X))
                elif step == 3:
                    n.wait()
                    v.tensor_copy(slot_i[:, :], slot_f[:, :]).then_inc(slots_ready, 1)

            def sum_context(b, step):
                r = b % CTXR
                if step == 0:
                    dve.wait_ge(ld_ring[r], 32 * (b // CTXR + 1))
                    n.up(v.tensor_tensor(ctx_ring[:, r, 0:6, :], ctx_ring[:, r, 0:6, :], ctx_ring[:, r, 6:12, :],
                                         ALU.add))
                elif step == 1:
                    n.wait()
                    n.up(v.tensor_tensor(ctx_ring[:, r, 9:12, :], ctx_ring[:, r, 0:3, :], ctx_ring[:, r, 3:6, :],
                                         ALU.add))
                else:
                    if b in POOL_SUMS:
                        dve.wait_ge(csum_ready, POOL_SUMS.index(b) + 1)
                    n.wait()
                    v.reduce_sum(ctx_sum[:, b, :], ctx_ring[:, r, 9:13, :].rearrange("p j d -> p d j"), AX.X
                                 ).then_inc(ctx_sum_ready, 1)

            def bias_columns(step):
                b1_T = bias_T[:, 3 * PAIRS:NB].rearrange("p (e c) -> p e c", e=E)
                if step == 0:
                    n.up(v.tensor_scalar(relu_b1[:, :, :], b1_T, 0.0, None, ALU.max))
                    v.tensor_copy(packs[:, :, B1_AT:W2_AT], b1_T).then_inc(b1_ready, 1)
                else:
                    n.wait()
                    v.tensor_tensor(relu_col[:, :, :, :], relu_b1[:, :, :, None].to_broadcast([P, E, FC, E]),
                                    eye[:, :, None, :].to_broadcast([P, E, FC, E]), ALU.mult).then_inc(col_ready, 1)

            def tiles_so_far(extra):
                n.up(v.scalar_tensor_tensor(out=count_1[:, :], in0=next_row[0:1, :], scalar=float(extra),
                                            in1=region[0:1, :], op0=ALU.add, op1=ALU.subtract))
                n.wait()
                n.up(v.tensor_tensor(full_c[:, :, :], count_1[:, :, None].to_broadcast([1, E, B * QT]),
                                     steps_f[:, None, :].to_broadcast([1, E, B * QT]), ALU.is_gt))
                n.wait()
                n.up(v.reduce_sum(tiles_e[:, :], full_c[:, :, :], AX.X))

            def passed_by(k0, k1):
                K = k1 - k0
                n.up(v.tensor_tensor(passed[:, 0:K, :], tile_f[:, 0:K, None].to_broadcast([1, K, E]),
                                     tiles_to[:, None, :].to_broadcast([1, K, E]), ALU.is_ge))

            def jumps_of(k0, k1):
                K = k1 - k0
                n.up(v.reduce_sum(tab_f[:, 0, k0:k1], passed[:, 0:K, :], AX.X))
                n.up(v.tensor_tensor(jumped[:, 0:K, :], passed[:, 0:K, :], jump[:, None, :].to_broadcast([1, K, E]),
                                     ALU.mult))

            def expert_and_jump(k0, k1):
                n.up(v.reduce_sum(tab_f[:, 1, k0:k1], jumped[:, 0:k1 - k0, :], AX.X))
                n.up(v.tensor_scalar(tile_expert[:, k0:k1], tab_f[:, 0, k0:k1], float(E - 1), None, ALU.min))

            def first_rows(k0, k1):
                n.up(v.scalar_tensor_tensor(out=tab_f[:, 1, k0:k1], in0=tile_f[:, 0:k1 - k0], scalar=float(P),
                                            in1=tab_f[:, 1, k0:k1], op0=ALU.mult, op1=ALU.add))

            def early_table(step):
                n.wait()
                if step == 0:
                    v.tensor_copy(pad_at[:, :], next_row[0:1, :]).then_inc(pad_ready, 1)
                    tiles_so_far(1 - P)
                elif step == 1:
                    n.up(v.tensor_tensor_scan(tiles_to[:, :], ones_r[0:1, 0:E], tiles_e[:, :], 0.0, ALU.mult, ALU.add))
                    n.up(v.tensor_scalar(jump[:, :], tiles_e[:, :], -float(P), float(CAP), ALU.mult, ALU.add))
                elif step == 2:
                    passed_by(0, EARLY)
                    n.up(v.tensor_tensor(before_e[:, :], tiles_e[:, :], tiles_to[:, :], ALU.subtract))
                elif step == 3:
                    jumps_of(0, EARLY)
                    n.up(v.tensor_scalar(before_e[:, :], before_e[:, :], float(EARLY), None, ALU.add))
                elif step == 4:
                    expert_and_jump(0, EARLY)
                    n.up(v.scalar_tensor_tensor(out=early_e[:, 0:E], in0=before_e[:, :], scalar=0.0,
                                                in1=tiles_e[:, :], op0=ALU.max, op1=ALU.min))
                elif step == 5:
                    first_rows(0, EARLY)
                    n.up(v.tensor_tensor(jump_late[:, :], early_e[:, 1:E + 1], early_e[:, 0:E], ALU.subtract))
                    n.up(v.tensor_scalar(start_late[:, :], early_e[:, 0:1], float(P), None, ALU.mult))
                elif step == 6:
                    n.up(v.tensor_scalar(tile_row[:, 0:EARLY], tab_f[:, 1, 0:EARLY], float(PADROW), None, ALU.min))
                    n.up(v.tensor_scalar(jump_late[:, :], jump_late[:, :], float(P), float(CAP), ALU.mult, ALU.add))
                elif step == 7:
                    v.engine_nop().then_inc(early_table_ready, 1)

            def late_table(step):
                n.wait()
                if step == 0:
                    tiles_so_far(0)
                elif step == 1:
                    n.up(v.tensor_tensor(tiles_e[:, :], tiles_e[:, :], early_e[:, 0:E], ALU.subtract))
                elif step == 2:
                    n.up(v.tensor_tensor_scan(tiles_to[:, :], ones_r[0:1, 0:E], tiles_e[:, :], 0.0, ALU.mult, ALU.add))
                    n.up(v.scalar_tensor_tensor(out=jump[:, :], in0=tiles_e[:, :], scalar=-float(P),
                                                in1=jump_late[:, :], op0=ALU.mult, op1=ALU.add))
                elif step == 3:
                    passed_by(EARLY, NTILES)
                elif step == 4:
                    jumps_of(EARLY, NTILES)
                elif step == 5:
                    expert_and_jump(EARLY, NTILES)
                elif step == 6:
                    first_rows(EARLY, NTILES)
                elif step == 7:
                    n.up(v.tensor_scalar(tile_row[:, EARLY:NTILES], tab_f[:, 1, EARLY:NTILES], start_late[0:1, 0:1],
                                         float(PADROW), ALU.add, ALU.min))
                elif step == 8:
                    v.engine_nop().then_inc(table_ready, 1)

            def between(b, j, at, first, last):
                here = 6 * j + at
                if first:
                    if here < 3 * (B - 2):
                        if here % 3 == 1:
                            norm_stats(2 + here // 3)
                        if here % 3 == 2:
                            norm_sums(2 + here // 3)
                    if 20 <= here < 32:
                        norm_scales(2 * QT, NT, here - 20)
                    if 40 <= here < 42:
                        bias_columns(here - 40)
                    for i, at_ in enumerate(SUM_AT):
                        if 0 <= here - at_ < 3 and (i not in POOL_SUMS or here - at_ == 2):
                            sum_context(i, here - at_)
                    return
                if 4 <= here < 20:
                    second_norm(b - 1, here - 4)
                if 30 <= here < 36:
                    choose(b - 1, here - 30)
                if 38 <= here < 42:
                    place(b - 1, here - 38)
                if last and here >= 42:
                    for step in ((0,), (1,), (2,), (3,), (4, 5), (6, 7))[here - 42]:
                        early_table(step)

            def batch(b, first=False, last=False):
                for j in range(PAIRS):
                    p = 8 * b + j
                    ahead = not (last and j >= PAIRS - AHEAD)
                    if j == 0 and not last:
                        normalise_x(b + 1)
                    for h in range(2):
                        if ahead:
                            maximum(p + AHEAD, h, (2 * (j + AHEAD) + h) % SLOTS)
                        between(b, j, 2 * h, first, last)
                        if not (last and j == PAIRS - 1):
                            keep_probT(p + 1, h, (2 * j + 2 + h) % SLOTS)
                        between(b, j, 2 * h + 1, first, last)
                    if not last and j > 0:
                        keep_qodd(8 * (b + 1) + j - 1, j - 1)
                    if ahead:
                        fix_sums(p + AHEAD, 2 * (j + AHEAD) % SLOTS)
                    between(b, j, 4, first, last)
                    if ahead:
                        invert_sums(p + AHEAD, 2 * (j + AHEAD) % SLOTS)
                    between(b, j, 5, first, last)
                    if j == PAIRS - AHEAD - 1 and not last:
                        dve.wait_ge(max_ready, 4 * 8 * (b + 1))
                        mask_of(b + 1)
                    if first:
                        if j == 5:
                            n.up(v.tensor_copy(mask_f[:, :], mask_rows[:, :]))
                            n.wait()
                            v.tensor_tensor_scan(blind[:, :], mask_f[:, :], mask_f[:, :], 1.0, ALU.min, ALU.min
                                                 ).then_inc(y_kept, 1)
                        if j == 7:
                            dve.wait_ge(y_done, 1)
                            v.tensor_copy(mean_y[:, :], ps_y).then_inc(y_kept, 1)
                            dve.wait_ge(y_kept, 2)
                            v.tensor_tensor(mean_rows[:, :, :], mean_y[:, None, :].to_broadcast([B, B, D]),
                                            ident[0:B, 0:B, None].to_broadcast([B, B, D]), ALU.mult
                                            ).then_inc(y_kept, 1)
                if not last:
                    keep_qodd(8 * (b + 1) + 7, 7)

            q_v = q_pad[:, :, :].rearrange("p (n two) s -> p n two s", two=2)
            v.memset(q_v[0:DK, :, 1, :], 0.0).then_inc(odd_zero, 1)
            dve.wait_ge(ld_x[0], 16)
            norm_stats(0)
            norm_sums(0)
            for step in range(12):
                norm_scales(0, QT, step)
            n.wait()
            normalise_x(0)
            dve.wait_ge(ld_mask, 16 * 2)
            dve.wait_ge(const_ready, CONSTS)
            mask_of(0)
            dve.wait_ge(biasT_ready, 1)
            for j in range(PAIRS):
                if j > 2:
                    norm_scales(QT, 2 * QT, 2 * j - 6)
                if 3 <= j < 3 + AHEAD:
                    for h in range(2):
                        maximum(j - 3, h, 2 * (j - 3) + h)
                keep_qodd(j, j, q_banks[j % 3])
                if j > 2:
                    norm_scales(QT, 2 * QT, 2 * j - 5)
                if 4 <= j < 4 + AHEAD:
                    fix_sums(j - 4, 2 * (j - 4))
                    invert_sums(j - 4, 2 * (j - 4))
                if j == 1:
                    dve.wait_ge(ld_x[1], 16)
                    norm_stats(1)
                if j == 2:
                    norm_sums(1)
            for h in range(2):
                norm_scales(QT, 2 * QT, 10 + h)
                keep_probT(0, h, h)
            n.wait()
            batch(0, first=True)
            dve.wait_ge(ld_small, 16 * 5)
            dve.wait_ge(const_ready, CONSTS)
            with dve.Fori(1, B - 1) as b:
                n.enter(b - 1, PER_BATCH)
                batch(b)
                n.leave(B - 2)
            batch(B - 1, last=True)
            def weights_of(tile, r, part):
                if part == 0:
                    dve.wait_ge(h_kept, FC * (tile - 1))
                    v.tensor_copy(w1_now[:, r % 2, :], packs[:, bass.ds(expert, 1), 0:W2_AT]).then_inc(w1_ready, 1)
                else:
                    wait(dve, y2_done, tile - W2R + 1)
                    v.tensor_copy(w2_now[:, r % W2R, :], packs[:, bass.ds(expert, 1), W2_AT:PACK]
                                  ).then_inc(w2_ready, 1)

            def finish(tile, r):
                dve.wait_ge(y2_done, tile + 1)
                v.scalar_tensor_tensor(out=tile_out[:, r, :], in0=ps_out[r % 2][:, 0:D], scalar=tg[:, 1:2],
                                       in1=tile_in[:, r, 0:D], op0=ALU.mult, op1=ALU.add).then_inc(out_ready, 1)

            def expert_of(tile):
                return dve.value_load(tile_expert[0:1, bass.ds(tile, 1)], min_val=0, max_val=E - 1)

            dve.wait_ge(ld_ffn, 16 * (E + 2))
            for step in range(16):
                second_norm(B - 1, step, ps_qk)
            dve.wait_ge(empty_done, 1)
            n.up(v.tensor_copy(empty[:, :], ps_c))
            n.wait()
            v.tensor_tensor(empty[:, :], empty[:, :], b2_s[:, :], ALU.add).then_inc(empty_kept, 1)
            expert = expert_of(0)
            weights_of(0, 0, 1)
            dve.wait_ge(rest_done, 1)
            v.tensor_tensor(rest[:, :], ps_rest, b2_s[:, :], ALU.add).then_inc(rest_ready, 1)
            expert = expert_of(1)
            weights_of(1, 1, 1)
            for step in range(6):
                choose(B - 1, step)
            for tile in range(2, W2R):
                expert = expert_of(tile)
                weights_of(tile, tile, 1)
            expert = expert_of(W2R)
            finish(0, 0)
            weights_of(W2R, W2R, 1)
            for step in range(4):
                place(B - 1, step)
            for step in range(9):
                if step == 3:
                    finish(1, 1)
                late_table(step)
            expert = expert_of(W2R + 1)
            weights_of(W2R + 1, W2R + 1, 1)
            finish(2, 2)
            expert = expert_of(W2R + 2)
            weights_of(W2R + 2, W2R + 2, 1)
            finish(3, 3)
            expert = expert_of(EARLY)
            weights_of(EARLY, EARLY, 0)
            finish(4, 4)
            weights_of(EARLY, EARLY, 1)
            with dve.Fori(0, TURNS) as i:
                for r in range(RING):
                    tile = i * RING + EARLY + r
                    expert = expert_of(tile + 1)
                    weights_of(tile + 1, EARLY + r + 1, 0)
                    finish(tile - 2, (EARLY + r - 2) % RING)
                    weights_of(tile + 1, EARLY + r + 1, 1)
            for tile in range(MT - 2, MT):
                finish(tile, tile % RING)

        @block.tensor
        def _(pe):
            t_ = nc.tensor

            def mm(out_, lhsT, rhs, start=True, stop=True, loose=False):
                return t_.matmul(out_, lhsT, rhs, start=start, stop=stop, skip_group_check=loose)

            def input_transposes(b):
                pe.wait_ge(xnorm_ready, 2 * b + 2)
                pe.wait_ge(ctxnow_ready, b)
                wait(pe, qk_kept, 16 * b)
                wait(pe, qodd_kept, 8 * b)
                for t in range(QT):
                    t_.transpose(ps_qk[:, t * P:(t + 1) * P], x_norm[:, t, :], ident[:, :])
                for t in range(QT):
                    last = t_.transpose(ps_qk[:, S + t * P:S + (t + 1) * P], ctx_now[:, t, :], ident[:, :])
                last.then_inc(inT_done, 1)

            def project_qk(b, j):
                p = 8 * b + j
                if j == 0:
                    pe.wait_ge(inT_ready, b + 1)
                wait(pe, qk_kept, 2 * p)
                wait(pe, qodd_kept, p)
                mm(ps_qk[:, 0:S], wq_s[:, j * P:(j + 1) * P], xT)
                mm(ps_qk[:, S:2 * S], wk_s[:, j * P:(j + 1) * P], cT).then_inc(qk_done, 1)

            def first_kv(j):
                bank = kv_banks[j % 3]
                wait(pe, qk_kept, j - 2)
                wait(pe, v_kept, j - 2)
                mm(bank[:, 0:S], wk_s[:, j * P:(j + 1) * P], cT)
                if j == 0:
                    pe.wait_ge(ld_wv, 16)
                for t in range(QT):
                    last = mm(bank[:, S + t * P:S + (t + 1) * P], cT[:, t * P:(t + 1) * P],
                              wv_s[:, j * P:(j + 1) * P])
                last.then_inc(v_done, 1)

            def first_q(j):
                wait(pe, qk_kept, PAIRS + j - 2 if j > 2 else 0)
                wait(pe, qodd_kept, j - 2)
                mm(q_banks[j % 3][:, 0:S], wq_s[:, j * P:(j + 1) * P], xT).then_inc(qk_done, 1)

            def project_v(b, j):
                p = 8 * b + j
                wait(pe, v_kept, p)
                for t in range(QT):
                    last = mm(ps_v[:, t * P:(t + 1) * P], cT[:, t * P:(t + 1) * P], wv_s[:, j * P:(j + 1) * P])
                last.then_inc(v_done, 1)

            def scores(p, j, h, kept=None):
                head = 2 * p + h
                pe.wait_ge(qk_kept, 2 * p + 2 if kept is None else kept)
                if h == 1:
                    pe.wait_ge(qodd_kept, p + 1)
                wait(pe, max_ready, 2 * (head - 1))
                mm(ps_s[h][:, 0:P], q_pad[:, 2 * j + h, 0:P], k_T[:, j, 0:P])
                mm(ps_s[h][:, P:W3], q_pad[:, 2 * j + h, P:S], k_T[:, j, :]).then_inc(scores_done, 1)

            def transpose_probs(p, h, slot):
                head = 2 * p + h
                pe.wait_ge(prob_ready, 2 * head + 2)
                wait(pe, probT_kept, head - 1)
                for i in range(3):
                    last = t_.transpose(ps_t[slot % 2][:, i * P:(i + 1) * P], prob[:, slot, i * P:(i + 1) * P],
                                        ident[:, :])
                last.then_inc(probT_done, 1)

            def values(p, j):
                pe.wait_ge(probT_kept, 2 * p + 2)
                pe.wait_ge(v_kept, p + 1)
                wait(pe, oT_kept, p)
                for t in range(QT):
                    for h in range(2):
                        slot = (2 * j + h) % TSLOTS
                        last = mm(ps_o[h * DK:(h + 1) * DK, t * P:S],
                                  v_nat[:, t, (2 * j + h) * DK:(2 * j + h + 1) * DK],
                                  prob_T[:, slot, t * S:t * S + S - t * P], start=t == 0, stop=t == QT - 1)
                last.then_inc(pv_done, 1)

            def output_projection(b, first):
                wait(pe, slots_ready, b)
                if first:
                    pe.wait_ge(y_kept, 2)
                for t in range(QT):
                    for c in range(PAIRS):
                        if t == 0 and c >= PAIRS - 2:
                            pe.wait_ge(oT_kept, 8 * b + c + 1)
                        mm(ps_w[:, t * P:(t + 1) * P], o_T[:, c, t * P:(t + 1) * P], wo_s[:, c, :],
                           start=c == 0, stop=False)
                    if first:
                        pe.wait_ge(y_kept, 3)
                    last = mm(ps_w[:, t * P:(t + 1) * P], blind[:, t * P:(t + 1) * P],
                              mean_rows[:, bass.ds(b, 1), :], start=False, stop=True)
                last.then_inc(wo_done, 1)

            def norm_transposes(b):
                pe.wait_ge(rows_ready, 2 * b + 2)
                for t in range(QT):
                    last = t_.transpose(ps_w[:, S + t * P:S + (t + 1) * P], rows[:, t, D:2 * D], ident[:, :])
                last.then_inc(x2T_done, 1)

            def router(b):
                pe.wait_ge(x2T_kept, b + 1)
                for t in range(QT):
                    last = mm(ps_lg[:, t, :], x2_T[:, t * P:(t + 1) * P], wr_s[:, :])
                last.then_inc(logits_done, 1)

            def ranks(b):
                pe.wait_ge(choice_ready, b + 1)
                mm(ps_rk[:, 0, :], before[:, :], choice_b[:, 0, :])
                mm(ps_rk[:, 1, :], before[:, :], choice_b[:, 1, :], stop=False)
                mm(ps_rk[:, 1, :], ones_b[:, :], choice_b[:, 0, :], start=False)
                mm(ps_ct, ones_b[:, :], choice_b[:, 0, :], stop=False)
                mm(ps_ct, ones_b[:, :], choice_b[:, 1, :], start=False).then_inc(rank_done, 1)

            def mean_of(b):
                pe.wait_ge(ctx_sum_ready, b + 1)
                mm(ps_mean[:, b:b + 1], ctx_sum[:, b, :], mean_w[:, :]).then_inc(mean_done, 1)

            def means_through_wv(lo, hi):
                pe.wait_ge(mean_kept, 1)
                for c in range(lo, hi):
                    last = mm(ps_u[:, c * B:(c + 1) * B], wv_s[:, c * P:(c + 1) * P], ctx_mean[:, :])
                last.then_inc(u_done, 1)

            def means_through_wo():
                pe.wait_ge(u_kept, 1)
                for c in range(PAIRS):
                    last = mm(ps_y, u_T[:, c, :], wo_s[:, c, :], start=c == 0, stop=c == PAIRS - 1)
                last.then_inc(y_done, 1)

            def last_projection(c):
                b = B - 1
                if c == 0:
                    pe.wait_ge(qk_kept, 16 * B)
                    pe.wait_ge(qodd_kept, 8 * B)
                    for t in range(QT):
                        mm(ps_qk[:, t * P:(t + 1) * P], blind[:, t * P:(t + 1) * P], mean_rows[:, b, :],
                           start=t == 0, stop=False, loose=True)
                pe.wait_ge(oT_kept, 8 * b + c + 1)
                for t in range(QT):
                    last = mm(ps_qk[:, t * P:(t + 1) * P], o_T[:, c, t * P:(t + 1) * P], wo_s[:, c, :],
                              start=False, stop=c == PAIRS - 1, loose=True)
                if c == PAIRS - 1:
                    last.then_inc(wo_done, 1)

            def empty_product(e):
                if e == 0:
                    pe.wait_ge(b1_ready, 1)
                    pe.wait_ge(col_ready, 1)
                    pe.wait_ge(ld_ffn, 16 * (E + 2))
                    pe.wait_ge(v_kept, 8 * B)
                for c in range(FC):
                    last = mm(ps_c, relu_col[:, e, c, :], w2_s[:, e, c, :], start=e + c == 0,
                              stop=e + c == E + FC - 2)
                if e == E - 1:
                    last.then_inc(empty_done, 1)

            def batch(b, first=False, last=False):
                for j in range(PAIRS):
                    p = 8 * b + j
                    for h in range(2):
                        if not (last and j >= PAIRS - AHEAD):
                            scores(p + AHEAD, (j + AHEAD) % PAIRS, h,
                                   PAIRS + j + AHEAD + 1 if first and j + AHEAD < PAIRS else None)
                        if not (last and j == PAIRS - 1):
                            transpose_probs(p + 1, h, (2 * j + 2 + h) % SLOTS)
                    if not last and j > 0:
                        project_qk(b + 1, j - 1)
                        project_v(b + 1, j - 1)
                    if first and j == 6:
                        pe.wait_ge(ld_wo, 16)
                    if first:
                        for late in {2: (0,), 3: (1,), 4: (2,), 5: (3, 4), 6: (5, 6, 7)}.get(j, ()):
                            mean_of(late)
                    if first and j == 7:
                        means_through_wv(PAIRS // 2, PAIRS)
                    if j == 6 and not first:
                        ranks(b - 1)
                    if last and j < E // 2:
                        empty_product(j)
                    values(p, j)
                    if first and j == 6:
                        means_through_wv(0, PAIRS // 2)
                    if last and j > 0:
                        last_projection(j - 1)
                    if j == 0 and not last:
                        input_transposes(b + 1)
                    if j == 3 and not first:
                        norm_transposes(b - 1)
                    if j == 4 and not first:
                        router(b - 1)
                if last:
                    last_projection(PAIRS - 1)
                elif first:
                    means_through_wo()
                    project_v(b + 1, 7)
                    output_projection(b, first)
                    project_qk(b + 1, 7)
                else:
                    output_projection(b, first)
                    project_qk(b + 1, 7)
                    project_v(b + 1, 7)

            pe.wait_ge(ident_ready, 1)
            pe.wait_ge(ld_c[0], 16)
            for t in range(QT):
                last = t_.transpose(ps_s[0][:, t * P:(t + 1) * P], ctx_nat[:, t, :], ident[:, :])
            last.then_inc(first_cT_done, 1)
            pe.wait_ge(ld_bias, 16 * 4)
            t_.transpose(ps_w[:, 0:NB], bias_rows[:, :], ident[0:NB, 0:NB]).then_inc(biasT_done, 1)
            pe.wait_ge(first_cT_ready, 1)
            pe.wait_ge(ld_wk, 16)
            for j in range(PAIRS):
                if j == X_AT:
                    pe.wait_ge(xnorm_ready, QT)
                    for t in range(QT):
                        last = t_.transpose(ps_s[1][:, t * P:(t + 1) * P], x_norm[:, t, :], ident[:, :])
                    last.then_inc(inT_done, 1)
                first_kv(j)
            pe.wait_ge(ld_wq, 16)
            pe.wait_ge(inT_ready, 1)
            for j in range(PAIRS):
                first_q(j)
                if 2 <= j < 2 + AHEAD:
                    for h in range(2):
                        scores(j - 2, j - 2, h, PAIRS + j - 1)
            pe.wait_ge(const_ready, CONSTS)
            pe.wait_ge(qk_kept, PAIRS)
            pe.wait_ge(v_kept, PAIRS)
            for h in range(2):
                transpose_probs(0, h, h)
            batch(0, first=True)
            pe.wait_ge(ld_small, 16 * 5)
            with pe.Fori(1, B - 1) as b:
                batch(b)
            batch(B - 1, last=True)
            for e in range(E // 2, E):
                empty_product(e)

            def tile_transpose(tile, r, turn):
                pe.wait_ge(tile_loaded[r], 16 * turn + 16)
                wait(pe, tileT_kept, tile - 1)
                t_.transpose(ps_x[r % 2][:, 0:P], tile_in[:, r, D:2 * D], ident[:, :]).then_inc(tileT_done, 1)

            def first_product(tile, r, early=False):
                pe.wait_ge(tileT_kept, tile + 1)
                if early:
                    pe.wait_ge(w1_early, tile + 1)
                else:
                    pe.wait_ge(w1_ready, tile + 1 - EARLY)
                wait(pe, h_kept, FC * (tile - 1))
                for c in range(FC):
                    last = mm(ps_h[r % 2][:, c * P:(c + 1) * P], w1_now[:, r % 2, c * P:(c + 1) * P],
                              tile_T[:, r % 2, :])
                last.then_inc(h_done, 1)

            def second_product(tile, r):
                wait(pe, out_ready, tile - 1)
                mm(ps_out[r % 2][:, 0:D], w2_now[0:E, r % W2R, SEL_AT - W2_AT:PACK - W2_AT], rest[:, :], stop=False)
                for c in range(FC):
                    pe.wait_ge(h_kept, FC * tile + c + 1)
                    last = mm(ps_out[r % 2][:, 0:D], hidden[:, r % 2, c * P:(c + 1) * P],
                              w2_now[:, r % W2R, c * D:(c + 1) * D], start=False, stop=c == FC - 1)
                last.then_inc(y2_done, 1)

            tile_transpose(0, 0, 0)
            first_product(0, 0, True)
            tile_transpose(1, 1, 0)
            for tile in range(1, EARLY):
                if tile == LN_AT:
                    norm_transposes(B - 1)
                first_product(tile, tile, True)
                if tile == LN_AT:
                    pe.wait_ge(empty_kept, 1)
                    mm(ps_rest, others_p[0:E, :], empty[:, :]).then_inc(rest_done, 1)
                    router(B - 1)
                if tile == LN_AT + 1:
                    ranks(B - 1)
                if tile < EARLY - 1:
                    tile_transpose(tile + 1, tile + 1, 0)
                if tile == 1:
                    pe.wait_ge(rest_ready, 1)
                pe.wait_ge(w2_ready, tile)
                second_product(tile - 1, tile - 1)
            tile_transpose(EARLY, EARLY % RING, EARLY // RING)
            with pe.Fori(0, TURNS) as i:
                for r in range(RING):
                    tile = i * RING + EARLY + r
                    first_product(tile, (EARLY + r) % RING)
                    tile_transpose(tile + 1, (EARLY + r + 1) % RING, i + (EARLY + r + 1) // RING)
                    pe.wait_ge(w2_ready, tile)
                    second_product(tile - 1, (EARLY + r - 1) % RING)
            pe.wait_ge(w2_ready, MT)
            second_product(MT - 1, (MT - 1) % RING)


X_AT = 3
LN_AT = 1
CONSTS = 17
PER_BATCH = 37

_INS = ['x', 'ctx_1024', 'mask_BxS2_bf0', 'g_xattn', 'g_ffn', 'L0_xattn_Wq', 'L0_xattn_bq', 'L0_xattn_Wk', 'L0_xattn_bk',
        'L0_xattn_Wv', 'L0_xattn_bv', 'L0_xattn_Wo', 'L0_xattn_bo', 'L0_ffn_W1', 'L0_ffn_b1', 'L0_ffn_W2', 'L0_ffn_b2',
        'L0_ffn_Wr', 'L0_ffn_br']


def kernel(**inputs):
    import numpy as np
    import concourse.bacc as bacc
    from concourse.bass_utils import run_bass_kernel_spmd

    nc = bacc.Bacc("TRN2", target_bir_lowering=False, num_devices=1)
    arrays, args = {}, []
    for name in _INS:
        a = np.ascontiguousarray(inputs[name])
        arrays[f"in_{name}"] = a
        args.append(nc.dram_tensor(f"in_{name}", a.shape, mybir.dt.from_np(a.dtype), kind="ExternalInput").ap())
    result = nc.dram_tensor("out_0", (B, S, D), fp32, kind="ExternalOutput").ap()
    flamingo_layer(nc, *args, result)
    r = run_bass_kernel_spmd(nc, [arrays], core_ids=[0])
    return r.results[0]["out_0"]
```
